# Optimizing a Trainium2 kernel written in Bass

```python
import numpy as np
import jax
import jax.numpy as jnp

def _softmax(x, axis=-1):
    return jax.nn.softmax(x, axis=axis)

def _gelu(x):
    return jax.nn.gelu(x, approximate=True)

def _silu(x):
    return jax.nn.silu(x)

def _sigmoid(x):
    return jax.nn.sigmoid(x)

def _layernorm(x, axis=-1, eps=1e-05):
    m = jnp.mean(x, axis=axis, keepdims=True)
    v = jnp.var(x, axis=axis, keepdims=True)
    return (x - m) / jnp.sqrt(v + eps)

def _scatter_add(tgt, idx, src, axis=0):
    return tgt.at[idx].add(src)

def _segment_sum(src, seg, n):
    return jax.ops.segment_sum(src, seg, n)
kernel_name = 'mk_hybrid_d2_jaxref_r8_551ead'

def setup_inputs(seed: int=0):
    np.random.seed(seed)
    _w = jnp.asarray

    def _L0_attn_a_setup():
        import jax, jax.numpy as jnp
        import numpy as np
        D_MODEL, N_HEADS = (128, 16)
        D_H = D_MODEL // N_HEADS
        D_HR = D_H // 2
        D_LATENT = 32
        THETA = 10000.0

        def rope(x, theta=THETA):
            S, d = (x.shape[-2], x.shape[-1])
            inv = theta ** (-jnp.arange(0, d, 2, dtype=jnp.float32) / d)
            ang = jnp.arange(S, dtype=jnp.float32)[:, None] * inv
            cos, sin = (jnp.cos(ang), jnp.sin(ang))
            x1, x2 = (x[..., 0::2], x[..., 1::2])
            r1 = x1 * cos - x2 * sin
            r2 = x1 * sin + x2 * cos
            return jnp.stack([r1, r2], axis=-1).reshape(x.shape)
        key = jax.random.key(seed)
        ks = jax.random.split(key, 9)
        s = lambda fan_in: 1.0 / np.sqrt(fan_in)
        return {'x': jax.random.normal(ks[0], (4, 256, D_MODEL), jnp.float32), 'W_DQ': jax.random.normal(ks[1], (D_MODEL, D_LATENT), jnp.float32) * s(D_MODEL), 'W_UQ': jax.random.normal(ks[2], (D_LATENT, N_HEADS * D_H), jnp.float32) * s(D_LATENT), 'W_QR': jax.random.normal(ks[3], (D_LATENT, N_HEADS * D_HR), jnp.float32) * s(D_LATENT), 'W_DKV': jax.random.normal(ks[4], (D_MODEL, D_LATENT), jnp.float32) * s(D_MODEL), 'W_UK': jax.random.normal(ks[5], (D_LATENT, N_HEADS * D_H), jnp.float32) * s(D_LATENT), 'W_UV': jax.random.normal(ks[6], (D_LATENT, N_HEADS * D_H), jnp.float32) * s(D_LATENT), 'W_KR': jax.random.normal(ks[7], (D_MODEL, D_HR), jnp.float32) * s(D_MODEL), 'W_O': jax.random.normal(ks[8], (N_HEADS * D_H, D_MODEL), jnp.float32) * s(N_HEADS * D_H)}
    _L0_attn_a_in = _L0_attn_a_setup()

    def _L0_attn_b_setup():
        import jax, jax.numpy as jnp
        import numpy as np
        N_EMBD = 128
        N_HEAD = 16
        HEAD_DIM = N_EMBD // N_HEAD
        LATENT_DIM = N_EMBD // 2
        B, T = (4, 256)
        key = jax.random.key(seed)
        ks = jax.random.split(key, 5)

        def init(k, fan_in, fan_out):
            bound = 1.0 / np.sqrt(fan_in)
            return jax.random.uniform(k, (fan_in, fan_out), jnp.float32, -bound, bound)
        return {'x': jax.random.normal(ks[0], (B, T, N_EMBD), jnp.float32), 'Wc_down': init(ks[1], N_EMBD, LATENT_DIM), 'Wq_up': init(ks[2], LATENT_DIM, N_EMBD), 'Wkv_up': init(ks[3], LATENT_DIM, 2 * HEAD_DIM), 'Wc_proj': init(ks[4], N_EMBD, N_EMBD)}
    _L0_attn_b_in = _L0_attn_b_setup()

    def _L0_ffn_setup():
        import jax, jax.numpy as jnp
        import numpy as np
        DIM = 128
        HIDDEN = 384
        SCALE = 1.0 / 127.0

        def _dequant(w_int, dtype):
            return w_int.astype(dtype) * jnp.asarray(SCALE, dtype)
        key = jax.random.key(seed)
        k_x, k_g, k_u, k_d = jax.random.split(key, 4)
        x = jax.random.normal(k_x, (4, 256, DIM), dtype=jnp.float32)
        w_gate = jax.random.randint(k_g, (HIDDEN, DIM), -127, 128, dtype=jnp.int32)
        w_up = jax.random.randint(k_u, (HIDDEN, DIM), -127, 128, dtype=jnp.int32)
        w_down = jax.random.randint(k_d, (DIM, HIDDEN), -127, 128, dtype=jnp.int32)
        return {'x': x, 'w_gate': w_gate, 'w_up': w_up, 'w_down': w_down}
    _L0_ffn_in = _L0_ffn_setup()

    def _L1_attn_a_setup():
        import jax, jax.numpy as jnp
        import numpy as np
        key = jax.random.key(seed)
        k_u, k_wl, k_b, k_c = jax.random.split(key, 4)
        B_, T, D, N = (4, 512, 128, 32)
        u = jax.random.normal(k_u, (B_, T, D), dtype=jnp.float32)
        Wl = jax.random.normal(k_wl, (N, D), dtype=jnp.float32) * 0.02
        bl = jnp.full((N,), 2.0, dtype=jnp.float32)
        xav_b = 0.5 * np.sqrt(6.0 / (D + N))
        Wb = jax.random.uniform(k_b, (N, D), dtype=jnp.float32, minval=-xav_b, maxval=xav_b)
        xav_c = 0.5 * np.sqrt(6.0 / (N + D))
        Wc = jax.random.uniform(k_c, (D, N), dtype=jnp.float32, minval=-xav_c, maxval=xav_c)
        Dp = jnp.zeros((D,), dtype=jnp.float32)
        return {'u': u, 'Wl': Wl, 'bl': bl, 'Wb': Wb, 'Wc': Wc, 'Dp': Dp}
    _L1_attn_a_in = _L1_attn_a_setup()

    def _L1_attn_b_setup():
        import jax, jax.numpy as jnp
        import numpy as np
        B, T, D, C = (16, 512, 128, 128)
        key = jax.random.key(seed)
        ks = jax.random.split(key, 15)

        def w(k, out_dim, in_dim):
            return jax.random.normal(k, (out_dim, in_dim), jnp.float32) / np.sqrt(in_dim).astype(np.float32)
        return {'x': jax.random.normal(ks[0], (B, T, D), jnp.float32), 'Wq': w(ks[1], C, D), 'bq': jnp.zeros((C,), jnp.float32), 'Wk': w(ks[2], C, D), 'bk': jnp.zeros((C,), jnp.float32), 'Wv': w(ks[3], C, D), 'bv': jnp.zeros((C,), jnp.float32), 'Wa': w(ks[4], 1, D), 'ba': jnp.zeros((1,), jnp.float32), 'Wb': w(ks[5], 1, D), 'bb': jnp.zeros((1,), jnp.float32), 'Wg': w(ks[6], C, D), 'bg': jnp.zeros((C,), jnp.float32), 'Wo': w(ks[7], D, C), 'bo': jnp.zeros((D,), jnp.float32)}
    _L1_attn_b_in = _L1_attn_b_setup()

    def _L1_ffn_setup():
        import jax, jax.numpy as jnp
        import numpy as np
        ALPHA = 1.702
        LIMIT = 7.0
        EPS = 1e-05
        E = 16
        K = 4

        def _swiglu(h):
            x_glu = jnp.minimum(h[..., ::2], LIMIT)
            x_lin = jnp.clip(h[..., 1::2], LIMIT, LIMIT)
            return x_glu * jax.nn.sigmoid(ALPHA * x_glu) * (x_lin + 1.0)
        key = jax.random.key(seed)
        ks = jax.random.split(key, 7)
        B, T, H, I = (1, 256, 128, 128)
        x = jax.random.normal(ks[0], (B, T, H), jnp.float32)
        scale = jnp.ones((H,), jnp.float32)
        gate_w = jax.random.normal(ks[1], (E, H), jnp.float32) * 0.02
        gate_b = jnp.zeros((E,), jnp.float32)
        mlp1_w = jax.random.normal(ks[2], (E, 2 * I, H), jnp.float32) * 0.02
        mlp1_b = jax.random.normal(ks[3], (E, 2 * I), jnp.float32) * 0.02
        mlp2_w = jax.random.normal(ks[4], (E, H, I), jnp.float32) * 0.02
        mlp2_b = jax.random.normal(ks[5], (E, H), jnp.float32) * 0.02
        return dict(x=x, scale=scale, gate_w=gate_w, gate_b=gate_b, mlp1_w=mlp1_w, mlp1_b=mlp1_b, mlp2_w=mlp2_w, mlp2_b=mlp2_b)
    _L1_ffn_in = _L1_ffn_setup()
    _d = {'L0_attn_a_x': _L0_attn_a_in['x'], 'L0_attn_a_W_DQ': _L0_attn_a_in['W_DQ'], 'L0_attn_a_W_UQ': _L0_attn_a_in['W_UQ'], 'L0_attn_a_W_QR': _L0_attn_a_in['W_QR'], 'L0_attn_a_W_DKV': _L0_attn_a_in['W_DKV'], 'L0_attn_a_W_UK': _L0_attn_a_in['W_UK'], 'L0_attn_a_W_UV': _L0_attn_a_in['W_UV'], 'L0_attn_a_W_KR': _L0_attn_a_in['W_KR'], 'L0_attn_a_W_O': _L0_attn_a_in['W_O'], 'L0_attn_b_Wc_down': _L0_attn_b_in['Wc_down'], 'L0_attn_b_Wq_up': _L0_attn_b_in['Wq_up'], 'L0_attn_b_Wkv_up': _L0_attn_b_in['Wkv_up'], 'L0_attn_b_Wc_proj': _L0_attn_b_in['Wc_proj'], 'L0_ffn_w_gate': _L0_ffn_in['w_gate'], 'L0_ffn_w_up': _L0_ffn_in['w_up'], 'L0_ffn_w_down': _L0_ffn_in['w_down'], 'L1_attn_a_Wl': _L1_attn_a_in['Wl'], 'L1_attn_a_bl': _L1_attn_a_in['bl'], 'L1_attn_a_Wb': _L1_attn_a_in['Wb'], 'L1_attn_a_Wc': _L1_attn_a_in['Wc'], 'L1_attn_a_Dp': _L1_attn_a_in['Dp'], 'L1_attn_b_Wq': _L1_attn_b_in['Wq'], 'L1_attn_b_bq': _L1_attn_b_in['bq'], 'L1_attn_b_Wk': _L1_attn_b_in['Wk'], 'L1_attn_b_bk': _L1_attn_b_in['bk'], 'L1_attn_b_Wv': _L1_attn_b_in['Wv'], 'L1_attn_b_bv': _L1_attn_b_in['bv'], 'L1_attn_b_Wa': _L1_attn_b_in['Wa'], 'L1_attn_b_ba': _L1_attn_b_in['ba'], 'L1_attn_b_Wb': _L1_attn_b_in['Wb'], 'L1_attn_b_bb': _L1_attn_b_in['bb'], 'L1_attn_b_Wg': _L1_attn_b_in['Wg'], 'L1_attn_b_bg': _L1_attn_b_in['bg'], 'L1_attn_b_Wo': _L1_attn_b_in['Wo'], 'L1_attn_b_bo': _L1_attn_b_in['bo'], 'L1_ffn_scale': _L1_ffn_in['scale'], 'L1_ffn_gate_w': _L1_ffn_in['gate_w'], 'L1_ffn_gate_b': _L1_ffn_in['gate_b'], 'L1_ffn_mlp1_w': _L1_ffn_in['mlp1_w'], 'L1_ffn_mlp1_b': _L1_ffn_in['mlp1_b'], 'L1_ffn_mlp2_w': _L1_ffn_in['mlp2_w'], 'L1_ffn_mlp2_b': _L1_ffn_in['mlp2_b']}
    _x0 = _d['L0_attn_a_x']
    _d['L0_attn_a_x'] = jax.random.normal(jax.random.fold_in(jax.random.key(seed), 1), (4, 1024, 128), dtype=_x0.dtype)
    del _x0
    return _d

def reference(L0_attn_a_x, L0_attn_a_W_DQ, L0_attn_a_W_UQ, L0_attn_a_W_QR, L0_attn_a_W_DKV, L0_attn_a_W_UK, L0_attn_a_W_UV, L0_attn_a_W_KR, L0_attn_a_W_O, L0_attn_b_Wc_down, L0_attn_b_Wq_up, L0_attn_b_Wkv_up, L0_attn_b_Wc_proj, L0_ffn_w_gate, L0_ffn_w_up, L0_ffn_w_down, L1_attn_a_Wl, L1_attn_a_bl, L1_attn_a_Wb, L1_attn_a_Wc, L1_attn_a_Dp, L1_attn_b_Wq, L1_attn_b_bq, L1_attn_b_Wk, L1_attn_b_bk, L1_attn_b_Wv, L1_attn_b_bv, L1_attn_b_Wa, L1_attn_b_ba, L1_attn_b_Wb, L1_attn_b_bb, L1_attn_b_Wg, L1_attn_b_bg, L1_attn_b_Wo, L1_attn_b_bo, L1_ffn_scale, L1_ffn_gate_w, L1_ffn_gate_b, L1_ffn_mlp1_w, L1_ffn_mlp1_b, L1_ffn_mlp2_w, L1_ffn_mlp2_b):

    def _L0_attn_a_ref(x, W_DQ, W_UQ, W_QR, W_DKV, W_UK, W_UV, W_KR, W_O):
        import jax, jax.numpy as jnp
        import numpy as np
        D_MODEL, N_HEADS = (128, 16)
        D_H = D_MODEL // N_HEADS
        D_HR = D_H // 2
        D_LATENT = 32
        THETA = 10000.0

        def rope(x, theta=THETA):
            S, d = (x.shape[-2], x.shape[-1])
            inv = theta ** (-jnp.arange(0, d, 2, dtype=jnp.float32) / d)
            ang = jnp.arange(S, dtype=jnp.float32)[:, None] * inv
            cos, sin = (jnp.cos(ang), jnp.sin(ang))
            x1, x2 = (x[..., 0::2], x[..., 1::2])
            r1 = x1 * cos - x2 * sin
            r2 = x1 * sin + x2 * cos
            return jnp.stack([r1, r2], axis=-1).reshape(x.shape)
        B, S, _ = x.shape
        d_qk = D_H + D_HR
        c_q = x @ W_DQ
        Qc = (c_q @ W_UQ).reshape(B, S, N_HEADS, D_H).transpose(0, 2, 1, 3)
        Qr = (c_q @ W_QR).reshape(B, S, N_HEADS, D_HR).transpose(0, 2, 1, 3)
        Qr = rope(Qr)
        c_kv = x @ W_DKV
        Kc = (c_kv @ W_UK).reshape(B, S, N_HEADS, D_H).transpose(0, 2, 1, 3)
        Kr = rope((x @ W_KR)[:, None, :, :])
        Kr = jnp.broadcast_to(Kr, (B, N_HEADS, S, D_HR))
        V = (c_kv @ W_UV).reshape(B, S, N_HEADS, D_H).transpose(0, 2, 1, 3)
        Q = jnp.concatenate([Qc, Qr], axis=-1)
        K = jnp.concatenate([Kc, Kr], axis=-1)
        scores = jnp.einsum('bhqd,bhkd->bhqk', Q, K)
        scores = jnp.clip(scores, -80.0, 80.0)
        causal = jnp.tril(jnp.ones((S, S), dtype=bool))
        scores = jnp.where(causal, scores, -jnp.inf)
        weights = jax.nn.softmax(scores / jnp.sqrt(jnp.float32(d_qk)), axis=-1)
        attn = jnp.einsum('bhqk,bhkd->bhqd', weights, V)
        attn = attn.transpose(0, 2, 1, 3).reshape(B, S, N_HEADS * D_H)
        return attn @ W_O

    def _L0_attn_b_ref(x, Wc_down, Wq_up, Wkv_up, Wc_proj):
        import jax, jax.numpy as jnp
        import numpy as np
        N_EMBD = 128
        N_HEAD = 16
        HEAD_DIM = N_EMBD // N_HEAD
        LATENT_DIM = N_EMBD // 2
        B, T = (4, 256)
        Bsz, Tlen, C = x.shape
        latent = x @ Wc_down
        q = (latent @ Wq_up).reshape(Bsz, Tlen, N_HEAD, HEAD_DIM)
        kv = latent @ Wkv_up
        k, v = (kv[..., :HEAD_DIM], kv[..., HEAD_DIM:])
        scale = 1.0 / np.sqrt(HEAD_DIM)
        att = jnp.einsum('bthd,bsd->bhts', q, k) * scale
        causal = jnp.tril(jnp.ones((Tlen, Tlen), dtype=bool))
        att = jnp.where(causal[None, None], att, -jnp.inf)
        att = jax.nn.softmax(att, axis=-1)
        y = jnp.einsum('bhts,bsd->bthd', att, v).reshape(Bsz, Tlen, C)
        return y @ Wc_proj

    def _L0_ffn_ref(x, w_gate, w_up, w_down):
        import jax, jax.numpy as jnp
        import numpy as np
        DIM = 128
        HIDDEN = 384
        SCALE = 1.0 / 127.0

        def _dequant(w_int, dtype):
            return w_int.astype(dtype) * jnp.asarray(SCALE, dtype)
        wg = _dequant(w_gate, x.dtype)
        wu = _dequant(w_up, x.dtype)
        wd = _dequant(w_down, x.dtype)
        gate = jnp.einsum('bsd,hd->bsh', x, wg)
        up = jnp.einsum('bsd,hd->bsh', x, wu)
        h = jax.nn.silu(gate) * up
        return jnp.einsum('bsh,dh->bsd', h, wd)

    def _L1_attn_a_ref(u, Wl, bl, Wb, Wc, Dp):
        import jax, jax.numpy as jnp
        import numpy as np
        lam = jax.nn.sigmoid(jnp.einsum('btd,nd->btn', u, Wl) + bl)
        Bu = jnp.einsum('btd,nd->btn', u, Wb)

        def step(h, inp):
            lam_t, bu_t = inp
            h = lam_t * h + bu_t
            return (h, h)
        h0 = jnp.zeros((u.shape[0], Wl.shape[0]), dtype=u.dtype)
        _, H = jax.lax.scan(step, h0, (jnp.swapaxes(lam, 0, 1), jnp.swapaxes(Bu, 0, 1)))
        H = jnp.swapaxes(H, 0, 1)
        y = jnp.einsum('btn,dn->btd', H, Wc) + u * Dp
        return y

    def _L1_attn_b_ref(x, Wq, bq, Wk, bk, Wv, bv, Wa, ba, Wb, bb, Wg, bg, Wo, bo):
        import jax, jax.numpy as jnp
        import numpy as np
        B, T, D, C = (16, 512, 128, 128)
        q = x @ Wq.T + bq
        k = x @ Wk.T + bk
        k = k / jnp.maximum(jnp.linalg.norm(k, axis=-1, keepdims=True), 1e-12)
        v = x @ Wv.T + bv
        alpha = jax.nn.sigmoid(x @ Wa.T + ba)
        beta = jax.nn.sigmoid(x @ Wb.T + bb)
        gate = jax.nn.sigmoid(x @ Wg.T + bg)
        Bb, Tt, Dd = x.shape
        Cc = q.shape[-1]

        def step(S, inp):
            q_t, k_t, v_t, a_t, b_t = inp
            a = a_t[:, :, None]
            b = b_t[:, :, None]
            Sk = jnp.einsum('bij,bj->bi', S, k_t)
            S = a * (S - b * (Sk[:, :, None] * k_t[:, None, :])) + b * (v_t[:, :, None] * k_t[:, None, :])
            o = jnp.einsum('bi,bij->bj', q_t, S)
            return (S, o)
        xs = (q.swapaxes(0, 1), k.swapaxes(0, 1), v.swapaxes(0, 1), alpha.swapaxes(0, 1), beta.swapaxes(0, 1))
        S0 = jnp.zeros((Bb, Cc, Cc), x.dtype)
        _, o = jax.lax.scan(step, S0, xs)
        o = o.swapaxes(0, 1) * gate
        return o @ Wo.T + bo

    def _L1_ffn_ref(x, scale, gate_w, gate_b, mlp1_w, mlp1_b, mlp2_w, mlp2_b):
        import jax, jax.numpy as jnp
        import numpy as np
        ALPHA = 1.702
        LIMIT = 7.0
        EPS = 1e-05
        E = 16
        K = 4

        def _swiglu(h):
            x_glu = jnp.minimum(h[..., ::2], LIMIT)
            x_lin = jnp.clip(h[..., 1::2], LIMIT, LIMIT)
            return x_glu * jax.nn.sigmoid(ALPHA * x_glu) * (x_lin + 1.0)
        t = x * jax.lax.rsqrt(jnp.mean(x * x, axis=-1, keepdims=True) + EPS) * scale
        g = jnp.einsum('bth,eh->bte', t, gate_w) + gate_b
        vals, idx = jax.lax.top_k(g, K)
        w = jax.nn.softmax(vals, axis=-1)
        route = jnp.sum(jax.nn.one_hot(idx, E, dtype=t.dtype) * w[..., None], axis=-2)
        route_e = jnp.moveaxis(route, -1, 0)

        def step(acc, p):
            w1, b1, w2, b2, r = p
            h = jnp.einsum('bth,ih->bti', t, w1) + b1
            s = _swiglu(h)
            y = jnp.einsum('bti,hi->bth', s, w2) + b2
            return (acc + r[..., None] * y, None)
        acc, _ = jax.lax.scan(step, jnp.zeros_like(x), (mlp1_w, mlp1_b, mlp2_w, mlp2_b, route_e))
        return x + acc
    x = L0_attn_a_x
    x = x + _L0_attn_a_ref(_layernorm(x, axis=-1), L0_attn_a_W_DQ, L0_attn_a_W_UQ, L0_attn_a_W_QR, L0_attn_a_W_DKV, L0_attn_a_W_UK, L0_attn_a_W_UV, L0_attn_a_W_KR, L0_attn_a_W_O)
    x = x + _L0_ffn_ref(_layernorm(x, axis=-1), L0_ffn_w_gate, L0_ffn_w_up, L0_ffn_w_down)
    x = x + _L0_attn_b_ref(_layernorm(x, axis=-1), L0_attn_b_Wc_down, L0_attn_b_Wq_up, L0_attn_b_Wkv_up, L0_attn_b_Wc_proj)
    x = x + _L0_ffn_ref(_layernorm(x, axis=-1), L0_ffn_w_gate, L0_ffn_w_up, L0_ffn_w_down)
    x = x + _L1_attn_a_ref(_layernorm(x, axis=-1), L1_attn_a_Wl, L1_attn_a_bl, L1_attn_a_Wb, L1_attn_a_Wc, L1_attn_a_Dp)
    x = x + _L1_ffn_ref(_layernorm(x, axis=-1), L1_ffn_scale, L1_ffn_gate_w, L1_ffn_gate_b, L1_ffn_mlp1_w, L1_ffn_mlp1_b, L1_ffn_mlp2_w, L1_ffn_mlp2_b)
    x = x + _L1_attn_b_ref(_layernorm(x, axis=-1), L1_attn_b_Wq, L1_attn_b_bq, L1_attn_b_Wk, L1_attn_b_bk, L1_attn_b_Wv, L1_attn_b_bv, L1_attn_b_Wa, L1_attn_b_ba, L1_attn_b_Wb, L1_attn_b_bb, L1_attn_b_Wg, L1_attn_b_bg, L1_attn_b_Wo, L1_attn_b_bo)
    x = x + _L1_ffn_ref(_layernorm(x, axis=-1), L1_ffn_scale, L1_ffn_gate_w, L1_ffn_gate_b, L1_ffn_mlp1_w, L1_ffn_mlp1_b, L1_ffn_mlp2_w, L1_ffn_mlp2_b)
    return x

_drawn_inputs = setup_inputs


def setup_inputs(seed=0):
    import zlib

    import numpy as np

    out = dict(_drawn_inputs(seed))
    spreads = {'L1_attn_a_bl': (2.0, 0.6),
     'L1_attn_a_Dp': (0.0, 2.0),
     'L1_attn_b_bq': (0.0, 0.8),
     'L1_attn_b_bk': (0.0, 0.8),
     'L1_attn_b_bv': (0.0, 0.8),
     'L1_attn_b_bg': (0.0, 0.8),
     'L1_attn_b_bo': (0.0, 2.0),
     'L1_ffn_scale': (1.0, 0.6),
     'L1_ffn_gate_b': (0.0, 0.8)}
    factors = {'L0_attn_b_Wc_down': 8.0,
     'L0_attn_b_Wq_up': 8.0,
     'L0_attn_b_Wkv_up': 8.0,
     'L0_attn_b_Wc_proj': 8.0,
     'L1_attn_a_Wl': 8.0,
     'L1_attn_a_Wb': 8.0,
     'L1_attn_a_Wc': 8.0,
     'L1_attn_b_Wq': 8.0,
     'L1_attn_b_Wk': 8.0,
     'L1_attn_b_Wv': 8.0,
     'L1_attn_b_Wa': 8.0,
     'L1_attn_b_Wb': 8.0,
     'L1_attn_b_Wg': 8.0,
     'L1_attn_b_Wo': 8.0,
     'L1_ffn_gate_w': 8.0,
     'L1_ffn_mlp1_w': 8.0,
     'L1_ffn_mlp1_b': 64.0,
     'L1_ffn_mlp2_w': 8.0,
     'L1_ffn_mlp2_b': 64.0}
    for name, (base, spread) in spreads.items():
        noise = np.random.default_rng([zlib.crc32(name.encode()), seed]).standard_normal(out[name].shape)
        drawn = base * np.exp(spread * noise) if base else spread * noise
        out[name] = jnp.asarray(drawn.astype(out[name].dtype))
    for name, factor in factors.items():
        out[name] = (out[name] * factor).astype(out[name].dtype)
    return out
```

```python
from contextlib import ExitStack

import numpy as np

import concourse.bass as bass
from concourse import mybir

F32 = mybir.dt.float32
BF16 = mybir.dt.bfloat16
I32 = mybir.dt.int32
ALU = mybir.AluOpType
ACT = mybir.ActivationFunctionType
AX_X = mybir.AxisListType.X

P = 128
B, S, D = 4, 1024, 128
TOK = B * S
NT = TOK // P
TB = S // P
GW = 512
NG = TOK // GW
GT = GW // P
H, DH, DR = 16, 8, 4
HG = H // 4
LAT_A, LAT_B = 32, 64
HID = 384
HC = HID // P
NS = 32
E, TOPK = 16, 4
LN_EPS = 1e-5
NEG = -1.0e30
CLIP = 80.0
PARTS = 3
PAIRS = PARTS * PARTS
QC = PAIRS * DH
QR = PAIRS * DR


class Stage:

    def __init__(self, nc, name):
        self.nc, self.name, self.ctx, self.sems = nc, name, ExitStack(), []

    def __enter__(self):
        self.ctx.__enter__()
        return self

    def __exit__(self, *a):
        self.ctx.__exit__(*a)
        self.nc.clear_and_free_semaphores(self.sems)
        self.nc.all_engine_barrier()

    def sb(self, name, shape, dt=F32):
        return self.ctx.enter_context(self.nc.sbuf_tensor(f"{self.name}_{name}", shape, dt))

    def ps(self, name, shape, dt=F32):
        return self.ctx.enter_context(self.nc.psum_tensor(f"{self.name}_{name}", shape, dt))

    def sem(self, name):
        self.sems.append(self.nc.alloc_semaphore(f"{self.name}_{name}"))
        return self.sems[-1]

    def block(self):
        return self.ctx.enter_context(self.nc.Block())


def spread(ap, n):
    return ap.rearrange("p (a o) -> p a o", o=1).to_broadcast([ap.shape[0], ap.shape[1], n])


def load_x(nc, x_in, consts, X, C):
    tables = [n for n in consts if n in C]
    with Stage(nc, "load") as st:
        done = st.sem("done")
        cast = st.sem("cast")
        block = st.block()

        @block.sync
        def _(sp):
            sp.dma_start(X[:, :, :], x_in.rearrange("b (t p) d -> p (b t) d", p=P)).then_inc(done, 16)
            for name in tables:
                sp.dma_start(C[name][:, :], consts[name]).then_inc(done, 16)

        @block.vector
        def _(dve):
            dve.wait_ge(done, 16 * (1 + len(tables)))
            for name in ("ident", "neg_kq", "neg_qk"):
                dve.tensor_copy(C[f"{name}_b"][:, :], C[name][:, :]).then_inc(cast, 1)


def norm_stage(nc, name, X, XnT, C, gain=None):
    rms = gain is not None
    with Stage(nc, name) as st:
        xc = st.sb("xc", [P, NT, D])
        xn = st.sb("xn", [P, NT, D])
        xr = st.sb("xr", [P, NT, D]) if rms else xn
        sq = st.sb("sq", [P, 2, TB, D])
        total = st.sb("total", [P, NT])
        mean = st.sb("mean", [P, NT])
        squares = st.sb("squares", [P, NT])
        var = st.sb("var", [P, 2, NT])
        dev = st.sb("dev", [P, 2, NT])
        rstd = st.sb("rstd", [P, 2, NT])
        power = st.sb("power", [P, 2, NT])
        turned = st.ps("turned", [P, 2, 2, GW])
        gcol = st.sb("gcol", [P, 1])
        s_gain = st.sem("gain")
        s_sum = st.sem("sum")
        s_mean = st.sem("mean")
        s_cent = st.sem("cent")
        s_sq = st.sem("sq")
        s_ss = st.sem("ss")
        s_var = st.sem("var")
        s_dev = st.sem("dev")
        s_rstd = st.sem("rstd")
        s_pow = st.sem("pow")
        s_xn = st.sem("xn")
        s_xr = st.sem("xr")
        s_res = st.sem("res")
        s_turn = st.sem("turn")
        s_out = st.sem("out")
        tiles = [slice(TB * b, TB * b + TB) for b in range(B)]
        block = st.block()

        @block.sync
        def _(sp):
            if rms:
                sp.dma_start(gcol[:, :], gain.rearrange("(p o) -> p o", o=1)).then_inc(s_gain, 16)

        @block.gpsimd
        def _(pool):
            if rms:
                for b, t in enumerate(tiles):
                    pool.wait_ge(s_xn, b + 1)
                    pool.tensor_tensor(X[:, t, :], X[:, t, :], xn[:, t, :], ALU.add).then_inc(s_res, 1)

        @block.vector
        def _(dve):
            for b, t in enumerate(tiles):
                dve.reduce_sum(total[:, t], X[:, t, :], AX_X).then_inc(s_sum, 1)
                dve.wait_ge(s_sum, b + 1)
                dve.tensor_scalar(mean[:, t], total[:, t], 1.0 / D, None, ALU.mult).then_inc(s_mean, 1)
                dve.wait_ge(s_mean, b + 1)
                dve.tensor_tensor(xc[:, t, :], X[:, t, :], spread(mean[:, t], D), ALU.subtract).then_inc(s_cent, 1)
            for b, t in enumerate(tiles):
                dve.wait_ge(s_sq, b + 1)
                dve.reduce_sum(squares[:, t], sq[:, b % 2, :, :], AX_X).then_inc(s_ss, 1)
                dve.wait_ge(s_ss, b + 1)
                dve.tensor_scalar(var[:, 0, t], squares[:, t], 1.0 / D, LN_EPS, ALU.mult, ALU.add).then_inc(s_var, 1)
            for b, t in enumerate(tiles):
                dve.wait_ge(s_dev, b + 1)
                dve.reciprocal(rstd[:, 0, t], dev[:, 0, t]).then_inc(s_rstd, 1)
                dve.wait_ge(s_rstd, b + 1)
                dve.tensor_tensor(xn[:, t, :], xc[:, t, :], spread(rstd[:, 0, t], D), ALU.mult).then_inc(s_xn, 1)
            if rms:
                dve.tensor_tensor(power[:, 0, :], squares[:, :], rstd[:, 0, :], ALU.mult).then_inc(s_pow, 1)
                dve.wait_ge(s_pow, 1)
                dve.tensor_tensor(power[:, 1, :], power[:, 0, :], rstd[:, 0, :], ALU.mult).then_inc(s_pow, 1)
                dve.wait_ge(s_pow, 2)
                dve.tensor_scalar(var[:, 1, :], power[:, 1, :], 1.0 / D, LN_EPS, ALU.mult, ALU.add).then_inc(s_var, 1)
                dve.wait_ge(s_dev, B + 1)
                dve.reciprocal(rstd[:, 1, :], dev[:, 1, :]).then_inc(s_rstd, 1)
                dve.wait_ge(s_rstd, B + 1)
                for b, t in enumerate(tiles):
                    dve.tensor_tensor(xr[:, t, :], xn[:, t, :], spread(rstd[:, 1, t], D), ALU.mult).then_inc(s_xr, 1)

        @block.scalar
        def _(act):
            for b, t in enumerate(tiles):
                act.wait_ge(s_cent, b + 1)
                if b >= 2:
                    act.wait_ge(s_ss, b - 1)
                act.activation(sq[:, b % 2, :, :], xc[:, t, :], ACT.Square).then_inc(s_sq, 1)
            for b, t in enumerate(tiles):
                act.wait_ge(s_var, b + 1)
                act.activation(dev[:, 0, t], var[:, 0, t], ACT.Sqrt).then_inc(s_dev, 1)
            if rms:
                act.wait_ge(s_var, B + 1)
                act.activation(dev[:, 1, :], var[:, 1, :], ACT.Sqrt).then_inc(s_dev, 1)
                act.wait_ge(s_gain, 16)
            for b in range(B):
                act.wait_ge(s_turn, b + 1)
                out, in_ = XnT[:, b * S:(b + 1) * S], turned[:, b % 2, :, :]
                if rms:
                    act.mul(out, in_, gcol[:, 0:1]).then_inc(s_out, 1)
                else:
                    act.copy(out, in_).then_inc(s_out, 1)

        @block.tensor
        def _(pe):
            for b in range(B):
                pe.wait_ge(s_xr if rms else s_xn, b + 1)
                if b >= 2:
                    pe.wait_ge(s_out, b - 1)
                for i in range(TB):
                    mm = pe.transpose(turned[:, b % 2, i // GT, (i % GT) * P:(i % GT + 1) * P],
                                      xr[:, TB * b + i, :], C["ident"][:, :])
                mm.then_inc(s_turn, 1)


def store_x(nc, X, out):
    with Stage(nc, "store") as st:
        done = st.sem("done")
        block = st.block()

        @block.sync
        def _(sp):
            sp.dma_start(out.rearrange("b (t p) d -> p (b t) d", p=P), X[:, :, :]).then_inc(done, 16)
            sp.wait_ge(done, 16)


def gated_mlp(nc, name, X, XnT, C, w_gate, w_up, w_down):
    scale = float(np.float32(1.0 / 127.0))
    with Stage(nc, name) as st:
        raw = st.sb("raw", [P, 3, HC, P], I32)
        wide = st.sb("wide", [P, 3, HC, P])
        wgT = st.sb("wgT", [P, HC, P])
        wuT = st.sb("wuT", [P, HC, P])
        wdT = st.sb("wdT", [P, HC, P])
        act_g = st.sb("act_g", [P, 2, GW])
        hidden = st.sb("hidden", [P, 2, HC, GW])
        gate = st.ps("gate", [P, 2, GW])
        up = st.ps("up", [P, 2, GW])
        down = st.ps("down", [P, 2, GT, P])
        s_w = st.sem("w")
        s_wide = st.sem("wide")
        s_turn = st.sem("turn")
        s_wT = st.sem("wT")
        s_gu = st.sem("gate_up")
        s_silu = st.sem("silu")
        s_hid = st.sem("hid")
        s_down = st.sem("down")
        s_res = st.sem("res")
        weights = ((wgT, gate), (wuT, up), (wdT, down))
        block = st.block()

        @block.sync
        def _(sp):
            sp.dma_start(raw[:, 0, :, :], w_gate.rearrange("(c p) d -> p c d", p=P)).then_inc(s_w, 16)
            sp.dma_start(raw[:, 1, :, :], w_up.rearrange("(c p) d -> p c d", p=P)).then_inc(s_w, 16)
            sp.dma_start(raw[:, 2, :, :], w_down.rearrange("p (c h) -> p c h", c=HC)).then_inc(s_w, 16)

        @block.tensor
        def _(pe):
            for k, (_, bank) in enumerate(weights):
                pe.wait_ge(s_wide, k + 1)
                for c in range(HC):
                    dst = bank[:, 0, c, :] if k == 2 else bank[:, 0, c * P:(c + 1) * P]
                    mm = pe.transpose(dst, wide[:, k, c, :], C["ident"][:, :])
                mm.then_inc(s_turn, 1)
            pe.wait_ge(s_wT, 3)
            with pe.Fori(0, NG // 2) as r:
                for u in range(2):
                    g = r * 2 + u
                    for c in range(HC):
                        k = g * HC + c
                        pe.wait_ge(s_hid, k + 1)
                        b = (u * HC + c) % 2
                        xg = XnT[:, bass.ds(g * GW, GW)]
                        pe.matmul(gate[:, b, :], wgT[:, c, :], xg, start=True, stop=True)
                        pe.matmul(up[:, b, :], wuT[:, c, :], xg, start=True, stop=True).then_inc(s_gu, 1)
                    pe.wait_ge(s_hid, g * HC + HC + 2)
                    pe.wait_ge(s_res, g + 1)
                    for i in range(GT):
                        for c in range(HC):
                            mm = pe.matmul(down[:, u, i, :], hidden[:, u, c, i * P:(i + 1) * P],
                                           wdT[:, c, :], start=(c == 0), stop=(c == HC - 1))
                    mm.then_inc(s_down, 1)

        @block.scalar
        def _(act):
            with act.Fori(0, NG // 2) as r:
                for u in range(2):
                    for c in range(HC):
                        k = r * (2 * HC) + (u * HC + c)
                        b = (u * HC + c) % 2
                        act.wait_ge(s_gu, k + 1)
                        act.wait_ge(s_hid, k + 1)
                        act.activation(act_g[:, b, :], gate[:, b, :], ACT.Silu).then_inc(s_silu, 1)

        @block.vector
        def _(dve):
            dve.wait_ge(s_w, 48)
            for k in range(3):
                dve.tensor_scalar(wide[:, k, :, :], raw[:, k, :, :], scale, None, ALU.mult).then_inc(s_wide, 1)
            for k, (wT, bank) in enumerate(weights):
                dve.wait_ge(s_turn, k + 1)
                src = bank[:, 0, 0:HC, :] if k == 2 else bank[:, 0, 0:HC * P].rearrange("p (c n) -> p c n", c=HC)
                dve.tensor_copy(wT[:, :, :], src).then_inc(s_wT, 1)
            dve.sem_inc(s_hid, 2)
            dve.sem_inc(s_res, 2)
            with dve.Fori(0, NG // 2) as r:
                for u in range(2):
                    g = r * 2 + u
                    for c in range(HC):
                        k = g * HC + c
                        b = (u * HC + c) % 2
                        dve.wait_ge(s_silu, k + 1)
                        dve.tensor_tensor(hidden[:, u, c, :], act_g[:, b, :], up[:, b, :], ALU.mult).then_inc(s_hid, 1)
                    dve.wait_ge(s_down, g + 1)
                    xt = X[:, bass.ds(g * GT, GT), :]
                    dve.tensor_tensor(xt, down[:, u, :, :], xt, ALU.add).then_inc(s_res, 1)


SEGMENTS = [[(0, 0, 1024)], [(1, 0, 896), (7, 896, 128)], [(2, 0, 768), (6, 768, 256)],
            [(3, 0, 640), (5, 640, 384)], [(4, 0, 512)]]
NSEG = len(SEGMENTS)
ITS = B * HG


def width(k):
    return sum(w for _, _, w in SEGMENTS[k])


class Scratch:

    def __init__(self, nc, name, rotary):
        def dram(n, shape, dt=BF16):
            return nc.dram_tensor(f"{name}_{n}", shape, dt, kind="Internal").ap()

        self.qc = dram("qc", (ITS, PARTS, 4 * DH, S))
        self.kc = dram("kc", (ITS, PARTS, 4 * DH if rotary else DH, S))
        self.sums = dram("sums", (4, ITS, S), F32)
        if rotary:
            self.qr = dram("qr", (ITS, PARTS, 4 * DR, S))
            self.kr = dram("kr", (ITS, PARTS, DR, S))
        else:
            self.mx = dram("mx", (PARTS, ITS, 4, S))


def project_a(nc, name, XnT, C, W, scratch, V):
    with Stage(nc, name) as st:
        wd = st.sb("wd", [P, 2, LAT_A])
        wq = st.sb("wq", [LAT_A, P])
        wk = st.sb("wk", [LAT_A, P])
        wv = st.sb("wv", [LAT_A, P])
        wqr = st.sb("wqr", [LAT_A, 2, H * DR])
        wkr = st.sb("wkr", [P, 2, DR])
        xs = st.sb("xs", [P, 2, GW])
        lat = st.sb("lat", [LAT_A, 2, 2, GW])
        NR = H * DR + DR
        cos = st.sb("cos", [NR, S])
        sin = st.sb("sin", [NR, S])
        turn_c = st.sb("turn_c", [NR, GW])
        turn_s = st.sb("turn_s", [NR, GW])
        turned = st.sb("turned", [NR, GW])
        rest = st.sb("rest", [P, 3, GW])
        parts = st.sb("parts", [P, 2, 3, PARTS, GW], BF16)
        p_lat = st.ps("p_lat", [LAT_A, 2, GW])
        p_rot = st.ps("p_rot", [NR, 2, GW])
        p_qk = st.ps("p_qk", [P, 2, GW])
        p_v = st.ps("p_v", [P, GT, P])
        s_w = st.sem("w")
        s_swap = st.sem("swap")
        s_xs = st.sem("xs")
        s_lat = st.sem("lat")
        s_lats = st.sem("lats")
        s_rot = st.sem("rot")
        s_q = st.sem("q")
        s_k = st.sem("k")
        s_v = st.sem("v")
        s_vout = st.sem("vout")
        s_trig = st.sem("trig")
        s_turned = st.sem("turned")
        s_p1 = st.sem("part1")
        s_rest = st.sem("rest")
        s_p2 = st.sem("part2")
        s_p3 = st.sem("part3")
        s_out = [st.sem("out0"), st.sem("out1")]
        NOUT = 4 * HG
        rows = (P, P, NR)
        block = st.block()

        @block.sync
        def _(sp):
            for dst, src in ((wd[:, 0, :], W['W_DQ']), (wd[:, 1, :], W['W_DKV']), (wq[:, :], W['W_UQ']),
                             (wk[:, :], W['W_UK']), (wv[:, :], W['W_UV']), (wqr[:, 0, :], W['W_QR']),
                             (wkr[:, 0, :], W['W_KR']), (cos[:, :], W['cos']), (sin[:, :], W['sin'])):
                sp.dma_start(dst, src).then_inc(s_w, 16)
            sp.sem_inc(s_out[0], 16 * NOUT)
            sp.sem_inc(s_out[1], 16 * NOUT)
            with sp.Fori(0, NG // 2) as r:
                for u in range(2):
                    g = r * 2 + u
                    cols = slice(u * GW, (u + 1) * GW)
                    sp.wait_ge(s_p3, g * 3 + 6)
                    for hg in range(HG):
                        for w, dram, a, n in ((0, scratch.qc, 4 * DH * hg, 4 * DH), (1, scratch.kc, 4 * DH * hg, 4 * DH),
                                              (2, scratch.qr, 4 * DR * hg, 4 * DR), (2, scratch.kr, H * DR, DR)):
                            dst = dram[bass.ds(r * HG + hg, 1), :, :, cols].squeeze(0).rearrange("i e t -> e i t")
                            sp.dma_start(dst, parts[a:a + n, u, w, :, :]).then_inc(s_out[u], 16)
            for u in range(2):
                sp.wait_ge(s_out[u], 16 * NOUT * (NG // 2 + 1))

        @block.gpsimd
        def _(pool):
            pool.wait_ge(s_w, 9 * 16)
            for w in (wqr, wkr):
                pair = w[:, :, :].rearrange("p s (n e) -> p s n e", e=2)
                pool.tensor_copy(pair[:, 1, :, 0], pair[:, 0, :, 1]).then_inc(s_swap, 1)
                pool.tensor_copy(pair[:, 1, :, 1], pair[:, 0, :, 0]).then_inc(s_swap, 1)
            pool.sem_inc(s_p3, 3)
            with pool.Fori(0, NG // 2) as r:
                for u in range(2):
                    g = r * 2 + u
                    pool.wait_ge(s_v, g + 1)
                    pool.tensor_copy(xs[:, u, :], XnT[:, bass.ds(g * GW, GW)]).then_inc(s_xs, 1)
                    pool.wait_ge(s_trig, g * 2 + 2)
                    pool.wait_ge(s_rest, g * 3 + 3)
                    pool.tensor_tensor(turned[:, :], turn_c[:, :], turn_s[:, :], ALU.add).then_inc(s_turned, 1)
                    for w in range(3):
                        n = rows[w]
                        pool.wait_ge(s_p2, g * 3 + w + 1)
                        pool.tensor_tensor(parts[0:n, u, w, 2, :], rest[0:n, w, :], parts[0:n, u, w, 1, :],
                                           ALU.subtract).then_inc(s_p3, 1)

        @block.tensor
        def _(pe):
            pe.wait_ge(s_swap, 4)
            pe.sem_inc(s_v, 2)
            with pe.Fori(0, NG // 2) as r:
                for u in range(2):
                    g = r * 2 + u
                    pe.wait_ge(s_xs, g + 1)
                    pe.wait_ge(s_lats, g + 1)
                    for k in range(2):
                        mm = pe.matmul(p_lat[:, k, :], wd[:, k, :], xs[:, u, :], start=True, stop=True)
                    mm.then_inc(s_lat, 1)
                    pe.wait_ge(s_lats, g + 2)
                    pe.wait_ge(s_turned, g + 1)
                    for k in range(2):
                        pe.matmul(p_rot[0:H * DR, k, :], wqr[:, k, :], lat[:, u, 0, :], start=True, stop=True)
                        mm = pe.matmul(p_rot[H * DR:NR, k, :], wkr[:, k, :], xs[:, u, :], start=True, stop=True)
                    mm.then_inc(s_rot, 1)
                    pe.wait_ge(s_rest, g * 3 + 3)
                    pe.matmul(p_qk[:, 0, :], wq[:, :], lat[:, u, 0, :], start=True, stop=True).then_inc(s_q, 1)
                    pe.matmul(p_qk[:, 1, :], wk[:, :], lat[:, u, 1, :], start=True, stop=True).then_inc(s_k, 1)
                    pe.wait_ge(s_vout, g + 1)
                    for i in range(GT):
                        mm = pe.matmul(p_v[:, i, :], lat[:, u, 1, i * P:(i + 1) * P], wv[:, :], start=True, stop=True)
                    mm.then_inc(s_v, 1)

        @block.scalar
        def _(act):
            act.sem_inc(s_lats, 1)
            with act.Fori(0, NG // 2) as r:
                for u in range(2):
                    g = r * 2 + u
                    act.wait_ge(s_lat, g + 1)
                    act.wait_ge(s_v, g + 1)
                    act.copy(lat[:, u, :, :], p_lat[:, :, :]).then_inc(s_lats, 1)
                    act.wait_ge(s_out[u], 16 * NOUT * (r + 1))
                    for w, ready in ((0, s_q), (1, s_k), (2, s_turned)):
                        n = rows[w]
                        src = turned[:, :] if w == 2 else p_qk[:, w, :]
                        act.wait_ge(ready, g + (2 if w == 2 else 1))
                        act.copy(parts[0:n, u, w, 0, :], src).then_inc(s_p1, 1)
                    for w in range(3):
                        n = rows[w]
                        act.wait_ge(s_rest, g * 3 + w + 4)
                        act.copy(parts[0:n, u, w, 1, :], rest[0:n, w, :]).then_inc(s_p2, 1)

        @block.vector
        def _(dve):
            dve.sem_inc(s_turned, 1)
            dve.sem_inc(s_rest, 3)
            dve.sem_inc(s_vout, 1)
            with dve.Fori(0, NG // 2) as r:
                for u in range(2):
                    g = r * 2 + u
                    cols = slice(u * GW, (u + 1) * GW)
                    dve.wait_ge(s_rot, g + 1)
                    dve.wait_ge(s_turned, g + 1)
                    dve.tensor_tensor(turn_c[:, :], p_rot[:, 0, :], cos[:, cols], ALU.mult).then_inc(s_trig, 1)
                    dve.tensor_tensor(turn_s[:, :], p_rot[:, 1, :], sin[:, cols], ALU.mult).then_inc(s_trig, 1)
                    for w in range(3):
                        n = rows[w]
                        src = turned[:, :] if w == 2 else p_qk[:, w, :]
                        dve.wait_ge(s_p1, g * 3 + w + 1)
                        dve.wait_ge(s_p3, g * 3 + w + 1)
                        dve.tensor_tensor(rest[0:n, w, :], src, parts[0:n, u, w, 0, :], ALU.subtract).then_inc(s_rest, 1)
                    dve.wait_ge(s_v, g + 3)
                    dst = V[:, bass.ds(r * HG, HG), u * GT:(u + 1) * GT, :].rearrange("p g i e -> p i g e")
                    dve.tensor_copy(dst, p_v[:, :, :].rearrange("p i (g e) -> p i g e", g=HG)).then_inc(s_vout, 1)


def attend(nc, name, rows, V, OT, C, scale, clip, load, nload, kh):
    with Stage(nc, name) as st:
        Q = st.sb("Q", [rows, 2, 4, S], BF16)
        K = st.sb("K", [rows, 2, kh, S], BF16)
        Pr = st.sb("Pr", [P, 2, 4, S])
        Vs = st.sb("Vs", [P, 2, TB, kh, 32])
        scores = st.ps("scores", [P, 2, S])
        summed = st.ps("summed", [P, 2, S])
        s_load = [st.sem("load0"), st.sem("load1")]
        s_set = st.sem("set")
        s_ones = st.sem("ones")
        s_vs = st.sem("vs")
        s_scores = st.sem("scores")
        s_exp = st.sem("exp")
        s_clip = st.sem("clip")
        s_sum = st.sem("sum")
        s_ot = st.sem("ot")
        SC0 = 2 * 4 * NSEG
        EX0 = 2
        SU0 = 2 * NSEG
        OT0 = 2
        block = st.block()

        @block.sync
        def _(sp):
            sp.wait_ge(s_ones, 1)
            with sp.Fori(0, ITS // 2) as r:
                for u in range(2):
                    it = r * 2 + u
                    sp.wait_ge(s_scores, it * (4 * NSEG) + SC0 - 4 * NSEG)
                    load(sp, Q, K, it, u, s_load[u])

        @block.gpsimd
        def _(pool):
            pool.memset(K[:, :, :, :], 1.0).then_inc(s_ones, 1)
            pool.memset(Vs[:, :, :, :, :], 0.0).then_inc(s_set, 1)
            pool.wait_ge(s_set, 1)
            pool.memset(Vs[:, :, :, :, DH:DH + 1], 1.0).then_inc(s_set, 1)
            pool.wait_ge(s_set, 2)
            with pool.Fori(0, ITS // 2) as r:
                for u in range(2):
                    it = r * 2 + u
                    pool.wait_ge(s_sum, it * NSEG + SU0 - NSEG)
                    src = V[:, bass.ds(it, 1), :, :].squeeze(1).rearrange("p k (j d) -> p k j d", j=kh)
                    pool.tensor_copy(Vs[:, u, :, :, 0:DH], src).then_inc(s_vs, 1)

        @block.tensor
        def _(pe):
            def make_scores(it, u, k, j):
                n = it * (4 * NSEG) + (4 * k + j)
                pe.wait_ge(s_exp, n + 1)
                out = scores[:, j % 2, :]
                for kb, c0, w in SEGMENTS[k]:
                    keys = K[:, u, j % kh, kb * P:(kb + 1) * P]
                    at = c0
                    while at < c0 + w:
                        end = min(c0 + w, (at // GW + 1) * GW)
                        q0 = kb * P + at - c0
                        mm = pe.matmul(out[:, at:end], keys, Q[:, u, j, q0:q0 + end - at], start=True, stop=True)
                        if not clip and at == c0:
                            mm = pe.matmul(out[:, at:at + P], C["ident_b"][:, :], C["neg_kq_b"][:, :],
                                           start=False, stop=True, skip_group_check=True)
                        at = end
                mm.then_inc(s_scores, 1)

            def pieces(k):
                return [(kb, c0, a, b) for kb, c0, _ in SEGMENTS[k]
                        for a, b in ((kb * P, GW), (max(kb * P, GW), S)) if a < b]

            def sum_values(u, k, some):
                for kb, c0, q0, q1 in some:
                    for j in range(4):
                        mm = pe.matmul(summed[32 * j:32 * j + 32, u, q0:q1], Vs[:, u, kb, j % kh, :],
                                       Pr[:, (u + k) % 2, j, c0 + q0 - kb * P:c0 + q1 - kb * P],
                                       start=(kb == 0), stop=(kb == (3 if q1 == GW else 4)),
                                       skip_group_check=True)
                return mm

            def loads(r, u):
                pe.wait_ge(s_load[u], nload * 16 * (r + 1))

            def iteration(r, u, final):
                it = r * 2 + u
                pe.wait_ge(s_vs, it + 1)
                pe.wait_ge(s_ot, it + 1)
                for k in range(NSEG):
                    ahead = (it, u, k + 1) if k + 1 < NSEG else (it + 1, 1 - u, 0)
                    scored = k + 1 < NSEG or not final
                    if scored:
                        if k + 1 == NSEG:
                            loads(r + u, 1 - u)
                        make_scores(*ahead, 0)
                        make_scores(*ahead, 1)
                    if clip:
                        pe.wait_ge(s_clip, (it * NSEG + k) * 4 + 4)
                    else:
                        pe.wait_ge(s_exp, (it * NSEG + k) * 4 + 4 + EX0)
                    some = pieces(k)
                    cut = (len(some) + 1) // 2
                    mm = sum_values(u, k, some[:cut])
                    if scored:
                        make_scores(*ahead, 2)
                    if some[cut:]:
                        mm = sum_values(u, k, some[cut:])
                    mm.then_inc(s_sum, 1)
                    if scored:
                        make_scores(*ahead, 3)

            pe.sem_inc(s_scores, SC0)
            pe.sem_inc(s_sum, SU0)
            loads(0, 0)
            for j in range(4):
                make_scores(0, 0, 0, j)
            with pe.Fori(0, ITS // 2 - 1) as r:
                iteration(r, 0, False)
                iteration(r, 1, False)
            iteration(ITS // 2 - 1, 0, False)
            iteration(ITS // 2 - 1, 1, True)

        @block.scalar
        def _(act):
            act.sem_inc(s_exp, EX0)
            with act.Fori(0, ITS // 2) as r:
                for u in range(2):
                    it = r * 2 + u
                    for k in range(NSEG):
                        act.wait_ge(s_sum, it * NSEG + (k - 1 + SU0))
                        for j in range(4):
                            n = it * (4 * NSEG) + (4 * k + j)
                            act.wait_ge(s_scores, n + 1 + SC0)
                            w = width(k)
                            act.activation(Pr[:, (u + k) % 2, j, 0:w], scores[:, j % 2, 0:w], ACT.Exp,
                                           scale=scale).then_inc(s_exp, 1)

        @block.vector
        def _(dve):
            dve.sem_inc(s_ot, OT0)
            with dve.Fori(0, ITS // 2) as r:
                for u in range(2):
                    it = r * 2 + u
                    if clip:
                        lo, hi = float(np.exp(-CLIP * scale)), float(np.exp(CLIP * scale))
                        for k in range(NSEG):
                            for j in range(4):
                                n = it * (4 * NSEG) + (4 * k + j)
                                dve.wait_ge(s_exp, n + 1 + EX0)
                                w = Pr[:, (u + k) % 2, j, :]
                                for i, (kb, c0, cols) in enumerate(SEGMENTS[k]):
                                    d = w[:, c0:c0 + P]
                                    ins = dve.scalar_tensor_tensor(out=d, in0=d, scalar=lo, in1=C["top_kq"][:, :],
                                                                   op0=ALU.max, op1=ALU.min)
                                    if cols > P:
                                        e = w[:, c0 + P:c0 + cols]
                                        ins = dve.tensor_scalar(e, e, lo, hi, ALU.max, ALU.min)
                                ins.then_inc(s_clip, 1)
                    dve.wait_ge(s_sum, it * NSEG + (NSEG + SU0))
                    dve.tensor_copy(OT[:, bass.ds(it, 1), :].squeeze(1), summed[:, u, :]).then_inc(s_ot, 1)


def project_out(nc, name, X, OT, C, w_o, scratch):
    with Stage(nc, name) as st:
        wo = st.sb("wo", [P, HG, D])
        even = st.sb("even", [P, GW])
        inv = st.sb("inv", [P, GW])
        heads = st.sb("heads", [P, 2, HG, GW])
        factor = st.ps("factor", [P, HG, GW])
        y = st.ps("y", [P, 2, GT, P])
        s_zero = st.sem("zero")
        s_w = st.sem("w")
        s_even = st.sem("even")
        s_inv = st.sem("inv")
        s_back = st.sem("back")
        s_fac = st.sem("fac")
        s_heads = st.sem("heads")
        s_y = st.sem("y")
        s_res = st.sem("res")
        all_rows = scratch.sums.rearrange("j i (h n) -> (j i h) n", n=GW)
        block = st.block()


        @block.sync
        def _(sp):
            for j in range(4):
                row = 32 * j + DH
                sp.dma_start(scratch.sums[j:j + 1, :, :], OT[row:row + 1, :, :]).then_inc(s_even, 16)
            sp.wait_ge(s_even, 64)
            sp.dma_start(even[:, :], all_rows).then_inc(s_even, 16)
            sp.wait_ge(s_zero, 1)
            src = w_o.rearrange("(g j d) n -> j d g n", g=HG, j=4)
            for j in range(4):
                sp.dma_start(wo[32 * j:32 * j + DH, :, :], src[j]).then_inc(s_w, 16)
            sp.wait_ge(s_inv, 1)
            sp.dma_start(all_rows, inv[:, :]).then_inc(s_back, 16)
            sp.wait_ge(s_back, 16)
            for j in range(4):
                row = 32 * j + DH
                sp.dma_start(OT[row:row + 1, :, :], scratch.sums[j:j + 1, :, :]).then_inc(s_back, 16)

        @block.gpsimd
        def _(pool):
            pool.memset(wo[:, :, :], 0.0).then_inc(s_zero, 1)

        @block.tensor
        def _(pe):
            def spread_inverses(r, u):
                g = r * 2 + u
                for hg in range(HG):
                    pe.wait_ge(s_heads, g * HG + (hg + 1))
                    o = OT[:, bass.ds(r * HG + hg, 1), u * GW:(u + 1) * GW].squeeze(1)
                    pe.matmul(factor[:, hg, :], C["pick_sum"][:, :], o, start=True, stop=True).then_inc(s_fac, 1)

            def product(r, u):
                g = r * 2 + u
                pe.wait_ge(s_heads, g * HG + 2 * HG)
                pe.wait_ge(s_res, g + 1)
                for i in range(GT):
                    for hg in range(HG):
                        mm = pe.matmul(y[:, u, i, :], heads[:, u, hg, i * P:(i + 1) * P], wo[:, hg, :],
                                       start=(hg == 0), stop=(hg == HG - 1))
                mm.then_inc(s_y, 1)

            pe.sem_inc(s_y, 2)
            pe.wait_ge(s_w, 64)
            pe.wait_ge(s_back, 80)
            spread_inverses(0, 0)
            with pe.Fori(0, NG // 2 - 1) as r:
                spread_inverses(r, 1)
                product(r, 0)
                spread_inverses(r + 1, 0)
                product(r, 1)
            spread_inverses(NG // 2 - 1, 1)
            product(NG // 2 - 1, 0)
            product(NG // 2 - 1, 1)

        @block.vector
        def _(dve):
            dve.wait_ge(s_even, 80)
            dve.reciprocal(inv[:, :], even[:, :]).then_inc(s_inv, 1)
            dve.sem_inc(s_heads, HG)
            dve.sem_inc(s_res, 2)

            def scale(r, u):
                g = r * 2 + u
                dve.wait_ge(s_y, g + 1)
                for hg in range(HG):
                    dve.wait_ge(s_fac, g * HG + (hg + 1))
                    o = OT[:, bass.ds(r * HG + hg, 1), u * GW:(u + 1) * GW].squeeze(1)
                    dve.tensor_tensor(heads[:, u, hg, :], factor[:, hg, :], o, ALU.mult).then_inc(s_heads, 1)

            def add(r, u):
                g = r * 2 + u
                dve.wait_ge(s_y, g + 3)
                xt = X[:, bass.ds(g * GT, GT), :]
                dve.tensor_tensor(xt, y[:, u, :, :], xt, ALU.add).then_inc(s_res, 1)

            scale(0, 0)
            with dve.Fori(0, NG // 2 - 1) as r:
                scale(r, 1)
                add(r, 0)
                scale(r + 1, 0)
                add(r, 1)
            scale(NG // 2 - 1, 1)
            add(NG // 2 - 1, 0)
            add(NG // 2 - 1, 1)


def attention_a(nc, name, X, XnT, C, W):
    scratch = Scratch(nc, name, True)
    with ExitStack() as ctx:
        V = ctx.enter_context(nc.sbuf_tensor(f"{name}_V", [P, ITS, TB, 4 * DH], F32))
        project_a(nc, f"{name}p", XnT, C, W, scratch, V)

        def load(sp, Q, K, it, u, sem):
            one = bass.ds(it, 1)
            for i in range(PARTS):
                qc = scratch.qc[one, i, :, :].squeeze(0).rearrange("(j d) t -> d j t", d=DH)
                qr = scratch.qr[one, i, :, :].squeeze(0).rearrange("(j d) t -> d j t", d=DR)
                kc = scratch.kc[one, :, :, :].squeeze(0).rearrange("i (j d) t -> i d j t", d=DH)
                kr = scratch.kr[one, :, :, :].squeeze(0)
                for m in range(PARTS):
                    a, b = (i * PARTS + m) * DH, QC + (i * PARTS + m) * DR
                    sp.dma_start(Q[a:a + DH, u, :, :], qc).then_inc(sem, 16)
                    sp.dma_start(Q[b:b + DR, u, :, :], qr).then_inc(sem, 16)
                    sp.dma_start(K[a:a + DH, u, :, :], kc[m]).then_inc(sem, 16)
                    sp.dma_start(K[b:b + DR, u, :, :],
                                 kr[m:m + 1].rearrange("i d t -> d i t").to_broadcast([DR, 4, S])).then_inc(sem, 16)

        OT = ctx.enter_context(nc.sbuf_tensor(f"{name}_OT", [P, ITS, S], F32))
        attend(nc, f"{name}s", QC + QR, V, OT, C, float((DH + DR) ** -0.5), True, load, 4 * PAIRS, 4)
        project_out(nc, f"{name}o", X, OT, C, W['W_O'], scratch)


def project_b(nc, name, XnT, C, W, scratch, V):
    with Stage(nc, name) as st:
        wd = st.sb("wd", [P, LAT_B])
        wq = st.sb("wq", [LAT_B, P])
        wkv = st.sb("wkv", [LAT_B, 2 * DH])
        lat = st.sb("lat", [LAT_B, 2, GW])
        rest = st.sb("rest", [P, 2, GW])
        parts = st.sb("parts", [P, 2, 2, PARTS, GW], BF16)
        p_lat = st.ps("p_lat", [LAT_B, GW])
        p_q = st.ps("p_q", [P, GW])
        p_k = st.ps("p_k", [DH, GW])
        p_v = st.ps("p_v", [P, GT, P])
        s_w = st.sem("w")
        s_lat = st.sem("lat")
        s_lats = st.sem("lats")
        s_q = st.sem("q")
        s_k = st.sem("k")
        s_v = st.sem("v")
        s_vout = st.sem("vout")
        s_p1 = st.sem("part1")
        s_rest = st.sem("rest")
        s_p2 = st.sem("part2")
        s_p3 = st.sem("part3")
        s_out = [st.sem("out0"), st.sem("out1")]
        NOUT = 2 * HG
        rows = (P, DH)
        banks = (p_q, p_k)
        block = st.block()

        @block.sync
        def _(sp):
            for dst, src in ((wd, W['Wc_down']), (wq, W['Wq_up']), (wkv, W['Wkv_up'])):
                sp.dma_start(dst[:, :], src).then_inc(s_w, 16)
            sp.sem_inc(s_out[0], 16 * NOUT)
            sp.sem_inc(s_out[1], 16 * NOUT)
            with sp.Fori(0, NG // 2) as r:
                for u in range(2):
                    g = r * 2 + u
                    cols = slice(u * GW, (u + 1) * GW)
                    sp.wait_ge(s_p3, g * 2 + 4)
                    for hg in range(HG):
                        for w, dram, a, n in ((0, scratch.qc, 4 * DH * hg, 4 * DH), (1, scratch.kc, 0, DH)):
                            dst = dram[bass.ds(r * HG + hg, 1), :, :, cols].squeeze(0).rearrange("i e t -> e i t")
                            sp.dma_start(dst, parts[a:a + n, u, w, :, :]).then_inc(s_out[u], 16)
            for u in range(2):
                sp.wait_ge(s_out[u], 16 * NOUT * (NG // 2 + 1))

        @block.gpsimd
        def _(pool):
            pool.sem_inc(s_p3, 2)
            with pool.Fori(0, NG // 2) as r:
                for u in range(2):
                    g = r * 2 + u
                    for w in range(2):
                        n = rows[w]
                        pool.wait_ge(s_p2, g * 2 + w + 1)
                        pool.tensor_tensor(parts[0:n, u, w, 2, :], rest[0:n, w, :], parts[0:n, u, w, 1, :],
                                           ALU.subtract).then_inc(s_p3, 1)

        @block.tensor
        def _(pe):
            pe.wait_ge(s_w, 48)
            pe.sem_inc(s_v, 2)
            with pe.Fori(0, NG // 2) as r:
                for u in range(2):
                    g = r * 2 + u
                    pe.wait_ge(s_lats, g + 1)
                    pe.matmul(p_lat[:, :], wd[:, :], XnT[:, bass.ds(g * GW, GW)], start=True,
                              stop=True).then_inc(s_lat, 1)
                    pe.wait_ge(s_lats, g + 2)
                    pe.wait_ge(s_rest, g * 2 + 2)
                    pe.matmul(p_q[:, :], wq[:, :], lat[:, u, :], start=True, stop=True).then_inc(s_q, 1)
                    pe.matmul(p_k[:, :], wkv[:, 0:DH], lat[:, u, :], start=True, stop=True).then_inc(s_k, 1)
                    pe.wait_ge(s_vout, g + 1)
                    for i in range(GT):
                        mm = pe.matmul(p_v[:, i, 0:DH], lat[:, u, i * P:(i + 1) * P], wkv[:, DH:2 * DH],
                                       start=True, stop=True)
                    mm.then_inc(s_v, 1)

        @block.scalar
        def _(act):
            act.sem_inc(s_lats, 1)
            with act.Fori(0, NG // 2) as r:
                for u in range(2):
                    g = r * 2 + u
                    act.wait_ge(s_lat, g + 1)
                    act.wait_ge(s_v, g + 1)
                    act.copy(lat[:, u, :], p_lat[:, :]).then_inc(s_lats, 1)
                    act.wait_ge(s_out[u], 16 * NOUT * (r + 1))
                    for w, ready in ((0, s_q), (1, s_k)):
                        act.wait_ge(ready, g + 1)
                        act.copy(parts[0:rows[w], u, w, 0, :], banks[w][:, :]).then_inc(s_p1, 1)
                    for w in range(2):
                        n = rows[w]
                        act.wait_ge(s_rest, g * 2 + w + 3)
                        act.copy(parts[0:n, u, w, 1, :], rest[0:n, w, :]).then_inc(s_p2, 1)

        @block.vector
        def _(dve):
            dve.sem_inc(s_rest, 2)
            dve.sem_inc(s_vout, 1)
            with dve.Fori(0, NG // 2) as r:
                for u in range(2):
                    g = r * 2 + u
                    for w in range(2):
                        n = rows[w]
                        dve.wait_ge(s_p1, g * 2 + w + 1)
                        dve.wait_ge(s_p3, g * 2 + w + 1)
                        dve.tensor_tensor(rest[0:n, w, :], banks[w][:, :], parts[0:n, u, w, 0, :],
                                          ALU.subtract).then_inc(s_rest, 1)
                    dve.wait_ge(s_v, g + 3)
                    dst = V[:, bass.ds(r * HG, HG), u * GT:(u + 1) * GT, :]
                    src = p_v[:, :, 0:DH].rearrange("p (o i) e -> p o i e", o=1).to_broadcast([P, HG, GT, DH])
                    dve.tensor_copy(dst, src).then_inc(s_vout, 1)


ROW_SEGMENTS = [[(7, 0, 1024)], [(6, 0, 896), (0, 896, 128)], [(5, 0, 768), (1, 768, 256)],
                [(4, 0, 640), (2, 640, 384)], [(3, 0, 512)]]


def row_maxima(nc, name, C, load, nload, M):
    NS4 = 4
    with Stage(nc, name) as st:
        Q = st.sb("Q", [QC, 2, 4, S], BF16)
        K = st.sb("K", [QC, 2, 1, S], BF16)
        top = st.sb("top", [P, 2, 4, TB])
        scores = st.ps("scores", [P, NS4, S])
        s_load = [st.sem("load0"), st.sem("load1")]
        s_scores = st.sem("scores")
        s_max = st.sem("max")
        s_kept = st.sem("kept")
        SC0 = 2 * 4 * NSEG
        block = st.block()

        @block.sync
        def _(sp):
            with sp.Fori(0, ITS // 2) as r:
                for u in range(2):
                    it = r * 2 + u
                    sp.wait_ge(s_scores, it * (4 * NSEG) + SC0 - 4 * NSEG)
                    load(sp, Q, K, it, u, s_load[u])

        @block.tensor
        def _(pe):
            pe.sem_inc(s_scores, SC0)
            with pe.Fori(0, ITS // 2) as r:
                for u in range(2):
                    it = r * 2 + u
                    pe.wait_ge(s_load[u], nload * 16 * (r + 1))
                    for c in range(4 * NSEG):
                        j, k = c // NSEG, c % NSEG
                        pe.wait_ge(s_max, it * (4 * NSEG) + (c + 1))
                        out = scores[:, c % NS4, :]
                        for qb, c0, w in ROW_SEGMENTS[k]:
                            at = c0
                            while at < c0 + w:
                                end = min(c0 + w, (at // GW + 1) * GW)
                                mm = pe.matmul(out[:, at:end], Q[:, u, j, qb * P:(qb + 1) * P],
                                               K[:, u, 0, at - c0:end - c0], start=True, stop=True)
                                at = end
                            mm = pe.matmul(out[:, at - P:at], C["ident_b"][:, :], C["neg_qk_b"][:, :],
                                           start=False, stop=True, skip_group_check=True)
                        mm.then_inc(s_scores, 1)

        @block.vector
        def _(dve):
            dve.sem_inc(s_max, NS4)
            with dve.Fori(0, ITS // 2) as r:
                for u in range(2):
                    it = r * 2 + u
                    for c in range(4 * NSEG):
                        j, k = c // NSEG, c % NSEG
                        dve.wait_ge(s_scores, it * (4 * NSEG) + (c + 1 + SC0))
                        for qb, c0, w in ROW_SEGMENTS[k]:
                            ins = dve.reduce_max(top[:, u, j, qb:qb + 1], scores[:, c % NS4, c0:c0 + w], AX_X)
                        ins.then_inc(s_max, 1)
                    dve.wait_ge(s_max, it * (4 * NSEG) + (4 * NSEG + NS4))
                    dve.tensor_copy(M[:, bass.ds(it * 4 * TB, 4 * TB)],
                                    top[:, u, :, :].rearrange("p j k -> p (j k)")).then_inc(s_kept, 1)


def send_maxima(nc, name, C, M, scratch):
    with Stage(nc, name) as st:
        turned = st.ps("turned", [P, B, P])
        neg = st.sb("neg", [P, B, P])
        rest = st.sb("rest", [P, B, P])
        parts = st.sb("parts", [P, PARTS, B, P], BF16)
        s_turn = st.sem("turn")
        s_step = st.sem("step")
        s_out = st.sem("out")
        block = st.block()

        @block.tensor
        def _(pe):
            for b in range(B):
                mm = pe.transpose(turned[:, b, :], M[:, b * P:(b + 1) * P], C["ident"][:, :])
            mm.then_inc(s_turn, 1)

        @block.vector
        def _(dve):
            dve.wait_ge(s_turn, 1)
            dve.tensor_scalar(neg[:, :, :], turned[:, :, :], -1.0, None, ALU.mult).then_inc(s_step, 1)
            src = neg
            for i in range(PARTS):
                dve.wait_ge(s_step, 2 * i + 1)
                dve.tensor_copy(parts[:, i, :, :], src[:, :, :]).then_inc(s_step, 1)
                if i < PARTS - 1:
                    dve.wait_ge(s_step, 2 * i + 2)
                    dve.tensor_tensor(rest[:, :, :], src[:, :, :], parts[:, i, :, :], ALU.subtract).then_inc(s_step, 1)
                    src = rest

        @block.sync
        def _(sp):
            sp.wait_ge(s_step, 2 * PARTS)
            for i in range(PARTS):
                dst = scratch.mx[i].rearrange("(b g) j (k q) -> (g j k) b q", g=HG, q=P)
                sp.dma_start(dst, parts[:, i, :, :]).then_inc(s_out, 16)
            sp.wait_ge(s_out, 16 * PARTS)


def attention_b(nc, name, X, XnT, C, W):
    scratch = Scratch(nc, name, False)
    with ExitStack() as ctx:
        V = ctx.enter_context(nc.sbuf_tensor(f"{name}_V", [P, ITS, TB, DH], F32))
        M = ctx.enter_context(nc.sbuf_tensor(f"{name}_M", [P, ITS * 4 * TB], F32))
        project_b(nc, f"{name}p", XnT, C, W, scratch, V)

        def load(sp, Q, K, it, u, sem):
            one = bass.ds(it, 1)
            kc = scratch.kc[one, :, :, :].squeeze(0)
            for i in range(PARTS):
                qc = scratch.qc[one, i, :, :].squeeze(0).rearrange("(j d) t -> d j t", d=DH)
                for m in range(PARTS):
                    a = (i * PARTS + m) * DH
                    sp.dma_start(Q[a:a + DH, u, :, :], qc).then_inc(sem, 16)
                    sp.dma_start(K[a:a + DH, u, 0, :], kc[m]).then_inc(sem, 16)

        def load_with_maxima(sp, Q, K, it, u, sem):
            load(sp, Q, K, it, u, sem)
            sp.dma_start(Q[QC:QC + PARTS, u, :, :],
                         scratch.mx[:, bass.ds(it, 1), :, :].squeeze(1)).then_inc(sem, 16)

        row_maxima(nc, f"{name}m", C, load, 2 * PAIRS, M)
        send_maxima(nc, f"{name}t", C, M, scratch)
        OT = ctx.enter_context(nc.sbuf_tensor(f"{name}_OT", [P, ITS, S], F32))
        attend(nc, f"{name}s", QC + PARTS, V, OT, C, float(DH ** -0.5), False, load_with_maxima, 2 * PAIRS + 1, 1)
        project_out(nc, f"{name}o", X, OT, C, W['Wc_proj'], scratch)


def recurrence(nc, name, X, XnT, C, W):
    with Stage(nc, name) as st:
        wl = st.sb("wl", [NS, 2, P])
        wlT = st.sb("wlT", [P, 2, NS])
        wc = st.sb("wc", [P, B, NS])
        wcT = st.sb("wcT", [P, P])
        bl = st.sb("bl", [P, 1])
        dp = st.sb("dp", [P, 1])
        diag = st.sb("diag", [P, P])
        lam = st.sb("lam", [P, S])
        states = st.sb("states", [P, S])
        p_w = st.ps("p_w", [P, GW])
        z = st.ps("z", [P, S])
        bu = st.ps("bu", [P, S])
        y = st.ps("y", [P, 2, GT, P])
        s_w = st.sem("w")
        s_turn = st.sem("turn")
        s_wT = st.sem("wT")
        s_z = st.sem("z")
        s_bu = st.sem("bu")
        s_lam = st.sem("lam")
        s_scan = st.sem("scan")
        s_y = st.sem("y")
        s_res = st.sem("res")
        block = st.block()

        @block.sync
        def _(sp):
            sp.dma_start(wl[:, 0, :], W['Wl']).then_inc(s_w, 16)
            sp.dma_start(wl[:, 1, :], W['Wb']).then_inc(s_w, 16)
            sp.dma_start(dp[:, :], W['Dp'].rearrange("(p o) -> p o", o=1)).then_inc(s_w, 16)
            for b in range(B):
                sp.dma_start(wc[:, b, :], W['Wc']).then_inc(s_w, 16)
                sp.dma_start(bl[b * NS:(b + 1) * NS, :], W['bl'].rearrange("(p o) -> p o", o=1)).then_inc(s_w, 16)

        @block.tensor
        def _(pe):
            pe.wait_ge(s_w, 16 * (3 + 2 * B))
            for k in range(2):
                pe.transpose(p_w[:, k * NS:(k + 1) * NS], wl[:, k, :], C["ident"][0:NS, 0:NS])
            pe.transpose(p_w[:, P:2 * P], wc[:, :, :], C["ident"][:, :]).then_inc(s_turn, 1)
            pe.wait_ge(s_wT, 3)
            for k, (dst, sem) in enumerate(((z, s_z), (bu, s_bu))):
                for half in range(2):
                    for b in range(B):
                        cols = slice(half * GW, (half + 1) * GW)
                        t0 = b * S + half * GW
                        mm = pe.matmul(dst[b * NS:(b + 1) * NS, cols], wlT[:, k, :], XnT[:, t0:t0 + GW],
                                       start=True, stop=True)
                mm.then_inc(sem, 1)
            pe.wait_ge(s_scan, 1)
            for g in range(NG):
                b = g // 2
                if g >= 2:
                    pe.wait_ge(s_res, g - 1)
                for i in range(GT):
                    t = g * GT + i
                    at = (t % TB) * P
                    pe.matmul(y[:, g % 2, i, :], states[b * NS:(b + 1) * NS, at:at + P],
                              wcT[b * NS:(b + 1) * NS, :], start=True, stop=False)
                    mm = pe.matmul(y[:, g % 2, i, :], XnT[:, t * P:(t + 1) * P], diag[:, :], start=False, stop=True)
                mm.then_inc(s_y, 1)

        @block.scalar
        def _(act):
            act.wait_ge(s_z, 1)
            act.activation(lam[:, :], z[:, :], ACT.Sigmoid, bias=bl[:, 0:1]).then_inc(s_lam, 1)

        @block.vector
        def _(dve):
            dve.wait_ge(s_turn, 1)
            dve.tensor_copy(wlT[:, :, :], p_w[:, 0:2 * NS].rearrange("p (k n) -> p k n", k=2)).then_inc(s_wT, 1)
            dve.tensor_copy(wcT[:, :], p_w[:, P:2 * P]).then_inc(s_wT, 1)
            dve.tensor_scalar(diag[:, :], C["ident"][:, :], dp[:, 0:1], None, ALU.mult).then_inc(s_wT, 1)
            dve.wait_ge(s_bu, 1)
            dve.wait_ge(s_lam, 1)
            dve.tensor_tensor_scan(states[:, :], lam[:, :], bu[:, :], 0.0, ALU.mult, ALU.add).then_inc(s_scan, 1)
            for g in range(NG):
                dve.wait_ge(s_y, g + 1)
                xt = X[:, g * GT:(g + 1) * GT, :]
                dve.tensor_tensor(xt, y[:, g % 2, :, :], xt, ALU.add).then_inc(s_res, 1)


LIMIT, ALPHA = 7.0, 1.702
ROUTE_AT = 32
FAR = -3.0e38


class Experts:

    def __init__(self, nc, ctx):
        def sb(n, shape, dt=F32):
            return ctx.enter_context(nc.sbuf_tensor(f"experts_{n}", shape, dt))

        self.w1T = sb("w1T", [P, E, P])
        self.w2T = sb("w2T", [P, E, P])
        self.b1 = sb("b1", [P, E])
        self.b2 = sb("b2", [E, P])
        self.gwT = sb("gwT", [P, E])
        self.gb = sb("gb", [P, E])
        self.pick = sb("pick", [96, E, P], BF16)


def load_experts(nc, name, C, W, X_):
    with Stage(nc, name) as st:
        raw = st.sb("raw", [P, 2, E, P])
        b1raw = st.sb("b1raw", [E, 2 * P])
        gw = st.sb("gw", [E, P])
        turned = st.ps("turned", [P, 2, GT, P])
        small = st.ps("small", [P, 2 * E])
        s_w = st.sem("w")
        s_zero = st.sem("zero")
        s_turn = st.sem("turn")
        s_out = st.sem("out")
        s_small = st.sem("small")
        NB = 2 * E // GT
        block = st.block()

        @block.sync
        def _(sp):
            sp.dma_start(raw[:, 0, :, :], W['mlp1_w'].rearrange("e (i s) h -> s i e h", s=2)[0]).then_inc(s_w, 16)
            sp.dma_start(raw[:, 1, :, :], W['mlp2_w'].rearrange("e i h -> i e h")).then_inc(s_w, 16)
            sp.dma_start(b1raw[:, :], W['mlp1_b']).then_inc(s_w, 16)
            sp.dma_start(gw[:, :], W['gate_w']).then_inc(s_w, 16)
            sp.dma_start(X_.b2[:, :], W['mlp2_b']).then_inc(s_w, 16)
            sp.dma_start(X_.gb[:, :], W['gate_b'].rearrange("(o e) -> o e", o=1).to_broadcast([P, E])).then_inc(s_w, 16)

        @block.tensor
        def _(pe):
            pe.wait_ge(s_w, 96)
            pe.transpose(small[:, 0:E], b1raw[:, :].rearrange("e (i s) -> e s i", s=2)[:, 0, :], C["ident"][0:E, 0:E])
            pe.transpose(small[:, E:2 * E], gw[:, :], C["ident"][0:E, 0:E]).then_inc(s_small, 1)
            for n in range(NB):
                if n >= 2:
                    pe.wait_ge(s_out, n - 1)
                for i in range(GT):
                    k, e = n // (NB // 2), (n % (NB // 2)) * GT + i
                    mm = pe.transpose(turned[:, n % 2, i, :], raw[:, k, e, :], C["ident"][:, :])
                mm.then_inc(s_turn, 1)

        @block.vector
        def _(dve):
            dve.wait_ge(s_small, 1)
            dve.tensor_copy(X_.b1[:, :], small[:, 0:E]).then_inc(s_zero, 1)
            dve.tensor_copy(X_.gwT[:, :], small[:, E:2 * E]).then_inc(s_zero, 1)
            dve.tensor_copy(X_.pick[:, :, :], C["pick_row"][:, :].rearrange("k (e o) -> k e o", o=1)
                            .to_broadcast([96, E, P])).then_inc(s_zero, 1)

        @block.scalar
        def _(act):
            for n in range(NB):
                act.wait_ge(s_turn, n + 1)
                e = (n % (NB // 2)) * GT
                dst = (X_.w1T, X_.w2T)[n // (NB // 2)]
                act.copy(dst[:, e:e + GT, :], turned[:, n % 2, :, :]).then_inc(s_out, 1)


def route(nc, name, XnT, C, X_, routeT, routes_b):
    with Stage(nc, name) as st:
        gates = st.sb("gates", [P, NT, E + 8])
        rest_g = st.sb("rest_g", [P, NT, E + 8])
        best = st.sb("best", [P, NT, 8])
        taken = st.sb("taken", [P, NT, E])
        diff = st.sb("diff", [P, NT, E])
        weight = st.sb("weight", [P, NT, E])
        kept = st.sb("kept", [P, NT, E])
        total = st.sb("total", [P, NT])
        inv = st.sb("inv", [P, NT])
        routes = st.sb("routes", [P, NT, E])
        rest = st.sb("rest", [E, 2, TOK // 2])
        logits = st.ps("logits", [P, NT, E])
        turned = st.ps("turned", [E, TOK // 2])
        s_far = st.sem("far")
        s_clear = st.sem("clear")
        s_log = st.sem("log")
        s_gate = st.sem("gate")
        s_best = st.sem("best")
        s_four = st.sem("four")
        s_left = st.sem("left")
        s_diff = st.sem("diff")
        s_exp = st.sem("exp")
        s_step = st.sem("step")
        s_turn = st.sem("turn")
        s_whole = st.sem("whole")
        s_part = st.sem("part")
        block = st.block()

        @block.gpsimd
        def _(pool):
            pool.memset(gates[:, :, E:E + 8], FAR).then_inc(s_far, 1)
            pool.memset(routes_b[:, :], 0.0).then_inc(s_clear, 1)

        @block.tensor
        def _(pe):
            for t in range(NT):
                mm = pe.matmul(logits[:, t, :], XnT[:, t * P:(t + 1) * P], X_.gwT[:, :], start=True, stop=True)
            mm.then_inc(s_log, 1)
            pe.wait_ge(s_step, 5)
            for half in range(2):
                if half:
                    pe.wait_ge(s_part, PARTS + 2)
                for i in range(NT // 2):
                    mm = pe.transpose(turned[:, i * P:(i + 1) * P], routes[:, half * NT // 2 + i, :], C["ident"][:, :])
                mm.then_inc(s_turn, 1)

        @block.scalar
        def _(act):
            act.wait_ge(s_diff, 1)
            act.activation(weight[:, :, :], diff[:, :, :], ACT.Exp).then_inc(s_exp, 1)
            for half in range(2):
                act.wait_ge(s_turn, half + 1)
                act.wait_ge(s_part, half * (PARTS + 2)) if half else None
                act.copy(routeT[:, half * TOK // 2:(half + 1) * TOK // 2], turned[:, :]).then_inc(s_whole, 1)

        @block.vector
        def _(dve):
            dve.wait_ge(s_log, 1)
            gb = X_.gb[:, :].rearrange("p (o e) -> p o e", o=1).to_broadcast([P, NT, E])
            dve.tensor_tensor(gates[:, :, 0:E], logits[:, :, :], gb, ALU.add).then_inc(s_gate, 1)
            dve.wait_ge(s_gate, 1)
            dve.wait_ge(s_far, 1)
            for t in range(NT):
                dve.max(best[:, t, :], gates[:, t, 0:E]).then_inc(s_best, 1)
            dve.wait_ge(s_best, NT)
            dve.tensor_tensor(diff[:, :, :], gates[:, :, 0:E], best[:, :, 0:1].to_broadcast([P, NT, E]),
                              ALU.subtract).then_inc(s_diff, 1)
            dve.memset(best[:, :, TOPK:8], FAR).then_inc(s_four, 1)
            dve.wait_ge(s_four, 1)
            for t in range(NT):
                dve.match_replace(rest_g[:, t, :], best[:, t, :], gates[:, t, :], FAR).then_inc(s_left, 1)
            dve.wait_ge(s_left, NT)
            dve.tensor_scalar(taken[:, :, :], rest_g[:, :, 0:E], FAR, None, ALU.is_equal).then_inc(s_step, 1)
            dve.wait_ge(s_step, 1)
            dve.wait_ge(s_exp, 1)
            dve.tensor_tensor(kept[:, :, :], weight[:, :, :], taken[:, :, :], ALU.mult).then_inc(s_step, 1)
            dve.wait_ge(s_step, 2)
            dve.reduce_sum(total[:, :], kept[:, :, :], AX_X).then_inc(s_step, 1)
            dve.wait_ge(s_step, 3)
            dve.reciprocal(inv[:, :], total[:, :]).then_inc(s_step, 1)
            dve.wait_ge(s_step, 4)
            dve.tensor_tensor(routes[:, :, :], kept[:, :, :], spread(inv[:, :], E), ALU.mult).then_inc(s_step, 1)
            dve.wait_ge(s_clear, 1)
            for half in range(2):
                cols = slice(half * TOK // 2, (half + 1) * TOK // 2)
                dve.wait_ge(s_whole, half + 1)
                src = routeT[:, cols]
                base = half * (PARTS + 2)
                for i in range(PARTS):
                    part = routes_b[i * ROUTE_AT:i * ROUTE_AT + E, cols]
                    dve.wait_ge(s_part, base + 2 * i) if base + 2 * i else None
                    dve.tensor_copy(part, src).then_inc(s_part, 1)
                    if i < PARTS - 1:
                        dve.wait_ge(s_part, base + 2 * i + 1)
                        dve.tensor_tensor(rest[:, i % 2, :], src, part, ALU.subtract).then_inc(s_part, 1)
                        src = rest[:, i % 2, :]


def experts(nc, name, X, XnT, C, X_, routeT, routes_b):
    with Stage(nc, name) as st:
        limited = st.sb("limited", [P, 2, GW])
        glu = st.sb("glu", [P, 2, GW])
        hidden = st.sb("hidden", [P, 2, GW])
        r_slot = st.sb("r_slot", [E, 2, GW])
        h = st.ps("h", [P, 2, GW])
        r_all = st.ps("r_all", [P, 2, GW])
        y = st.ps("y", [P, 2, GT, P])
        s_rs = st.sem("rs")
        s_h = st.sem("h")
        s_lim = st.sem("lim")
        s_glu = st.sem("glu")
        s_hid = st.sem("hid")
        s_r = st.sem("r")
        s_y = st.sem("y")
        s_res = st.sem("res")
        block = st.block()

        @block.tensor
        def _(pe):
            def up(g, e):
                n = g * E + e
                pe.wait_ge(s_lim, n + 1)
                pe.matmul(h[:, e % 2, :], X_.w1T[:, e, :], XnT[:, bass.ds(g * GW, GW)], start=True,
                          stop=True).then_inc(s_h, 1)

            def spread_route(g, e):
                n = g * E + e
                pe.wait_ge(s_hid, n + 1)
                pe.matmul(r_all[:, e % 2, :], X_.pick[:, e, :], routes_b[:, bass.ds(g * GW, GW)], start=True,
                          stop=True).then_inc(s_r, 1)

            def later(g, e):
                return (g, e) if e < E else (g + 1, e - E)

            def group(g, u, final):
                pe.wait_ge(s_res, g + 1)
                pe.wait_ge(s_rs, g + 1)
                for i in range(GT):
                    pe.matmul(y[:, u, i, :], r_slot[:, u, i * P:(i + 1) * P], X_.b2[:, :], start=(i == 0),
                              stop=False, skip_group_check=True)
                for e in range(E):
                    if not final or e + 2 < E:
                        up(*later(g, e + 2))
                    if not final or e + 1 < E:
                        spread_route(*later(g, e + 1))
                    pe.wait_ge(s_hid, g * E + (e + 3))
                    for i in range(GT):
                        mm = pe.matmul(y[:, u, i, :], hidden[:, e % 2, i * P:(i + 1) * P], X_.w2T[:, e, :],
                                       start=False, stop=(e == E - 1), skip_group_check=True)
                    mm.then_inc(s_y, 1)

            pe.sem_inc(s_y, 2 * E)
            up(0, 0)
            up(0, 1)
            spread_route(0, 0)
            with pe.Fori(0, NG // 2 - 1) as r:
                for u in range(2):
                    group(r * 2 + u, u, False)
            group(NG - 2, 0, False)
            group(NG - 1, 1, True)

        @block.scalar
        def _(act):
            with act.Fori(0, NG // 2) as r:
                for u in range(2):
                    g = r * 2 + u
                    act.wait_ge(s_y, g * E + E)
                    act.copy(r_slot[:, u, :], routeT[:, bass.ds(g * GW, GW)]).then_inc(s_rs, 1)
                    for e in range(E):
                        n = g * E + e
                        act.wait_ge(s_lim, n + 3)
                        act.wait_ge(s_hid, n + 1)
                        act.activation(glu[:, e % 2, :], limited[:, e % 2, :], ACT.Gelu_apprx_sigmoid).then_inc(s_glu, 1)

        @block.vector
        def _(dve):
            def limit(g, e):
                n = g * E + e
                dve.wait_ge(s_h, n + 1)
                dve.wait_ge(s_glu, n + 1)
                dve.tensor_scalar(limited[:, e % 2, :], h[:, e % 2, :], X_.b1[:, e:e + 1], LIMIT,
                                  ALU.add, ALU.min).then_inc(s_lim, 1)

            def weigh(g, e):
                n = g * E + e
                dve.wait_ge(s_glu, n + 3)
                dve.wait_ge(s_r, n + 1)
                dve.wait_ge(s_y, n + (2 * E - 1))
                dve.scalar_tensor_tensor(out=hidden[:, e % 2, :], in0=glu[:, e % 2, :], scalar=LIMIT + 1.0,
                                         in1=r_all[:, e % 2, :], op0=ALU.mult, op1=ALU.mult).then_inc(s_hid, 1)

            def group(g, u, final):
                for e in range(E):
                    if e + 1 < E:
                        limit(g, e + 1)
                    elif not final:
                        limit(g + 1, 0)
                    weigh(g, e)
                dve.wait_ge(s_y, g * E + 3 * E)
                xt = X[:, bass.ds(g * GT, GT), :]
                dve.tensor_tensor(xt, y[:, u, :, :], xt, ALU.add).then_inc(s_res, 1)

            dve.sem_inc(s_lim, 2)
            dve.sem_inc(s_hid, 2)
            dve.sem_inc(s_glu, 2)
            dve.sem_inc(s_res, 2)
            limit(0, 0)
            with dve.Fori(0, NG // 2 - 1) as r:
                for u in range(2):
                    group(r * 2 + u, u, False)
            group(NG - 2, 0, False)
            group(NG - 1, 1, True)


NCH = S // P
LEVELS = 7
PROJ = 3 * P + 2


def chunk(t, c):
    if len(t.shape) == 2:
        return t[:, :].rearrange("p (b c n) -> p b c n", b=B, n=P)[:, :, bass.ds(c, 1), :].squeeze(2)
    return t[:, :, :].rearrange("p (b c) n -> p b c n", b=B)[:, :, bass.ds(c, 1), :].squeeze(2)


def scalars(t, c):
    a = t.rearrange("p (b c) -> p b c", b=B)[:, :, bass.ds(c, 1)]
    return a.to_broadcast([P, B, P])


def delta_project(nc, name, XnT, C, W, Kt, Vt, Gt, qT, wo, cols):
    with Stage(nc, name) as st:
        raw = st.sb("raw", [P, 5, P])
        rawab = st.sb("rawab", [1, 2, P])
        wT = st.sb("wT", [P, P])
        wall = st.sb("wall", [P, PROJ])
        brow = st.sb("brow", [1, PROJ])
        bq = st.sb("bq", [P, 1])
        xs = st.sb("xs", [P, 2, GW])
        sq = st.sb("sq", [P, GT, P])
        logit = st.sb("logit", [P, 2, NT])
        length = st.sb("length", [P, NT])
        tmp = st.sb("tmp", [P, 6, NT])
        p_q = st.ps("p_q", [P, GW])
        p_all = st.ps("p_all", [P, GT, GW])
        p_w = st.ps("p_w", [P, 2, GT, P])
        s_w = st.sem("w")
        s_turn = st.sem("turn")
        s_wT = st.sem("wT")
        s_xs = st.sem("xs")
        s_q = st.sem("q")
        s_all = st.sem("all")
        s_qo = st.sem("qo")
        s_kv = st.sem("kv")
        s_gate = st.sem("gate")
        s_sq = st.sem("sq")
        s_len = st.sem("len")
        s_fin = st.sem("fin")
        s_act = st.sem("act")
        s_sum = st.sem("sum")
        names = ('Wq', 'Wk', 'Wv', 'Wg', 'Wo')
        block = st.block()

        @block.sync
        def _(sp):
            for i, n in enumerate(names):
                sp.dma_start(raw[:, i, :], W[n]).then_inc(s_w, 16)
            for i, n in enumerate(('Wa', 'Wb')):
                sp.dma_start(rawab[:, i, :], W[n]).then_inc(s_w, 16)
            sp.dma_start(bq[:, :], W['bq'].rearrange("(p o) -> p o", o=1)).then_inc(s_w, 16)
            for at, n in ((0, 'bk'), (P, 'bv'), (2 * P, 'bg'), (3 * P, 'ba'), (3 * P + 1, 'bb')):
                m = W[n].shape[0]
                sp.dma_start(brow[:, at:at + m], W[n].rearrange("(o n) -> o n", o=1)).then_inc(s_w, 16)

        @block.gpsimd
        def _(pool):
            with pool.Fori(0, NG // 2) as r:
                for u in range(2):
                    g = r * 2 + u
                    pool.wait_ge(s_all, g + 1)
                    pool.tensor_copy(xs[:, u, :], XnT[:, bass.ds(g * GW, GW)]).then_inc(s_xs, 1)

        @block.tensor
        def _(pe):
            pe.wait_ge(s_w, 16 * 13)
            for i in range(5):
                pe.transpose(p_w[:, i // GT, i % GT, :], raw[:, i, :], C["ident"][:, :])
            for i in range(2):
                mm = pe.transpose(p_w[:, 1, 1 + i, 0:1], rawab[:, i, :], C["ident"][0:1, 0:1])
            mm.then_inc(s_turn, 1)
            pe.sem_inc(s_all, 2)
            pe.wait_ge(s_wT, 4)
            with pe.Fori(0, NG // 2) as r:
                for u in range(2):
                    g = r * 2 + u
                    pe.wait_ge(s_xs, g + 1)
                    pe.wait_ge(s_qo, g + 1)
                    pe.matmul(p_q[:, :], wT[:, :], xs[:, u, :], start=True, stop=True).then_inc(s_q, 1)
                    pe.wait_ge(s_kv, g + 1)
                    pe.wait_ge(s_gate, g + 1)
                    for i in range(GT):
                        pe.matmul(p_all[:, i, 0:PROJ], C["ones"][0:1, :], brow[:, :], start=True, stop=False)
                        mm = pe.matmul(p_all[:, i, 0:PROJ], xs[:, u, i * P:(i + 1) * P], wall[:, :], start=False, stop=True)
                    mm.then_inc(s_all, 1)
            pe.wait_ge(s_fin, 8)
            for i, w in enumerate(("upto", "after", "ones")):
                mm = pe.matmul(p_w[:, 0, 0, i * NT:(i + 1) * NT], C[w][:, :], cols["la"][:, :], start=True, stop=True)
            mm.then_inc(s_sum, 1)

        @block.scalar
        def _(act):
            act.sem_inc(s_qo, 1)
            act.sem_inc(s_gate, 1)
            with act.Fori(0, NG // 2) as r:
                for u in range(2):
                    g = r * 2 + u
                    act.wait_ge(s_q, g + 1)
                    act.activation(qT[:, bass.ds(g * GW, GW)], p_q[:, :], ACT.Identity, bias=bq[:, 0:1]).then_inc(s_qo, 1)
                    act.wait_ge(s_all, g + 3)
                    act.activation(sq[:, :, :], p_all[:, :, 0:P], ACT.Square).then_inc(s_sq, 1)
                    act.activation(Gt[:, bass.ds(g * GT, GT), :], p_all[:, :, 2 * P:3 * P], ACT.Sigmoid).then_inc(s_gate, 1)
                    act.wait_ge(s_len, g + 1)
            act.wait_ge(s_kv, NG + 1)
            act.activation(cols["beta"][:, :], logit[:, 1, :], ACT.Sigmoid).then_inc(s_act, 1)
            act.wait_ge(s_fin, 1)
            act.activation(tmp[:, 1, :], tmp[:, 0, :], ACT.Exp, scale=-1.0).then_inc(s_act, 1)
            act.wait_ge(s_fin, 2)
            act.activation(tmp[:, 3, :], tmp[:, 2, :], ACT.Ln).then_inc(s_act, 1)
            act.activation(tmp[:, 4, :], length[:, :], ACT.Sqrt).then_inc(s_act, 1)
            act.wait_ge(s_sum, 1)
            for i, n in enumerate(("upto", "after", "whole")):
                act.activation(cols[n][:, :], p_w[:, 0, 0, i * NT:(i + 1) * NT], ACT.Exp).then_inc(s_act, 1)

        @block.vector
        def _(dve):
            dve.wait_ge(s_turn, 1)
            dve.tensor_copy(wT[:, :], p_w[:, 0, 0, :]).then_inc(s_wT, 1)
            dve.tensor_copy(wall[:, 0:3 * P], p_w[:, 0, 1:4, :].rearrange("p k n -> p (k n)")).then_inc(s_wT, 1)
            dve.tensor_copy(wo[:, :], p_w[:, 1, 0, :]).then_inc(s_wT, 1)
            dve.tensor_copy(wall[:, 3 * P:PROJ], p_w[:, 1, 1:3, 0]).then_inc(s_wT, 1)
            dve.sem_inc(s_kv, 1)
            with dve.Fori(0, NG // 2) as r:
                for u in range(2):
                    g = r * 2 + u
                    t = bass.ds(g * GT, GT)
                    dve.wait_ge(s_sq, g + 1)
                    dve.reduce_sum(length[:, t], sq[:, :, :], AX_X).then_inc(s_len, 1)
                    dve.wait_ge(s_gate, g + 2)
                    dve.tensor_copy(Kt[:, t, :], p_all[:, :, 0:P])
                    dve.tensor_copy(Vt[:, t, :], p_all[:, :, P:2 * P])
                    dve.tensor_copy(logit[:, 0, t], p_all[:, :, 3 * P])
                    dve.tensor_copy(logit[:, 1, t], p_all[:, :, 3 * P + 1]).then_inc(s_kv, 1)
            z = logit[:, 0, :]
            dve.wait_ge(s_kv, NG + 1)
            dve.scalar_tensor_tensor(out=tmp[:, 0, :], in0=z, scalar=-1.0, in1=z, op0=ALU.mult, op1=ALU.max).then_inc(s_fin, 1)
            dve.wait_ge(s_act, 2)
            dve.tensor_scalar(tmp[:, 2, :], tmp[:, 1, :], 1.0, None, ALU.add).then_inc(s_fin, 1)
            dve.wait_ge(s_act, 3)
            dve.scalar_tensor_tensor(out=cols["la"][:, :], in0=z, scalar=0.0, in1=tmp[:, 3, :], op0=ALU.min,
                                     op1=ALU.subtract).then_inc(s_fin, 1)
            dve.wait_ge(s_act, 4)
            dve.tensor_scalar(tmp[:, 5, :], tmp[:, 4, :], 1e-12, None, ALU.max).then_inc(s_fin, 1)
            dve.wait_ge(s_fin, 4)
            dve.reciprocal(cols["inv"][:, :], tmp[:, 5, :]).then_inc(s_fin, 1)
            dve.wait_ge(s_fin, 5)
            dve.tensor_tensor(cols["rate"][:, :], cols["inv"][:, :], cols["beta"][:, :], ALU.mult).then_inc(s_fin, 1)
            dve.tensor_tensor(Kt[:, :, :], Kt[:, :, :], spread(cols["inv"], P), ALU.mult).then_inc(s_fin, 1)
            dve.tensor_tensor(Vt[:, :, :], Vt[:, :, :], spread(cols["beta"], P), ALU.mult).then_inc(s_fin, 1)


def delta_invert(nc, name, C, Kt, cols, TT, WT, LT):
    with Stage(nc, name) as st:
        def pair(n):
            return [st.sb(f"{n}{v}", [P, B, P]) for v in range(2)]

        kn, kb, kT, kbT, mt, prod, xt = map(pair, ("kn", "kb", "kT", "kbT", "mt", "prod", "xt"))
        lad = prod
        x = kT
        bgk = kn
        inner = [st.sb(f"level{v}", [P, LEVELS - 2, B, P]) for v in range(2)]
        level = [[xt[v]] + [inner[v][:, n, :, :] for n in range(LEVELS - 2)] + [mt[v]] for v in range(2)]
        banks = [[st.ps(f"bank{v}{i}", [P, B, P]) for i in range(3)] for v in range(2)]
        s_in = [st.sem(f"in{v}") for v in range(2)]
        s_lev = [st.sem(f"lev{v}") for v in range(2)]
        s_pe = [st.sem(f"pe{v}") for v in range(2)]
        s_act = [st.sem(f"act{v}") for v in range(2)]
        s_dve = [st.sem(f"dve{v}") for v in range(2)]
        N_IN, N_LEV = 3, LEVELS + 2
        N_PE = 2 + 2 + 1 + 2 * (LEVELS - 1) + 1
        N_ACT = 2 + 1 + 1 + (LEVELS - 1) + 1
        N_DVE = 1 + 1 + (LEVELS - 1)
        block = st.block()

        def mask(n):
            return C[n][:, :].rearrange("p (o n) -> p o n", o=1).to_broadcast([P, B, P])

        @block.gpsimd
        def _(pool):
            for v in range(2):
                pool.sem_inc(s_in[v], N_IN)
                pool.sem_inc(s_lev[v], N_LEV)
            with pool.Fori(0, NCH // 2) as r:
                for v in range(2):
                    c = r * 2 + v
                    pool.wait_ge(s_pe[v], (r + 1) * N_PE)
                    pool.wait_ge(s_act[v], (r + 1) * N_ACT)
                    pool.tensor_copy(kn[v][:, :, :], chunk(Kt, c)).then_inc(s_in[v], 1)
                    pool.tensor_tensor(kb[v][:, :, :], chunk(Kt, c), scalars(cols["beta"], c), ALU.mult).then_inc(s_in[v], 1)
                    pool.tensor_tensor(lad[v][:, :, :], mask("after"), scalars(cols["la"], c), ALU.mult).then_inc(s_in[v], 1)
                for v in range(2):
                    c = r * 2 + v
                    pool.wait_ge(s_dve[v], (r + 1) * N_DVE + 1)
                    for n in range(LEVELS):
                        if n == LEVELS - 1:
                            pool.wait_ge(s_lev[v], (r + 1) * N_LEV + n)
                        pool.tensor_tensor(level[v][n][:, :, :], mt[v][:, :, :], mask(f"level{n}"), ALU.mult).then_inc(s_lev[v], 1)
                    pool.tensor_tensor(bgk[v][:, :, :], kb[v][:, :, :], scalars(cols["upto"], c), ALU.mult).then_inc(s_lev[v], 1)
                    pool.tensor_tensor(chunk(LT, c), chunk(LT, c), mask("upto"), ALU.mult).then_inc(s_lev[v], 1)

        @block.tensor
        def _(pe):
            for v in range(2):
                pe.sem_inc(s_pe[v], N_PE)
            with pe.Fori(0, NCH // 2) as r:
                p, a, d = (r + 1) * N_PE, (r + 1) * N_ACT, (r + 1) * N_DVE
                for v in range(2):
                    A, Bk, _ = banks[v]
                    pe.wait_ge(s_in[v], (r + 1) * N_IN + N_IN)
                    pe.wait_ge(s_act[v], a)
                    for b in range(B):
                        mm = pe.transpose(A[:, b, :], kn[v][:, b, :], C["ident"][:, :])
                    mm.then_inc(s_pe[v], 1)
                    for b in range(B):
                        mm = pe.transpose(Bk[:, b, :], kb[v][:, b, :], C["ident"][:, :])
                    mm.then_inc(s_pe[v], 1)
                for v in range(2):
                    A, Bk, _ = banks[v]
                    pe.wait_ge(s_act[v], a + 2)
                    for b in range(B):
                        mm = pe.matmul(A[:, b, :], kT[v][:, b, :], kbT[v][:, b, :], start=True, stop=True)
                    mm.then_inc(s_pe[v], 1)
                    for b in range(B):
                        mm = pe.matmul(Bk[:, b, :], lad[v][:, b, :], C["upto"][:, :], start=True, stop=True)
                    mm.then_inc(s_pe[v], 1)
                for v in range(2):
                    A = banks[v][0]
                    pe.wait_ge(s_dve[v], d + 2)
                    for b in range(B):
                        mm = pe.transpose(A[:, b, :], xt[v][:, b, :], C["ident"][:, :])
                    mm.then_inc(s_pe[v], 1)
                for n in range(1, LEVELS):
                    for v in range(2):
                        A = banks[v][0]
                        if n == 1:
                            pe.wait_ge(s_act[v], a + 4)
                            pe.wait_ge(s_lev[v], (r + 2) * N_LEV)
                        else:
                            pe.wait_ge(s_dve[v], d + 1 + n)
                        for b in range(B):
                            mm = pe.matmul(A[:, b, :], level[v][n][:, b, :], x[v][:, b, :], start=True, stop=True)
                        mm.then_inc(s_pe[v], 1)
                    for v in range(2):
                        _, Bk, Ck = banks[v]
                        pe.wait_ge(s_act[v], a + 4 + n)
                        for b in range(B):
                            if n < LEVELS - 1:
                                pe.matmul(Bk[:, b, :], xt[v][:, b, :], prod[v][:, b, :], start=True, stop=True)
                            mm = pe.matmul(Ck[:, b, :], prod[v][:, b, :], xt[v][:, b, :], start=True, stop=True)
                        mm.then_inc(s_pe[v], 1)
                for v in range(2):
                    A = banks[v][0]
                    pe.wait_ge(s_dve[v], d + N_DVE)
                    for b in range(B):
                        mm = pe.matmul(A[:, b, :], bgk[v][:, b, :], xt[v][:, b, :], start=True, stop=True)
                    mm.then_inc(s_pe[v], 1)

        @block.scalar
        def _(act):
            for v in range(2):
                act.sem_inc(s_act[v], N_ACT)
            with act.Fori(0, NCH // 2) as r:
                p, a, d = (r + 1) * N_PE, (r + 1) * N_ACT, (r + 1) * N_DVE
                for v in range(2):
                    A, Bk, _ = banks[v]
                    act.wait_ge(s_pe[v], p + 1)
                    act.copy(kT[v][:, :, :], A[:, :, :]).then_inc(s_act[v], 1)
                    act.wait_ge(s_pe[v], p + 2)
                    act.copy(kbT[v][:, :, :], Bk[:, :, :]).then_inc(s_act[v], 1)
                for v in range(2):
                    act.wait_ge(s_pe[v], p + 4)
                    act.activation(chunk(LT, r * 2 + v), banks[v][1][:, :, :], ACT.Exp).then_inc(s_act[v], 1)
                for v in range(2):
                    act.wait_ge(s_pe[v], p + 5)
                    act.copy(x[v][:, :, :], banks[v][0][:, :, :]).then_inc(s_act[v], 1)
                for n in range(1, LEVELS):
                    for v in range(2):
                        act.wait_ge(s_pe[v], p + 4 + 2 * n)
                        act.copy(prod[v][:, :, :], banks[v][0][:, :, :]).then_inc(s_act[v], 1)
                for v in range(2):
                    act.wait_ge(s_pe[v], p + N_PE)
                    act.mul(chunk(WT, r * 2 + v), banks[v][0][:, :, :], -1.0).then_inc(s_act[v], 1)

        @block.vector
        def _(dve):
            for v in range(2):
                dve.sem_inc(s_dve[v], N_DVE)
            with dve.Fori(0, NCH // 2) as r:
                p, a, d = (r + 1) * N_PE, (r + 1) * N_ACT, (r + 1) * N_DVE
                for v in range(2):
                    dve.wait_ge(s_act[v], a + 3)
                    dve.tensor_tensor(mt[v][:, :, :], banks[v][0][:, :, :], chunk(LT, r * 2 + v), ALU.mult).then_inc(s_dve[v], 1)
                for v in range(2):
                    dve.wait_ge(s_lev[v], (r + 1) * N_LEV + 1)
                    dve.tensor_tensor(xt[v][:, :, :], mask("ident"), level[v][0][:, :, :], ALU.subtract).then_inc(s_dve[v], 1)
                for n in range(1, LEVELS):
                    for v in range(2):
                        dve.wait_ge(s_pe[v], p + 5 + 2 * n)
                        if n < LEVELS - 1:
                            dve.tensor_tensor(x[v][:, :, :], x[v][:, :, :], banks[v][1][:, :, :], ALU.subtract)
                        else:
                            dve.tensor_tensor(chunk(TT, r * 2 + v), xt[v][:, :, :], banks[v][2][:, :, :], ALU.subtract)
                        dve.tensor_tensor(xt[v][:, :, :], xt[v][:, :, :], banks[v][2][:, :, :], ALU.subtract).then_inc(s_dve[v], 1)


def delta_scan(nc, name, C, Kt, Vt, Gt, qT, cols, TT, WT, LT):
    with Stage(nc, name) as st:
        def pair(n):
            return st.sb(n, [P, 2, B, P])

        tt, wt, qs, kn, bv, kd = map(pair, ("tt", "wt", "qs", "kn", "bv", "kd"))
        Ss = st.sb("S", [P, B, P])
        ST = st.sb("ST", [P, B, P])
        Sd = st.sb("Sd", [P, B, P])
        STd = st.sb("STd", [P, B, P])
        U = st.sb("U", [P, B, P])
        UT = st.sb("UT", [P, B, P])
        o1 = st.sb("o1", [P, B, P])
        o = st.sb("o", [P, B, P])
        pm = st.sb("pm", [P, B, P])
        p_u, p_ut, p_o1, p_s, p_st, p_p, p_o = (st.ps(n, [P, B, P]) for n in (
            "p_u", "p_ut", "p_o1", "p_s", "p_st", "p_p", "p_o"))
        s_load = [st.sem("load0"), st.sem("load1")]
        s_in = st.sem("in")
        s_dec = st.sem("dec")
        s_pe = st.sem("pe")
        s_u = st.sem("u")
        s_ut = st.sem("ut")
        s_dve = st.sem("dve")
        s_state = st.sem("state")
        s_og = st.sem("og")
        N_PE, N_DVE = 7, 3
        block = st.block()

        @block.sync
        def _(sp):
            with sp.Fori(0, NCH // 2) as r:
                for u in range(2):
                    c = r * 2 + u
                    sp.wait_ge(s_pe, c * N_PE + N_PE)
                    for dst, src in ((tt, TT), (wt, WT), (qs, qT), (kn, Kt), (bv, Vt)):
                        sp.dma_start(dst[:, u, :, :], chunk(src, c)).then_inc(s_load[u], 16)

        @block.gpsimd
        def _(pool):
            pool.sem_inc(s_og, 1)
            with pool.Fori(0, NCH // 2) as r:
                for u in range(2):
                    c = r * 2 + u
                    pool.wait_ge(s_pe, c * N_PE + N_PE)
                    pool.tensor_tensor(kd[:, u, :, :], chunk(Kt, c), scalars(cols["after"], c), ALU.mult).then_inc(s_in, 1)
                    pool.wait_ge(s_state, c * 2 + 2)
                    pool.tensor_tensor(STd[:, :, :], ST[:, :, :], scalars(cols["whole"], c), ALU.mult).then_inc(s_dec, 1)
                    pool.tensor_tensor(Sd[:, :, :], Ss[:, :, :], scalars(cols["whole"], c), ALU.mult).then_inc(s_dec, 1)
                    pool.wait_ge(s_dve, c * N_DVE + 2 * N_DVE)
                    pool.tensor_tensor(chunk(Gt, c), o[:, :, :], chunk(Gt, c), ALU.mult).then_inc(s_og, 1)

        @block.tensor
        def _(pe):
            pe.sem_inc(s_pe, 2 * N_PE)
            with pe.Fori(0, NCH // 2) as r:
                for u in range(2):
                    c = r * 2 + u
                    pe.wait_ge(s_load[u], 80 * (r + 1))
                    pe.wait_ge(s_state, c * 2 + 2)
                    for b in range(B):
                        pe.matmul(p_u[:, b, :], tt[:, u, b, :], bv[:, u, b, :], start=True, stop=False)
                        mm = pe.matmul(p_u[:, b, :], wt[:, u, b, :], ST[:, b, :], start=False, stop=True)
                    mm.then_inc(s_pe, 1)
                    for b in range(B):
                        pe.matmul(p_ut[:, b, :], bv[:, u, b, :], tt[:, u, b, :], start=True, stop=False)
                        mm = pe.matmul(p_ut[:, b, :], ST[:, b, :], wt[:, u, b, :], start=False, stop=True)
                    mm.then_inc(s_pe, 1)
                    for b in range(B):
                        mm = pe.matmul(p_o1[:, b, :], qs[:, u, b, :], Ss[:, b, :], start=True, stop=True)
                    mm.then_inc(s_pe, 1)
                    pe.wait_ge(s_u, c + 1)
                    pe.wait_ge(s_in, c + 1)
                    for b in range(B):
                        mm = pe.matmul(p_st[:, b, :], kd[:, u, b, :], U[:, b, :], start=True, stop=True)
                    mm.then_inc(s_pe, 1)
                    for b in range(B):
                        mm = pe.matmul(p_s[:, b, :], U[:, b, :], kd[:, u, b, :], start=True, stop=True)
                    mm.then_inc(s_pe, 1)
                    pe.wait_ge(s_ut, c + 1)
                    for b in range(B):
                        mm = pe.matmul(p_p[:, b, :], UT[:, b, :], qs[:, u, b, :], start=True, stop=True)
                    mm.then_inc(s_pe, 1)
                    pe.wait_ge(s_dve, c * N_DVE + (2 + N_DVE))
                    for b in range(B):
                        mm = pe.matmul(p_o[:, b, :], pm[:, b, :], kn[:, u, b, :], start=True, stop=True)
                    mm.then_inc(s_pe, 1)

        @block.scalar
        def _(act):
            with act.Fori(0, NCH // 2) as r:
                for u in range(2):
                    c = r * 2 + u
                    act.wait_ge(s_pe, c * N_PE + (1 + 2 * N_PE))
                    act.copy(U[:, :, :], p_u[:, :, :]).then_inc(s_u, 1)
                    act.wait_ge(s_pe, c * N_PE + (2 + 2 * N_PE))
                    act.copy(UT[:, :, :], p_ut[:, :, :]).then_inc(s_ut, 1)

        @block.vector
        def _(dve):
            dve.sem_inc(s_dve, N_DVE)
            dve.memset(Ss[:, :, :], 0.0).then_inc(s_state, 1)
            dve.memset(ST[:, :, :], 0.0).then_inc(s_state, 1)
            with dve.Fori(0, NCH // 2) as r:
                for u in range(2):
                    c = r * 2 + u
                    dve.wait_ge(s_pe, c * N_PE + (3 + 2 * N_PE))
                    dve.wait_ge(s_dve, c * N_DVE + N_DVE)
                    dve.tensor_tensor(o1[:, :, :], p_o1[:, :, :], scalars(cols["upto"], c), ALU.mult).then_inc(s_dve, 1)
                    dve.wait_ge(s_pe, c * N_PE + (4 + 2 * N_PE))
                    dve.wait_ge(s_dec, c * 2 + 2)
                    dve.tensor_tensor(ST[:, :, :], p_st[:, :, :], STd[:, :, :], ALU.add).then_inc(s_state, 1)
                    dve.wait_ge(s_pe, c * N_PE + (5 + 2 * N_PE))
                    dve.tensor_tensor(Ss[:, :, :], p_s[:, :, :], Sd[:, :, :], ALU.add).then_inc(s_state, 1)
                    dve.wait_ge(s_pe, c * N_PE + (6 + 2 * N_PE))
                    dve.tensor_tensor(pm[:, :, :], p_p[:, :, :], chunk(LT, c), ALU.mult).then_inc(s_dve, 1)
                    dve.wait_ge(s_pe, c * N_PE + 3 * N_PE)
                    dve.wait_ge(s_og, c + 1)
                    dve.wait_ge(s_dve, c * N_DVE + (1 + N_DVE))
                    dve.tensor_tensor(o[:, :, :], p_o[:, :, :], o1[:, :, :], ALU.add).then_inc(s_dve, 1)


def delta_out(nc, name, X, Gt, C, W, wo):
    with Stage(nc, name) as st:
        bo = st.sb("bo", [1, P])
        gT = st.sb("gT", [P, 2, GT, P])
        turned = st.ps("turned", [P, 2, GT, P])
        y = st.ps("y", [P, 2, GT, P])
        s_w = st.sem("w")
        s_turn = st.sem("turn")
        s_gT = st.sem("gT")
        s_y = st.sem("y")
        s_res = st.sem("res")
        block = st.block()

        @block.sync
        def _(sp):
            sp.dma_start(bo[:, :], W['bo'].rearrange("(o n) -> o n", o=1)).then_inc(s_w, 16)

        @block.tensor
        def _(pe):
            for g in range(NG + 1):
                if g < NG:
                    if g >= 2:
                        pe.wait_ge(s_gT, g - 1)
                    for i in range(GT):
                        mm = pe.transpose(turned[:, g % 2, i, :], Gt[:, g * GT + i, :], C["ident"][:, :])
                    mm.then_inc(s_turn, 1)
                if g >= 1:
                    h = g - 1
                    if h == 0:
                        pe.wait_ge(s_w, 16)
                    pe.wait_ge(s_gT, h + 1)
                    if h >= 2:
                        pe.wait_ge(s_res, h - 1)
                    for i in range(GT):
                        pe.matmul(y[:, h % 2, i, :], C["ones"][0:1, :], bo[:, :], start=True, stop=False)
                        mm = pe.matmul(y[:, h % 2, i, :], gT[:, h % 2, i, :], wo[:, :], start=False, stop=True)
                    mm.then_inc(s_y, 1)

        @block.scalar
        def _(act):
            for g in range(NG):
                act.wait_ge(s_turn, g + 1)
                if g >= 2:
                    act.wait_ge(s_y, g - 1)
                act.copy(gT[:, g % 2, :, :], turned[:, g % 2, :, :]).then_inc(s_gT, 1)

        @block.vector
        def _(dve):
            for g in range(NG):
                dve.wait_ge(s_y, g + 1)
                xt = X[:, g * GT:(g + 1) * GT, :]
                dve.tensor_tensor(xt, y[:, g % 2, :, :], xt, ALU.add).then_inc(s_res, 1)


def delta_rule(nc, name, X, XnT, C, W):
    with ExitStack() as ctx:
        def sb(n, shape):
            return ctx.enter_context(nc.sbuf_tensor(f"{name}_{n}", shape, F32))

        cols = {n: sb(n, [P, NT]) for n in ("la", "beta", "inv", "rate", "upto", "after", "whole")}
        wo = sb("wo", [P, P])
        Kt, Vt, Gt = (sb(n, [P, NT, P]) for n in ("K", "V", "G"))
        qT = sb("qT", [P, TOK])
        delta_project(nc, f"{name}p", XnT, C, W, Kt, Vt, Gt, qT, wo, cols)
        WT, LT = (sb(n, [P, NT, P]) for n in ("WT", "LT"))
        TT = XnT
        delta_invert(nc, f"{name}i", C, Kt, cols, TT, WT, LT)
        delta_scan(nc, f"{name}r", C, Kt, Vt, Gt, qT, cols, TT, WT, LT)
        delta_out(nc, f"{name}o", X, Gt, C, W, wo)


INPUTS = ['L0_attn_a_x', 'L0_attn_a_W_DQ', 'L0_attn_a_W_UQ', 'L0_attn_a_W_QR', 'L0_attn_a_W_DKV',
          'L0_attn_a_W_UK', 'L0_attn_a_W_UV', 'L0_attn_a_W_KR', 'L0_attn_a_W_O',
          'L0_attn_b_Wc_down', 'L0_attn_b_Wq_up', 'L0_attn_b_Wkv_up', 'L0_attn_b_Wc_proj',
          'L0_ffn_w_gate', 'L0_ffn_w_up', 'L0_ffn_w_down',
          'L1_attn_a_Wl', 'L1_attn_a_bl', 'L1_attn_a_Wb', 'L1_attn_a_Wc', 'L1_attn_a_Dp',
          'L1_attn_b_Wq', 'L1_attn_b_bq', 'L1_attn_b_Wk', 'L1_attn_b_bk', 'L1_attn_b_Wv', 'L1_attn_b_bv',
          'L1_attn_b_Wa', 'L1_attn_b_ba', 'L1_attn_b_Wb', 'L1_attn_b_bb', 'L1_attn_b_Wg', 'L1_attn_b_bg',
          'L1_attn_b_Wo', 'L1_attn_b_bo',
          'L1_ffn_scale', 'L1_ffn_gate_w', 'L1_ffn_gate_b', 'L1_ffn_mlp1_w', 'L1_ffn_mlp1_b',
          'L1_ffn_mlp2_w', 'L1_ffn_mlp2_b']


def constants():
    p = np.arange(P)
    keys, queries = p[:, None], p[None, :]
    hi = np.float32(np.exp(CLIP * (DH + DR) ** -0.5))
    pos = np.arange(S, dtype=np.float32)[None, :]
    freq = np.float32(10000.0) ** (-np.arange(0, DR, 2, dtype=np.float32) / DR)
    n = np.arange(H * DR + DR)
    angle = (pos * freq[(n % DR) // 2][:, None]).astype(np.float32)
    return {
        "ident": np.eye(P, dtype=np.float32),
        "neg_kq": np.where(keys > queries, NEG, 0).astype(np.float32),
        "neg_qk": np.where(queries > keys, NEG, 0).astype(np.float32),
        "ones": np.ones((P, P), np.float32),
        "upto": (keys <= queries).astype(np.float32),
        "after": (keys > queries).astype(np.float32),
        **{f"level{n}": ((keys >> (n + 1) == queries >> (n + 1)) & (queries >> n & 1 == 1) & (keys >> n & 1 == 0))
           .astype(np.float32) for n in range(LEVELS)},
        "pick_row": (np.arange(96)[:, None] % ROUTE_AT == np.arange(E)[None, :]).astype(np.float32),
        "top_kq": np.where(keys > queries, 0, hi).astype(np.float32),
        "pick_sum": (keys == 32 * (queries // 32) + DH).astype(np.float32),
        "cos": np.cos(angle),
        "sin": np.sin(angle) * np.where(n % 2, 1, -1).astype(np.float32)[:, None],
    }


STAGES = "afbfsmdm"


def build(nc, I, consts, out):
    with ExitStack() as ctx:
        X = ctx.enter_context(nc.sbuf_tensor("X", [P, NT, D], F32))
        C = {n: ctx.enter_context(nc.sbuf_tensor(f"c_{n}", list(a.shape), F32)) for n, a in consts.items()
             if n not in ("cos", "sin")}
        XnT = ctx.enter_context(nc.sbuf_tensor("XnT", [P, TOK], F32))
        for n in ("ident", "neg_kq", "neg_qk"):
            C[f"{n}_b"] = ctx.enter_context(nc.sbuf_tensor(f"c_{n}_b", [P, P], BF16))
        load_x(nc, I['L0_attn_a_x'], consts, X, C)
        X_ = None
        for n, s in enumerate(STAGES):
            if s == "a":
                W = {n: I[f'L0_attn_a_{n}'] for n in ('W_DQ', 'W_UQ', 'W_QR', 'W_DKV', 'W_UK', 'W_UV', 'W_KR', 'W_O')}
                norm_stage(nc, f"norm{n}", X, XnT, C)
                W["cos"], W["sin"] = consts["cos"], consts["sin"]
                attention_a(nc, f"attn{n}", X, XnT, C, W)
            if s == "b":
                W = {n: I[f'L0_attn_b_{n}'] for n in ('Wc_down', 'Wq_up', 'Wkv_up', 'Wc_proj')}
                norm_stage(nc, f"norm{n}", X, XnT, C)
                attention_b(nc, f"attn{n}", X, XnT, C, W)
            if s == "s":
                W = {n: I[f'L1_attn_a_{n}'] for n in ('Wl', 'bl', 'Wb', 'Wc', 'Dp')}
                norm_stage(nc, f"norm{n}", X, XnT, C)
                recurrence(nc, f"scan{n}", X, XnT, C, W)
            if s == "m":
                W = {n: I[f'L1_ffn_{n}'] for n in ('scale', 'gate_w', 'gate_b', 'mlp1_w', 'mlp1_b', 'mlp2_w', 'mlp2_b')}
                if X_ is None:
                    X_ = Experts(nc, ctx)
                    load_experts(nc, "experts", C, W, X_)
                norm_stage(nc, f"norm{n}", X, XnT, C, W['scale'])
                with nc.sbuf_tensor(f"routeT{n}", [E, TOK], F32) as routeT, \
                        nc.sbuf_tensor(f"routes{n}", [96, TOK], BF16) as routes_b:
                    route(nc, f"route{n}", XnT, C, X_, routeT, routes_b)
                    experts(nc, f"moe{n}", X, XnT, C, X_, routeT, routes_b)
            if s == "d":
                W = {n: I[f'L1_attn_b_{n}'] for n in ('Wq', 'bq', 'Wk', 'bk', 'Wv', 'bv', 'Wa', 'ba', 'Wb', 'bb',
                                                      'Wg', 'bg', 'Wo', 'bo')}
                norm_stage(nc, f"norm{n}", X, XnT, C)
                delta_rule(nc, f"delta{n}", X, XnT, C, W)
            if s == "f":
                norm_stage(nc, f"norm{n}", X, XnT, C)
                gated_mlp(nc, f"mlp{n}", X, XnT, C, I['L0_ffn_w_gate'], I['L0_ffn_w_up'], I['L0_ffn_w_down'])
        store_x(nc, X, out)


def kernel(**inputs):
    import concourse.bacc as _bacc
    from concourse.bass_utils import run_bass_kernel_spmd as _run

    nc = _bacc.Bacc("TRN2", target_bir_lowering=False, num_devices=1)
    arrays, args, tables = {}, {}, {}
    for name in INPUTS:
        a = np.ascontiguousarray(inputs[name])
        arrays[f"in_{name}_dram"] = a
        args[name] = nc.dram_tensor(f"in_{name}_dram", a.shape, mybir.dt.from_np(a.dtype), kind="ExternalInput").ap()
    for name, a in constants().items():
        arrays[f"const_{name}_dram"] = a
        tables[name] = nc.dram_tensor(f"const_{name}_dram", a.shape, mybir.dt.from_np(a.dtype), kind="ExternalInput").ap()
    out = nc.dram_tensor("out_0_dram", (B, S, D), F32, kind="ExternalOutput").ap()
    build(nc, args, tables, out)
    r = _run(nc, [arrays], core_ids=[0])
    return r.results[0]["out_0_dram"]
```

```python
from contextlib import ExitStack

import numpy as np

import concourse.bass as bass
from concourse import mybir

F32 = mybir.dt.float32
BF16 = mybir.dt.bfloat16
I32 = mybir.dt.int32
ALU = mybir.AluOpType
ACT = mybir.ActivationFunctionType
AX_X = mybir.AxisListType.X

P = 128
B, S, D = 4, 1024, 128
TOK = B * S
NT = TOK // P
TB = S // P
GW = 512
NG = TOK // GW
GT = GW // P
H, DH, DR = 16, 8, 4
HG = H // 4
LAT_A, LAT_B = 32, 64
HID = 384
HC = HID // P
NS = 32
E, TOPK = 16, 4
LN_EPS = 1e-5
NEG = -1.0e30
LOWEST = -3.0e38
CLIP = 80.0
PARTS = 3
PAIRS = PARTS * PARTS
QC = PAIRS * DH
QR = PAIRS * DR


class Stage:

    def __init__(self, nc, name):
        self.nc, self.name, self.ctx, self.sems = nc, name, ExitStack(), []

    def __enter__(self):
        self.ctx.__enter__()
        return self

    def __exit__(self, *a):
        self.ctx.__exit__(*a)
        self.nc.clear_and_free_semaphores(self.sems)
        self.nc.all_engine_barrier()

    def sb(self, name, shape, dt=F32):
        return self.ctx.enter_context(self.nc.sbuf_tensor(f"{self.name}_{name}", shape, dt))

    def ps(self, name, shape, dt=F32):
        return self.ctx.enter_context(self.nc.psum_tensor(f"{self.name}_{name}", shape, dt))

    def sem(self, name):
        self.sems.append(self.nc.alloc_semaphore(f"{self.name}_{name}"))
        return self.sems[-1]

    def block(self):
        return self.ctx.enter_context(self.nc.Block())


def spread(ap, n):
    return ap.rearrange("p (a o) -> p a o", o=1).to_broadcast([ap.shape[0], ap.shape[1], n])


def load_x(nc, x_in, consts, X, C):
    tables = [n for n in consts if n in C]
    with Stage(nc, "load") as st:
        done = st.sem("done")
        cast = st.sem("cast")
        block = st.block()

        @block.sync
        def _(sp):
            sp.dma_start(X[:, :, :], x_in.rearrange("b (t p) d -> p (b t) d", p=P)).then_inc(done, 16)
            for name in tables:
                sp.dma_start(C[name][:, :], consts[name]).then_inc(done, 16)

        @block.vector
        def _(dve):
            dve.wait_ge(done, 16 * (1 + len(tables)))
            for name in ("ident", "neg_kq", "neg_qk"):
                dve.tensor_copy(C[f"{name}_b"][:, :], C[name][:, :]).then_inc(cast, 1)


def norm_stage(nc, name, X, XnT, C, gain=None):
    rms = gain is not None
    with Stage(nc, name) as st:
        xc = st.sb("xc", [P, NT, D])
        xn = st.sb("xn", [P, NT, D])
        xr = st.sb("xr", [P, NT, D]) if rms else xn
        sq = st.sb("sq", [P, 2, TB, D])
        total = st.sb("total", [P, NT])
        mean = st.sb("mean", [P, NT])
        squares = st.sb("squares", [P, NT])
        var = st.sb("var", [P, 2, NT])
        dev = st.sb("dev", [P, 2, NT])
        rstd = st.sb("rstd", [P, 2, NT])
        power = st.sb("power", [P, 2, NT])
        turned = st.ps("turned", [P, 2, 2, GW])
        gcol = st.sb("gcol", [P, 1])
        s_gain = st.sem("gain")
        s_sum = st.sem("sum")
        s_mean = st.sem("mean")
        s_cent = st.sem("cent")
        s_sq = st.sem("sq")
        s_ss = st.sem("ss")
        s_var = st.sem("var")
        s_dev = st.sem("dev")
        s_rstd = st.sem("rstd")
        s_pow = st.sem("pow")
        s_xn = st.sem("xn")
        s_xr = st.sem("xr")
        s_res = st.sem("res")
        s_turn = st.sem("turn")
        s_out = st.sem("out")
        tiles = [slice(TB * b, TB * b + TB) for b in range(B)]
        block = st.block()

        @block.sync
        def _(sp):
            if rms:
                sp.dma_start(gcol[:, :], gain.rearrange("(p o) -> p o", o=1)).then_inc(s_gain, 16)

        @block.gpsimd
        def _(pool):
            if rms:
                for b, t in enumerate(tiles):
                    pool.wait_ge(s_xn, b + 1)
                    pool.tensor_tensor(X[:, t, :], X[:, t, :], xn[:, t, :], ALU.add).then_inc(s_res, 1)

        @block.vector
        def _(dve):
            for b, t in enumerate(tiles):
                dve.reduce_sum(total[:, t], X[:, t, :], AX_X).then_inc(s_sum, 1)
                dve.wait_ge(s_sum, b + 1)
                dve.tensor_scalar(mean[:, t], total[:, t], 1.0 / D, None, ALU.mult).then_inc(s_mean, 1)
                dve.wait_ge(s_mean, b + 1)
                dve.tensor_tensor(xc[:, t, :], X[:, t, :], spread(mean[:, t], D), ALU.subtract).then_inc(s_cent, 1)
            for b, t in enumerate(tiles):
                dve.wait_ge(s_sq, b + 1)
                dve.reduce_sum(squares[:, t], sq[:, b % 2, :, :], AX_X).then_inc(s_ss, 1)
                dve.wait_ge(s_ss, b + 1)
                dve.tensor_scalar(var[:, 0, t], squares[:, t], 1.0 / D, LN_EPS, ALU.mult, ALU.add).then_inc(s_var, 1)
            for b, t in enumerate(tiles):
                dve.wait_ge(s_dev, b + 1)
                dve.reciprocal(rstd[:, 0, t], dev[:, 0, t]).then_inc(s_rstd, 1)
                dve.wait_ge(s_rstd, b + 1)
                dve.tensor_tensor(xn[:, t, :], xc[:, t, :], spread(rstd[:, 0, t], D), ALU.mult).then_inc(s_xn, 1)
            if rms:
                dve.tensor_tensor(power[:, 0, :], squares[:, :], rstd[:, 0, :], ALU.mult).then_inc(s_pow, 1)
                dve.wait_ge(s_pow, 1)
                dve.tensor_tensor(power[:, 1, :], power[:, 0, :], rstd[:, 0, :], ALU.mult).then_inc(s_pow, 1)
                dve.wait_ge(s_pow, 2)
                dve.tensor_scalar(var[:, 1, :], power[:, 1, :], 1.0 / D, LN_EPS, ALU.mult, ALU.add).then_inc(s_var, 1)
                dve.wait_ge(s_dev, B + 1)
                dve.reciprocal(rstd[:, 1, :], dev[:, 1, :]).then_inc(s_rstd, 1)
                dve.wait_ge(s_rstd, B + 1)
                for b, t in enumerate(tiles):
                    dve.tensor_tensor(xr[:, t, :], xn[:, t, :], spread(rstd[:, 1, t], D), ALU.mult).then_inc(s_xr, 1)

        @block.scalar
        def _(act):
            for b, t in enumerate(tiles):
                act.wait_ge(s_cent, b + 1)
                if b >= 2:
                    act.wait_ge(s_ss, b - 1)
                act.activation(sq[:, b % 2, :, :], xc[:, t, :], ACT.Square).then_inc(s_sq, 1)
            for b, t in enumerate(tiles):
                act.wait_ge(s_var, b + 1)
                act.activation(dev[:, 0, t], var[:, 0, t], ACT.Sqrt).then_inc(s_dev, 1)
            if rms:
                act.wait_ge(s_var, B + 1)
                act.activation(dev[:, 1, :], var[:, 1, :], ACT.Sqrt).then_inc(s_dev, 1)
                act.wait_ge(s_gain, 16)
            for b in range(B):
                act.wait_ge(s_turn, b + 1)
                out, in_ = XnT[:, b * S:(b + 1) * S], turned[:, b % 2, :, :]
                if rms:
                    act.mul(out, in_, gcol[:, 0:1]).then_inc(s_out, 1)
                else:
                    act.copy(out, in_).then_inc(s_out, 1)

        @block.tensor
        def _(pe):
            for b in range(B):
                pe.wait_ge(s_xr if rms else s_xn, b + 1)
                if b >= 2:
                    pe.wait_ge(s_out, b - 1)
                for i in range(TB):
                    mm = pe.transpose(turned[:, b % 2, i // GT, (i % GT) * P:(i % GT + 1) * P],
                                      xr[:, TB * b + i, :], C["ident"][:, :])
                mm.then_inc(s_turn, 1)


def store_x(nc, X, out):
    with Stage(nc, "store") as st:
        done = st.sem("done")
        block = st.block()

        @block.sync
        def _(sp):
            sp.dma_start(out.rearrange("b (t p) d -> p (b t) d", p=P), X[:, :, :]).then_inc(done, 16)
            sp.wait_ge(done, 16)


def gated_mlp(nc, name, X, XnT, C, w_gate, w_up, w_down):
    scale = float(np.float32(1.0 / 127.0))
    with Stage(nc, name) as st:
        raw = st.sb("raw", [P, 3, HC, P], I32)
        wide = st.sb("wide", [P, 3, HC, P])
        wgT = st.sb("wgT", [P, HC, P])
        wuT = st.sb("wuT", [P, HC, P])
        wdT = st.sb("wdT", [P, HC, P])
        act_g = st.sb("act_g", [P, 2, GW])
        hidden = st.sb("hidden", [P, 2, HC, GW])
        gate = st.ps("gate", [P, 2, GW])
        up = st.ps("up", [P, 2, GW])
        down = st.ps("down", [P, 2, GT, P])
        s_w = st.sem("w")
        s_wide = st.sem("wide")
        s_turn = st.sem("turn")
        s_wT = st.sem("wT")
        s_gu = st.sem("gate_up")
        s_silu = st.sem("silu")
        s_hid = st.sem("hid")
        s_down = st.sem("down")
        s_res = st.sem("res")
        weights = ((wgT, gate), (wuT, up), (wdT, down))
        block = st.block()

        @block.sync
        def _(sp):
            sp.dma_start(raw[:, 0, :, :], w_gate.rearrange("(c p) d -> p c d", p=P)).then_inc(s_w, 16)
            sp.dma_start(raw[:, 1, :, :], w_up.rearrange("(c p) d -> p c d", p=P)).then_inc(s_w, 16)
            sp.dma_start(raw[:, 2, :, :], w_down.rearrange("p (c h) -> p c h", c=HC)).then_inc(s_w, 16)

        @block.tensor
        def _(pe):
            for k, (_, bank) in enumerate(weights):
                pe.wait_ge(s_wide, k + 1)
                for c in range(HC):
                    dst = bank[:, 0, c, :] if k == 2 else bank[:, 0, c * P:(c + 1) * P]
                    mm = pe.transpose(dst, wide[:, k, c, :], C["ident"][:, :])
                mm.then_inc(s_turn, 1)
            pe.wait_ge(s_wT, 3)
            with pe.Fori(0, NG // 2) as r:
                for u in range(2):
                    g = r * 2 + u
                    for c in range(HC):
                        k = g * HC + c
                        pe.wait_ge(s_hid, k + 1)
                        b = (u * HC + c) % 2
                        xg = XnT[:, bass.ds(g * GW, GW)]
                        pe.matmul(gate[:, b, :], wgT[:, c, :], xg, start=True, stop=True)
                        pe.matmul(up[:, b, :], wuT[:, c, :], xg, start=True, stop=True).then_inc(s_gu, 1)
                    pe.wait_ge(s_hid, g * HC + HC + 2)
                    pe.wait_ge(s_res, g + 1)
                    for i in range(GT):
                        for c in range(HC):
                            mm = pe.matmul(down[:, u, i, :], hidden[:, u, c, i * P:(i + 1) * P],
                                           wdT[:, c, :], start=(c == 0), stop=(c == HC - 1))
                    mm.then_inc(s_down, 1)

        @block.scalar
        def _(act):
            with act.Fori(0, NG // 2) as r:
                for u in range(2):
                    for c in range(HC):
                        k = r * (2 * HC) + (u * HC + c)
                        b = (u * HC + c) % 2
                        act.wait_ge(s_gu, k + 1)
                        act.wait_ge(s_hid, k + 1)
                        act.activation(act_g[:, b, :], gate[:, b, :], ACT.Silu).then_inc(s_silu, 1)

        @block.vector
        def _(dve):
            dve.wait_ge(s_w, 48)
            for k in range(3):
                dve.tensor_scalar(wide[:, k, :, :], raw[:, k, :, :], scale, None, ALU.mult).then_inc(s_wide, 1)
            for k, (wT, bank) in enumerate(weights):
                dve.wait_ge(s_turn, k + 1)
                src = bank[:, 0, 0:HC, :] if k == 2 else bank[:, 0, 0:HC * P].rearrange("p (c n) -> p c n", c=HC)
                dve.tensor_copy(wT[:, :, :], src).then_inc(s_wT, 1)
            dve.sem_inc(s_hid, 2)
            dve.sem_inc(s_res, 2)
            with dve.Fori(0, NG // 2) as r:
                for u in range(2):
                    g = r * 2 + u
                    for c in range(HC):
                        k = g * HC + c
                        b = (u * HC + c) % 2
                        dve.wait_ge(s_silu, k + 1)
                        dve.tensor_tensor(hidden[:, u, c, :], act_g[:, b, :], up[:, b, :], ALU.mult).then_inc(s_hid, 1)
                    dve.wait_ge(s_down, g + 1)
                    xt = X[:, bass.ds(g * GT, GT), :]
                    dve.tensor_tensor(xt, down[:, u, :, :], xt, ALU.add).then_inc(s_res, 1)


SEGMENTS = [[(0, 0, 1024)], [(1, 0, 896), (7, 896, 128)], [(2, 0, 768), (6, 768, 256)],
            [(3, 0, 640), (5, 640, 384)], [(4, 0, 512)]]
NSEG = len(SEGMENTS)
ITS = B * HG


def width(k):
    return sum(w for _, _, w in SEGMENTS[k])


class Scratch:

    def __init__(self, nc, name, rotary):
        def dram(n, shape, dt=BF16):
            return nc.dram_tensor(f"{name}_{n}", shape, dt, kind="Internal").ap()

        self.qc = dram("qc", (ITS, PARTS, 4 * DH, S))
        self.kc = dram("kc", (ITS, PARTS, 4 * DH if rotary else DH, S))
        self.sums = dram("sums", (4, ITS, S), F32)
        if rotary:
            self.qr = dram("qr", (ITS, PARTS, 4 * DR, S))
            self.kr = dram("kr", (ITS, PARTS, DR, S))
        else:
            self.mx = dram("mx", (PARTS, ITS, 4, S))


def project_a(nc, name, XnT, C, W, scratch, V):
    with Stage(nc, name) as st:
        wd = st.sb("wd", [P, 2, LAT_A])
        wq = st.sb("wq", [LAT_A, P])
        wk = st.sb("wk", [LAT_A, P])
        wv = st.sb("wv", [LAT_A, P])
        wqr = st.sb("wqr", [LAT_A, 2, H * DR])
        wkr = st.sb("wkr", [P, 2, DR])
        xs = st.sb("xs", [P, 2, GW])
        lat = st.sb("lat", [LAT_A, 2, 2, GW])
        NR = H * DR + DR
        cos = st.sb("cos", [NR, S])
        sin = st.sb("sin", [NR, S])
        turn_c = st.sb("turn_c", [NR, GW])
        turn_s = st.sb("turn_s", [NR, GW])
        turned = st.sb("turned", [NR, GW])
        rest = st.sb("rest", [P, 3, GW])
        parts = st.sb("parts", [P, 2, 3, PARTS, GW], BF16)
        p_lat = st.ps("p_lat", [LAT_A, 2, GW])
        p_rot = st.ps("p_rot", [NR, 2, GW])
        p_qk = st.ps("p_qk", [P, 2, GW])
        p_v = st.ps("p_v", [P, GT, P])
        s_w = st.sem("w")
        s_swap = st.sem("swap")
        s_xs = st.sem("xs")
        s_lat = st.sem("lat")
        s_lats = st.sem("lats")
        s_rot = st.sem("rot")
        s_q = st.sem("q")
        s_k = st.sem("k")
        s_v = st.sem("v")
        s_vout = st.sem("vout")
        s_trig = st.sem("trig")
        s_turned = st.sem("turned")
        s_p1 = st.sem("part1")
        s_rest = st.sem("rest")
        s_p2 = st.sem("part2")
        s_p3 = st.sem("part3")
        s_out = [st.sem("out0"), st.sem("out1")]
        NOUT = 4 * HG
        rows = (P, P, NR)
        block = st.block()

        @block.sync
        def _(sp):
            for dst, src in ((wd[:, 0, :], W['W_DQ']), (wd[:, 1, :], W['W_DKV']), (wq[:, :], W['W_UQ']),
                             (wk[:, :], W['W_UK']), (wv[:, :], W['W_UV']), (wqr[:, 0, :], W['W_QR']),
                             (wkr[:, 0, :], W['W_KR']), (cos[:, :], W['cos']), (sin[:, :], W['sin'])):
                sp.dma_start(dst, src).then_inc(s_w, 16)
            sp.sem_inc(s_out[0], 16 * NOUT)
            sp.sem_inc(s_out[1], 16 * NOUT)
            with sp.Fori(0, NG // 2) as r:
                for u in range(2):
                    g = r * 2 + u
                    cols = slice(u * GW, (u + 1) * GW)
                    sp.wait_ge(s_p3, g * 3 + 6)
                    for hg in range(HG):
                        for w, dram, a, n in ((0, scratch.qc, 4 * DH * hg, 4 * DH), (1, scratch.kc, 4 * DH * hg, 4 * DH),
                                              (2, scratch.qr, 4 * DR * hg, 4 * DR), (2, scratch.kr, H * DR, DR)):
                            dst = dram[bass.ds(r * HG + hg, 1), :, :, cols].squeeze(0).rearrange("i e t -> e i t")
                            sp.dma_start(dst, parts[a:a + n, u, w, :, :]).then_inc(s_out[u], 16)
            for u in range(2):
                sp.wait_ge(s_out[u], 16 * NOUT * (NG // 2 + 1))

        @block.gpsimd
        def _(pool):
            pool.wait_ge(s_w, 9 * 16)
            for w in (wqr, wkr):
                pair = w[:, :, :].rearrange("p s (n e) -> p s n e", e=2)
                pool.tensor_copy(pair[:, 1, :, 0], pair[:, 0, :, 1]).then_inc(s_swap, 1)
                pool.tensor_copy(pair[:, 1, :, 1], pair[:, 0, :, 0]).then_inc(s_swap, 1)
            pool.sem_inc(s_p3, 3)
            with pool.Fori(0, NG // 2) as r:
                for u in range(2):
                    g = r * 2 + u
                    pool.wait_ge(s_v, g + 1)
                    pool.tensor_copy(xs[:, u, :], XnT[:, bass.ds(g * GW, GW)]).then_inc(s_xs, 1)
                    pool.wait_ge(s_trig, g * 2 + 2)
                    pool.wait_ge(s_rest, g * 3 + 3)
                    pool.tensor_tensor(turned[:, :], turn_c[:, :], turn_s[:, :], ALU.add).then_inc(s_turned, 1)
                    for w in range(3):
                        n = rows[w]
                        pool.wait_ge(s_p2, g * 3 + w + 1)
                        pool.tensor_tensor(parts[0:n, u, w, 2, :], rest[0:n, w, :], parts[0:n, u, w, 1, :],
                                           ALU.subtract).then_inc(s_p3, 1)

        @block.tensor
        def _(pe):
            pe.wait_ge(s_swap, 4)
            pe.sem_inc(s_v, 2)
            with pe.Fori(0, NG // 2) as r:
                for u in range(2):
                    g = r * 2 + u
                    pe.wait_ge(s_xs, g + 1)
                    pe.wait_ge(s_lats, g + 1)
                    for k in range(2):
                        mm = pe.matmul(p_lat[:, k, :], wd[:, k, :], xs[:, u, :], start=True, stop=True)
                    mm.then_inc(s_lat, 1)
                    pe.wait_ge(s_lats, g + 2)
                    pe.wait_ge(s_turned, g + 1)
                    for k in range(2):
                        pe.matmul(p_rot[0:H * DR, k, :], wqr[:, k, :], lat[:, u, 0, :], start=True, stop=True)
                        mm = pe.matmul(p_rot[H * DR:NR, k, :], wkr[:, k, :], xs[:, u, :], start=True, stop=True)
                    mm.then_inc(s_rot, 1)
                    pe.wait_ge(s_rest, g * 3 + 3)
                    pe.matmul(p_qk[:, 0, :], wq[:, :], lat[:, u, 0, :], start=True, stop=True).then_inc(s_q, 1)
                    pe.matmul(p_qk[:, 1, :], wk[:, :], lat[:, u, 1, :], start=True, stop=True).then_inc(s_k, 1)
                    pe.wait_ge(s_vout, g + 1)
                    for i in range(GT):
                        mm = pe.matmul(p_v[:, i, :], lat[:, u, 1, i * P:(i + 1) * P], wv[:, :], start=True, stop=True)
                    mm.then_inc(s_v, 1)

        @block.scalar
        def _(act):
            act.sem_inc(s_lats, 1)
            with act.Fori(0, NG // 2) as r:
                for u in range(2):
                    g = r * 2 + u
                    act.wait_ge(s_lat, g + 1)
                    act.wait_ge(s_v, g + 1)
                    act.copy(lat[:, u, :, :], p_lat[:, :, :]).then_inc(s_lats, 1)
                    act.wait_ge(s_out[u], 16 * NOUT * (r + 1))
                    for w, ready in ((0, s_q), (1, s_k), (2, s_turned)):
                        n = rows[w]
                        src = turned[:, :] if w == 2 else p_qk[:, w, :]
                        act.wait_ge(ready, g + (2 if w == 2 else 1))
                        act.copy(parts[0:n, u, w, 0, :], src).then_inc(s_p1, 1)
                    for w in range(3):
                        n = rows[w]
                        act.wait_ge(s_rest, g * 3 + w + 4)
                        act.copy(parts[0:n, u, w, 1, :], rest[0:n, w, :]).then_inc(s_p2, 1)

        @block.vector
        def _(dve):
            dve.sem_inc(s_turned, 1)
            dve.sem_inc(s_rest, 3)
            dve.sem_inc(s_vout, 1)
            with dve.Fori(0, NG // 2) as r:
                for u in range(2):
                    g = r * 2 + u
                    cols = slice(u * GW, (u + 1) * GW)
                    dve.wait_ge(s_rot, g + 1)
                    dve.wait_ge(s_turned, g + 1)
                    dve.tensor_tensor(turn_c[:, :], p_rot[:, 0, :], cos[:, cols], ALU.mult).then_inc(s_trig, 1)
                    dve.tensor_tensor(turn_s[:, :], p_rot[:, 1, :], sin[:, cols], ALU.mult).then_inc(s_trig, 1)
                    for w in range(3):
                        n = rows[w]
                        src = turned[:, :] if w == 2 else p_qk[:, w, :]
                        dve.wait_ge(s_p1, g * 3 + w + 1)
                        dve.wait_ge(s_p3, g * 3 + w + 1)
                        dve.tensor_tensor(rest[0:n, w, :], src, parts[0:n, u, w, 0, :], ALU.subtract).then_inc(s_rest, 1)
                    dve.wait_ge(s_v, g + 3)
                    dst = V[:, bass.ds(r * HG, HG), u * GT:(u + 1) * GT, :].rearrange("p g i e -> p i g e")
                    dve.tensor_copy(dst, p_v[:, :, :].rearrange("p i (g e) -> p i g e", g=HG)).then_inc(s_vout, 1)


def attend(nc, name, rows, V, OT, C, scale, load, nload):
    with Stage(nc, name) as st:
        Q = st.sb("Q", [rows, 2, 4, S], BF16)
        K = st.sb("K", [rows, 2, 4, S], BF16)
        Pr = st.sb("Pr", [P, 2, 4, S])
        Vs = st.sb("Vs", [P, 2, TB, 4, 32])
        scores = st.ps("scores", [P, 2, S])
        summed = st.ps("summed", [P, 2, S])
        s_load = [st.sem("load0"), st.sem("load1")]
        s_set = st.sem("set")
        s_vs = st.sem("vs")
        s_scores = st.sem("scores")
        s_exp = st.sem("exp")
        s_clip = st.sem("clip")
        s_sum = st.sem("sum")
        s_ot = st.sem("ot")
        SC0 = 2 * 4 * NSEG
        EX0 = 2
        SU0 = 2 * NSEG
        OT0 = 2
        block = st.block()

        @block.sync
        def _(sp):
            with sp.Fori(0, ITS // 2) as r:
                for u in range(2):
                    it = r * 2 + u
                    sp.wait_ge(s_scores, it * (4 * NSEG) + SC0 - 4 * NSEG)
                    load(sp, Q, K, it, u, s_load[u])

        @block.gpsimd
        def _(pool):
            pool.memset(Vs[:, :, :, :, :], 0.0).then_inc(s_set, 1)
            pool.wait_ge(s_set, 1)
            pool.memset(Vs[:, :, :, :, DH:DH + 1], 1.0).then_inc(s_set, 1)
            pool.wait_ge(s_set, 2)
            with pool.Fori(0, ITS // 2) as r:
                for u in range(2):
                    it = r * 2 + u
                    pool.wait_ge(s_sum, it * NSEG + SU0 - NSEG)
                    src = V[:, bass.ds(it, 1), :, :].squeeze(1).rearrange("p k (j d) -> p k j d", j=4)
                    pool.tensor_copy(Vs[:, u, :, :, 0:DH], src).then_inc(s_vs, 1)

        @block.tensor
        def _(pe):
            def make_scores(it, u, k, j):
                n = it * (4 * NSEG) + (4 * k + j)
                pe.wait_ge(s_exp, n + 1)
                out = scores[:, j % 2, :]
                for kb, c0, w in SEGMENTS[k]:
                    keys = K[:, u, j, kb * P:(kb + 1) * P]
                    at = c0
                    while at < c0 + w:
                        end = min(c0 + w, (at // GW + 1) * GW)
                        q0 = kb * P + at - c0
                        mm = pe.matmul(out[:, at:end], keys, Q[:, u, j, q0:q0 + end - at], start=True, stop=True)
                        at = end
                mm.then_inc(s_scores, 1)

            def pieces(k):
                return [(kb, c0, a, b) for kb, c0, _ in SEGMENTS[k]
                        for a, b in ((kb * P, GW), (max(kb * P, GW), S)) if a < b]

            def sum_values(u, k, some):
                for kb, c0, q0, q1 in some:
                    for j in range(4):
                        mm = pe.matmul(summed[32 * j:32 * j + 32, u, q0:q1], Vs[:, u, kb, j, :],
                                       Pr[:, (u + k) % 2, j, c0 + q0 - kb * P:c0 + q1 - kb * P],
                                       start=(kb == 0), stop=(kb == (3 if q1 == GW else 4)),
                                       skip_group_check=True)
                return mm

            def loads(r, u):
                pe.wait_ge(s_load[u], nload * 16 * (r + 1))

            def iteration(r, u, final):
                it = r * 2 + u
                pe.wait_ge(s_vs, it + 1)
                pe.wait_ge(s_ot, it + 1)
                for k in range(NSEG):
                    ahead = (it, u, k + 1) if k + 1 < NSEG else (it + 1, 1 - u, 0)
                    scored = k + 1 < NSEG or not final
                    if scored:
                        if k + 1 == NSEG:
                            loads(r + u, 1 - u)
                        make_scores(*ahead, 0)
                        make_scores(*ahead, 1)
                    pe.wait_ge(s_clip, (it * NSEG + k) * 4 + 4)
                    some = pieces(k)
                    cut = (len(some) + 1) // 2
                    mm = sum_values(u, k, some[:cut])
                    if scored:
                        make_scores(*ahead, 2)
                    if some[cut:]:
                        mm = sum_values(u, k, some[cut:])
                    mm.then_inc(s_sum, 1)
                    if scored:
                        make_scores(*ahead, 3)

            pe.sem_inc(s_scores, SC0)
            pe.sem_inc(s_sum, SU0)
            loads(0, 0)
            for j in range(4):
                make_scores(0, 0, 0, j)
            with pe.Fori(0, ITS // 2 - 1) as r:
                iteration(r, 0, False)
                iteration(r, 1, False)
            iteration(ITS // 2 - 1, 0, False)
            iteration(ITS // 2 - 1, 1, True)

        @block.scalar
        def _(act):
            act.sem_inc(s_exp, EX0)
            with act.Fori(0, ITS // 2) as r:
                for u in range(2):
                    it = r * 2 + u
                    for k in range(NSEG):
                        act.wait_ge(s_sum, it * NSEG + (k - 1 + SU0))
                        for j in range(4):
                            n = it * (4 * NSEG) + (4 * k + j)
                            act.wait_ge(s_scores, n + 1 + SC0)
                            w = width(k)
                            act.activation(Pr[:, (u + k) % 2, j, 0:w], scores[:, j % 2, 0:w], ACT.Exp,
                                           scale=scale).then_inc(s_exp, 1)

        @block.vector
        def _(dve):
            dve.sem_inc(s_ot, OT0)
            with dve.Fori(0, ITS // 2) as r:
                for u in range(2):
                    it = r * 2 + u
                    lo, hi = float(np.exp(-CLIP * scale)), float(np.exp(CLIP * scale))
                    for k in range(NSEG):
                        for j in range(4):
                            n = it * (4 * NSEG) + (4 * k + j)
                            dve.wait_ge(s_exp, n + 1 + EX0)
                            w = Pr[:, (u + k) % 2, j, :]
                            for i, (kb, c0, cols) in enumerate(SEGMENTS[k]):
                                d = w[:, c0:c0 + P]
                                ins = dve.scalar_tensor_tensor(out=d, in0=d, scalar=lo, in1=C["top_kq"][:, :],
                                                               op0=ALU.max, op1=ALU.min)
                                if cols > P:
                                    e = w[:, c0 + P:c0 + cols]
                                    ins = dve.tensor_scalar(e, e, lo, hi, ALU.max, ALU.min)
                            ins.then_inc(s_clip, 1)
                    dve.wait_ge(s_sum, it * NSEG + (NSEG + SU0))
                    dve.tensor_copy(OT[:, bass.ds(it, 1), :].squeeze(1), summed[:, u, :]).then_inc(s_ot, 1)


def project_out(nc, name, X, OT, C, w_o, scratch):
    with Stage(nc, name) as st:
        wo = st.sb("wo", [P, HG, D])
        even = st.sb("even", [P, GW])
        inv = st.sb("inv", [P, GW])
        heads = st.sb("heads", [P, 2, HG, GW])
        factor = st.ps("factor", [P, HG, GW])
        y = st.ps("y", [P, 2, GT, P])
        s_zero = st.sem("zero")
        s_w = st.sem("w")
        s_even = st.sem("even")
        s_inv = st.sem("inv")
        s_back = st.sem("back")
        s_fac = st.sem("fac")
        s_heads = st.sem("heads")
        s_y = st.sem("y")
        s_res = st.sem("res")
        all_rows = scratch.sums.rearrange("j i (h n) -> (j i h) n", n=GW)
        block = st.block()


        @block.sync
        def _(sp):
            for j in range(4):
                row = 32 * j + DH
                sp.dma_start(scratch.sums[j:j + 1, :, :], OT[row:row + 1, :, :]).then_inc(s_even, 16)
            sp.wait_ge(s_even, 64)
            sp.dma_start(even[:, :], all_rows).then_inc(s_even, 16)
            sp.wait_ge(s_zero, 1)
            src = w_o.rearrange("(g j d) n -> j d g n", g=HG, j=4)
            for j in range(4):
                sp.dma_start(wo[32 * j:32 * j + DH, :, :], src[j]).then_inc(s_w, 16)
            sp.wait_ge(s_inv, 1)
            sp.dma_start(all_rows, inv[:, :]).then_inc(s_back, 16)
            sp.wait_ge(s_back, 16)
            for j in range(4):
                row = 32 * j + DH
                sp.dma_start(OT[row:row + 1, :, :], scratch.sums[j:j + 1, :, :]).then_inc(s_back, 16)

        @block.gpsimd
        def _(pool):
            pool.memset(wo[:, :, :], 0.0).then_inc(s_zero, 1)

        @block.tensor
        def _(pe):
            def spread_inverses(r, u):
                g = r * 2 + u
                for hg in range(HG):
                    pe.wait_ge(s_heads, g * HG + (hg + 1))
                    o = OT[:, bass.ds(r * HG + hg, 1), u * GW:(u + 1) * GW].squeeze(1)
                    pe.matmul(factor[:, hg, :], C["pick_sum"][:, :], o, start=True, stop=True).then_inc(s_fac, 1)

            def product(r, u):
                g = r * 2 + u
                pe.wait_ge(s_heads, g * HG + 2 * HG)
                pe.wait_ge(s_res, g + 1)
                for i in range(GT):
                    for hg in range(HG):
                        mm = pe.matmul(y[:, u, i, :], heads[:, u, hg, i * P:(i + 1) * P], wo[:, hg, :],
                                       start=(hg == 0), stop=(hg == HG - 1))
                mm.then_inc(s_y, 1)

            pe.sem_inc(s_y, 2)
            pe.wait_ge(s_w, 64)
            pe.wait_ge(s_back, 80)
            spread_inverses(0, 0)
            with pe.Fori(0, NG // 2 - 1) as r:
                spread_inverses(r, 1)
                product(r, 0)
                spread_inverses(r + 1, 0)
                product(r, 1)
            spread_inverses(NG // 2 - 1, 1)
            product(NG // 2 - 1, 0)
            product(NG // 2 - 1, 1)

        @block.vector
        def _(dve):
            dve.wait_ge(s_even, 80)
            dve.reciprocal(inv[:, :], even[:, :]).then_inc(s_inv, 1)
            dve.sem_inc(s_heads, HG)
            dve.sem_inc(s_res, 2)

            def scale(r, u):
                g = r * 2 + u
                dve.wait_ge(s_y, g + 1)
                for hg in range(HG):
                    dve.wait_ge(s_fac, g * HG + (hg + 1))
                    o = OT[:, bass.ds(r * HG + hg, 1), u * GW:(u + 1) * GW].squeeze(1)
                    dve.tensor_tensor(heads[:, u, hg, :], factor[:, hg, :], o, ALU.mult).then_inc(s_heads, 1)

            def add(r, u):
                g = r * 2 + u
                dve.wait_ge(s_y, g + 3)
                xt = X[:, bass.ds(g * GT, GT), :]
                dve.tensor_tensor(xt, y[:, u, :, :], xt, ALU.add).then_inc(s_res, 1)

            scale(0, 0)
            with dve.Fori(0, NG // 2 - 1) as r:
                scale(r, 1)
                add(r, 0)
                scale(r + 1, 0)
                add(r, 1)
            scale(NG // 2 - 1, 1)
            add(NG // 2 - 1, 0)
            add(NG // 2 - 1, 1)


def attention_a(nc, name, X, XnT, C, W):
    scratch = Scratch(nc, name, True)
    with ExitStack() as ctx:
        V = ctx.enter_context(nc.sbuf_tensor(f"{name}_V", [P, ITS, TB, 4 * DH], F32))
        project_a(nc, f"{name}p", XnT, C, W, scratch, V)

        def load(sp, Q, K, it, u, sem):
            one = bass.ds(it, 1)
            for i in range(PARTS):
                qc = scratch.qc[one, i, :, :].squeeze(0).rearrange("(j d) t -> d j t", d=DH)
                qr = scratch.qr[one, i, :, :].squeeze(0).rearrange("(j d) t -> d j t", d=DR)
                kc = scratch.kc[one, :, :, :].squeeze(0).rearrange("i (j d) t -> i d j t", d=DH)
                kr = scratch.kr[one, :, :, :].squeeze(0)
                for m in range(PARTS):
                    a, b = (i * PARTS + m) * DH, QC + (i * PARTS + m) * DR
                    sp.dma_start(Q[a:a + DH, u, :, :], qc).then_inc(sem, 16)
                    sp.dma_start(Q[b:b + DR, u, :, :], qr).then_inc(sem, 16)
                    sp.dma_start(K[a:a + DH, u, :, :], kc[m]).then_inc(sem, 16)
                    sp.dma_start(K[b:b + DR, u, :, :],
                                 kr[m:m + 1].rearrange("i d t -> d i t").to_broadcast([DR, 4, S])).then_inc(sem, 16)

        OT = ctx.enter_context(nc.sbuf_tensor(f"{name}_OT", [P, ITS, S], F32))
        attend(nc, f"{name}s", QC + QR, V, OT, C, float((DH + DR) ** -0.5), load, 4 * PAIRS)
        project_out(nc, f"{name}o", X, OT, C, W['W_O'], scratch)


def project_b(nc, name, XnT, C, W, scratch, V):
    with Stage(nc, name) as st:
        wd = st.sb("wd", [P, LAT_B])
        wq = st.sb("wq", [LAT_B, P])
        wkv = st.sb("wkv", [LAT_B, 2 * DH])
        lat = st.sb("lat", [LAT_B, 2, GW])
        rest = st.sb("rest", [P, 2, GW])
        parts = st.sb("parts", [P, 2, 2, PARTS, GW], BF16)
        p_lat = st.ps("p_lat", [LAT_B, GW])
        p_q = st.ps("p_q", [P, GW])
        p_k = st.ps("p_k", [DH, GW])
        p_v = st.ps("p_v", [P, GT, P])
        s_w = st.sem("w")
        s_lat = st.sem("lat")
        s_lats = st.sem("lats")
        s_q = st.sem("q")
        s_k = st.sem("k")
        s_v = st.sem("v")
        s_vout = st.sem("vout")
        s_p1 = st.sem("part1")
        s_rest = st.sem("rest")
        s_p2 = st.sem("part2")
        s_p3 = st.sem("part3")
        s_out = [st.sem("out0"), st.sem("out1")]
        NOUT = 2 * HG
        rows = (P, DH)
        banks = (p_q, p_k)
        block = st.block()

        @block.sync
        def _(sp):
            for dst, src in ((wd, W['Wc_down']), (wq, W['Wq_up']), (wkv, W['Wkv_up'])):
                sp.dma_start(dst[:, :], src).then_inc(s_w, 16)
            sp.sem_inc(s_out[0], 16 * NOUT)
            sp.sem_inc(s_out[1], 16 * NOUT)
            with sp.Fori(0, NG // 2) as r:
                for u in range(2):
                    g = r * 2 + u
                    cols = slice(u * GW, (u + 1) * GW)
                    sp.wait_ge(s_p3, g * 2 + 4)
                    for hg in range(HG):
                        for w, dram, a, n in ((0, scratch.qc, 4 * DH * hg, 4 * DH), (1, scratch.kc, 0, DH)):
                            dst = dram[bass.ds(r * HG + hg, 1), :, :, cols].squeeze(0).rearrange("i e t -> e i t")
                            sp.dma_start(dst, parts[a:a + n, u, w, :, :]).then_inc(s_out[u], 16)
            for u in range(2):
                sp.wait_ge(s_out[u], 16 * NOUT * (NG // 2 + 1))

        @block.gpsimd
        def _(pool):
            pool.sem_inc(s_p3, 2)
            with pool.Fori(0, NG // 2) as r:
                for u in range(2):
                    g = r * 2 + u
                    for w in range(2):
                        n = rows[w]
                        pool.wait_ge(s_p2, g * 2 + w + 1)
                        pool.tensor_tensor(parts[0:n, u, w, 2, :], rest[0:n, w, :], parts[0:n, u, w, 1, :],
                                           ALU.subtract).then_inc(s_p3, 1)

        @block.tensor
        def _(pe):
            pe.wait_ge(s_w, 48)
            pe.sem_inc(s_v, 2)
            with pe.Fori(0, NG // 2) as r:
                for u in range(2):
                    g = r * 2 + u
                    pe.wait_ge(s_lats, g + 1)
                    pe.matmul(p_lat[:, :], wd[:, :], XnT[:, bass.ds(g * GW, GW)], start=True,
                              stop=True).then_inc(s_lat, 1)
                    pe.wait_ge(s_lats, g + 2)
                    pe.wait_ge(s_rest, g * 2 + 2)
                    pe.matmul(p_q[:, :], wq[:, :], lat[:, u, :], start=True, stop=True).then_inc(s_q, 1)
                    pe.matmul(p_k[:, :], wkv[:, 0:DH], lat[:, u, :], start=True, stop=True).then_inc(s_k, 1)
                    pe.wait_ge(s_vout, g + 1)
                    for i in range(GT):
                        mm = pe.matmul(p_v[:, i, 0:DH], lat[:, u, i * P:(i + 1) * P], wkv[:, DH:2 * DH],
                                       start=True, stop=True)
                    mm.then_inc(s_v, 1)

        @block.scalar
        def _(act):
            act.sem_inc(s_lats, 1)
            with act.Fori(0, NG // 2) as r:
                for u in range(2):
                    g = r * 2 + u
                    act.wait_ge(s_lat, g + 1)
                    act.wait_ge(s_v, g + 1)
                    act.copy(lat[:, u, :], p_lat[:, :]).then_inc(s_lats, 1)
                    act.wait_ge(s_out[u], 16 * NOUT * (r + 1))
                    for w, ready in ((0, s_q), (1, s_k)):
                        act.wait_ge(ready, g + 1)
                        act.copy(parts[0:rows[w], u, w, 0, :], banks[w][:, :]).then_inc(s_p1, 1)
                    for w in range(2):
                        n = rows[w]
                        act.wait_ge(s_rest, g * 2 + w + 3)
                        act.copy(parts[0:n, u, w, 1, :], rest[0:n, w, :]).then_inc(s_p2, 1)

        @block.vector
        def _(dve):
            dve.sem_inc(s_rest, 2)
            dve.sem_inc(s_vout, 1)
            with dve.Fori(0, NG // 2) as r:
                for u in range(2):
                    g = r * 2 + u
                    for w in range(2):
                        n = rows[w]
                        dve.wait_ge(s_p1, g * 2 + w + 1)
                        dve.wait_ge(s_p3, g * 2 + w + 1)
                        dve.tensor_tensor(rest[0:n, w, :], banks[w][:, :], parts[0:n, u, w, 0, :],
                                          ALU.subtract).then_inc(s_rest, 1)
                    dve.wait_ge(s_v, g + 3)
                    dst = V[:, bass.ds(r * HG, HG), u * GT:(u + 1) * GT, :]
                    src = p_v[:, :, 0:DH].rearrange("p (o i) e -> p o i e", o=1).to_broadcast([P, HG, GT, DH])
                    dve.tensor_copy(dst, src).then_inc(s_vout, 1)


ROW_UNITS = [[(7, 0, 4)], [(7, 4, 4)], [(6, 0, 4)], [(6, 4, 3), (0, 0, 1)], [(5, 0, 4)],
             [(5, 4, 2), (1, 0, 2)], [(4, 0, 4)], [(4, 4, 1), (2, 0, 3)], [(3, 0, 4)]]
NUNIT = 4 * len(ROW_UNITS)


def attend_shared(nc, name, V, OT, C, scale, load, nload, mx):
    with Stage(nc, name) as st:
        Q = st.sb("Q", [QC + PARTS, 2, 4, S], BF16)
        K = st.sb("K", [QC + PARTS, 2, 1, S], BF16)
        Qm = st.sb("Qm", [QC, 2, 4, S], BF16)
        Km = st.sb("Km", [QC, 2, 1, S], BF16)
        Pr = st.sb("Pr", [P, 2, 4, S])
        Vs = st.sb("Vs", [P, 2, TB, 1, 32])
        top = st.sb("top", [P, 4, TB, 2])
        M = st.sb("M", [P, 4 * TB])
        neg = st.sb("neg", [4 * TB, P])
        rest = st.sb("rest", [4 * TB, P])
        parts = st.sb("parts", [4 * TB, PARTS, P], BF16)
        scores = st.ps("scores", [P, 2, S])
        summed = st.ps("summed", [P, S])
        rows = st.ps("rows", [P, 2, GW])
        s_load = [st.sem("load0"), st.sem("load1")]
        s_loadm = [st.sem("loadm0"), st.sem("loadm1")]
        s_set = st.sem("set")
        s_ones = st.sem("ones")
        s_vs = st.sem("vs")
        s_scores = st.sem("scores")
        s_exp = st.sem("exp")
        s_sum = st.sem("sum")
        s_ot = st.sem("ot")
        s_rows = st.sem("rows")
        s_read = st.sem("read")
        s_top = st.sem("top")
        s_turned = st.sem("turned")
        s_split = st.sem("split")
        s_mx = st.sem("mx")
        SC0 = 2 * 4 * NSEG
        EX0 = 2
        SU0 = 2 * NSEG
        NSTEP = 2 * PARTS
        LAST = ITS // 2 - 1
        block = st.block()

        @block.sync
        def _(sp):
            def load_rows(it, u):
                load(sp, Qm, Km, it, u, s_loadm[u])

            def send_and_load(it, u):
                load(sp, Q, K, it, u, s_load[u])
                sp.wait_ge(s_split, it * NSTEP + NSTEP)
                sp.dma_start(mx[:, bass.ds(it, 1), :, :].squeeze(1).rearrange("i j (k q) -> (j k) i q", q=P),
                             parts[:, :, :]).then_inc(s_mx, 16)
                sp.wait_ge(s_mx, it * 16 + 16)
                sp.dma_start(Q[QC:QC + PARTS, u, :, :], mx[:, bass.ds(it, 1), :, :].squeeze(1)).then_inc(s_load[u], 16)

            def iteration(r, u, rows_too=True):
                it = r * 2 + u
                if rows_too:
                    sp.wait_ge(s_rows, it * NUNIT + 2 * NUNIT)
                    load_rows(it + 3, 1 - u)
                sp.wait_ge(s_scores, it * (4 * NSEG) + SC0)
                send_and_load(it + 1, 1 - u)

            load_rows(0, 0)
            load_rows(1, 1)
            sp.wait_ge(s_rows, NUNIT)
            load_rows(2, 0)
            sp.wait_ge(s_ones, 1)
            send_and_load(0, 0)
            with sp.Fori(0, LAST - 1) as r:
                iteration(r, 0)
                iteration(r, 1)
            iteration(LAST - 1, 0)
            iteration(LAST - 1, 1, rows_too=False)
            iteration(LAST, 0, rows_too=False)

        @block.gpsimd
        def _(pool):
            pool.memset(K[:, :, :, :], 1.0).then_inc(s_ones, 1)
            pool.memset(top[:, :, :, :], LOWEST).then_inc(s_top, 1)
            pool.memset(Vs[:, :, :, :, :], 0.0).then_inc(s_set, 1)
            pool.wait_ge(s_set, 1)
            pool.memset(Vs[:, :, :, :, DH:DH + 1], 1.0).then_inc(s_set, 1)
            pool.wait_ge(s_set, 2)
            with pool.Fori(0, ITS // 2) as r:
                for u in range(2):
                    it = r * 2 + u
                    pool.wait_ge(s_sum, it * NSEG + SU0 - NSEG)
                    src = V[:, bass.ds(it, 1), :, :].squeeze(1).rearrange("p k (j d) -> p k j d", j=1)
                    pool.tensor_copy(Vs[:, u, :, :, 0:DH], src).then_inc(s_vs, 1)

        @block.tensor
        def _(pe):
            def make_scores(it, u, k, j):
                n = it * (4 * NSEG) + (4 * k + j)
                pe.wait_ge(s_exp, n + 1)
                out = scores[:, j % 2, :]
                for kb, c0, w in SEGMENTS[k]:
                    keys = K[:, u, 0, kb * P:(kb + 1) * P]
                    at = c0
                    while at < c0 + w:
                        end = min(c0 + w, (at // GW + 1) * GW)
                        q0 = kb * P + at - c0
                        mm = pe.matmul(out[:, at:end], keys, Q[:, u, j, q0:q0 + end - at], start=True, stop=True)
                        if at == c0:
                            mm = pe.matmul(out[:, at:at + P], C["ident_b"][:, :], C["neg_kq_b"][:, :],
                                           start=False, stop=True, skip_group_check=True)
                        at = end
                mm.then_inc(s_scores, 1)

            def make_rows(it, u, c):
                j, unit = c // len(ROW_UNITS), ROW_UNITS[c % len(ROW_UNITS)]
                pe.wait_ge(s_read, it * NUNIT + (c + 1))
                at = 0
                for qb, kb, n in unit:
                    end = at + n * P
                    mm = pe.matmul(rows[:, c % 2, at:end], Qm[:, u, j, qb * P:(qb + 1) * P],
                                   Km[:, u, 0, kb * P:(kb + n) * P], start=True, stop=True)
                    if kb + n == qb + 1:
                        mm = pe.matmul(rows[:, c % 2, end - P:end], C["ident_b"][:, :], C["neg_qk_b"][:, :],
                                       start=False, stop=True, skip_group_check=True)
                    at = end
                mm.then_inc(s_rows, 1)

            def turn(it):
                pe.wait_ge(s_top, it + 2)
                pe.transpose(rows[0:4 * TB, 1, 0:P], M[:, :], C["ident"][:, :]).then_inc(s_turned, 1)

            def turned_is_read(it):
                pe.wait_ge(s_split, it * NSTEP + 1)

            def pieces(k):
                return [(kb, c0, a, b) for kb, c0, _ in SEGMENTS[k]
                        for a, b in ((kb * P, GW), (max(kb * P, GW), S)) if a < b]

            def sum_values(u, k, some, some_rows):
                for n, (kb, c0, q0, q1) in enumerate(some):
                    if n:
                        some_rows(1)
                    for j in range(4):
                        mm = pe.matmul(summed[32 * j:32 * j + 32, q0:q1], Vs[:, u, kb, 0, :],
                                       Pr[:, (u + k) % 2, j, c0 + q0 - kb * P:c0 + q1 - kb * P],
                                       start=(kb == 0), stop=(kb == (3 if q1 == GW else 4)),
                                       skip_group_check=True)
                return mm

            def loads(r, u):
                pe.wait_ge(s_load[u], (nload + 1) * 16 * (r + 1))

            def iteration(r, u, final=False, rows_too=True):
                it = r * 2 + u
                units = iter(range(NUNIT if rows_too else 0))

                def some_rows(n):
                    for _ in range(n):
                        c = next(units, None)
                        if c is not None:
                            make_rows(it + 2, u, c)

                pe.wait_ge(s_vs, it + 1)
                for k in range(NSEG):
                    ahead = (it, u, k + 1) if k + 1 < NSEG else (it + 1, 1 - u, 0)
                    scored = k + 1 < NSEG or not final
                    if scored:
                        if k + 1 == NSEG:
                            loads(r + u, 1 - u)
                        make_scores(*ahead, 0)
                        some_rows(1 if k else 0)
                        make_scores(*ahead, 1)
                    if k == 0 and not final:
                        turn(it + 1)
                    some_rows(1 if k else 0)
                    pe.wait_ge(s_exp, (it * NSEG + k) * 4 + 4 + EX0)
                    if k == 0:
                        pe.wait_ge(s_ot, it + 1)
                        if rows_too:
                            pe.wait_ge(s_loadm[u], nload * 16 * (r + 2))
                            turned_is_read(it + 1)
                    some = pieces(k)
                    cut = (len(some) + 1) // 2
                    mm = sum_values(u, k, some[:cut], some_rows)
                    some_rows(2)
                    if scored:
                        make_scores(*ahead, 2)
                    if some[cut:]:
                        some_rows(1)
                        mm = sum_values(u, k, some[cut:], some_rows)
                    mm.then_inc(s_sum, 1)
                    some_rows(1)
                    if scored:
                        make_scores(*ahead, 3)
                    some_rows(1)
                some_rows(NUNIT)

            pe.sem_inc(s_scores, SC0)
            pe.sem_inc(s_sum, SU0)
            for it in range(2):
                pe.wait_ge(s_loadm[it], nload * 16)
                if it:
                    turn(0)
                    turned_is_read(0)
                for c in range(NUNIT):
                    make_rows(it, it, c)
            loads(0, 0)
            for j in range(4):
                make_scores(0, 0, 0, j)
            with pe.Fori(0, LAST) as r:
                iteration(r, 0)
                iteration(r, 1)
            iteration(LAST, 0, rows_too=False)
            iteration(LAST, 1, final=True, rows_too=False)

        @block.scalar
        def _(act):
            def weights(it, u, k):
                act.wait_ge(s_sum, it * NSEG + (k - 1 + SU0))
                for j in range(4):
                    act.wait_ge(s_scores, it * (4 * NSEG) + (4 * k + j + 1 + SC0))
                    w = width(k)
                    act.activation(Pr[:, (u + k) % 2, j, 0:w], scores[:, j % 2, 0:w], ACT.Exp,
                                   scale=scale).then_inc(s_exp, 1)

            def iteration(r, u, final=False):
                it = r * 2 + u
                for k in range(1, NSEG):
                    weights(it, u, k)
                if not final:
                    weights(it + 1, 1 - u, 0)
                act.wait_ge(s_sum, it * NSEG + (NSEG + SU0))
                act.copy(OT[:, bass.ds(it, 1), :].squeeze(1), summed[:, :]).then_inc(s_ot, 1)

            act.sem_inc(s_exp, EX0)
            act.sem_inc(s_ot, 1)
            weights(0, 0, 0)
            with act.Fori(0, LAST) as r:
                iteration(r, 0)
                iteration(r, 1)
            iteration(LAST, 0)
            iteration(LAST, 1, final=True)

        @block.vector
        def _(dve):
            def maxima(it):
                dve.wait_ge(s_top, it + 1)
                for c in range(NUNIT):
                    j, unit = c // len(ROW_UNITS), ROW_UNITS[c % len(ROW_UNITS)]
                    dve.wait_ge(s_rows, it * NUNIT + (c + 1))
                    at = 0
                    for qb, kb, n in unit:
                        end = at + n * P
                        ins = dve.reduce_max(top[:, j, qb, kb // 4:kb // 4 + 1], rows[:, c % 2, at:end], AX_X)
                        at = end
                    ins.then_inc(s_read, 1)
                dve.wait_ge(s_read, it * NUNIT + (NUNIT + 2))
                dve.reduce_max(M[:, :], top[:, :, :, :].rearrange("p j k b -> p (j k) b"), AX_X).then_inc(s_top, 1)

            def split(it):
                dve.wait_ge(s_turned, it + 1)
                dve.tensor_scalar(neg[:, :], rows[0:4 * TB, 1, 0:P], -1.0, None, ALU.mult).then_inc(s_split, 1)
                src = neg
                for i in range(PARTS):
                    dve.wait_ge(s_split, it * NSTEP + (2 * i + 1))
                    dve.tensor_copy(parts[:, i, :], src[:, :]).then_inc(s_split, 1)
                    if i < PARTS - 1:
                        dve.wait_ge(s_split, it * NSTEP + (2 * i + 2))
                        dve.tensor_tensor(rest[:, :], src[:, :], parts[:, i, :], ALU.subtract).then_inc(s_split, 1)
                        src = rest

            def iteration(r, u):
                it = r * 2 + u
                dve.wait_ge(s_mx, it * 16 + 16)
                split(it + 1)
                maxima(it + 2)

            dve.sem_inc(s_read, 2)
            maxima(0)
            split(0)
            maxima(1)
            with dve.Fori(0, LAST) as r:
                iteration(r, 0)
                iteration(r, 1)
            dve.wait_ge(s_mx, 16 * (ITS - 1))
            split(ITS - 1)


def attention_b(nc, name, X, XnT, C, W):
    scratch = Scratch(nc, name, False)
    with ExitStack() as ctx:
        V = ctx.enter_context(nc.sbuf_tensor(f"{name}_V", [P, ITS, TB, DH], F32))
        project_b(nc, f"{name}p", XnT, C, W, scratch, V)

        def load(sp, Q, K, it, u, sem):
            one = bass.ds(it, 1)
            kc = scratch.kc[one, :, :, :].squeeze(0)
            for i in range(PARTS):
                qc = scratch.qc[one, i, :, :].squeeze(0).rearrange("(j d) t -> d j t", d=DH)
                for m in range(PARTS):
                    a = (i * PARTS + m) * DH
                    sp.dma_start(Q[a:a + DH, u, :, :], qc).then_inc(sem, 16)
                    sp.dma_start(K[a:a + DH, u, 0, :], kc[m]).then_inc(sem, 16)

        OT = ctx.enter_context(nc.sbuf_tensor(f"{name}_OT", [P, ITS, S], F32))
        attend_shared(nc, f"{name}s", V, OT, C, float(DH ** -0.5), load, 2 * PAIRS, scratch.mx)
        project_out(nc, f"{name}o", X, OT, C, W['Wc_proj'], scratch)


def recurrence(nc, name, X, XnT, C, W):
    with Stage(nc, name) as st:
        wl = st.sb("wl", [NS, 2, P])
        wlT = st.sb("wlT", [P, 2, NS])
        wc = st.sb("wc", [P, B, NS])
        wcT = st.sb("wcT", [P, P])
        bl = st.sb("bl", [P, 1])
        dp = st.sb("dp", [P, 1])
        diag = st.sb("diag", [P, P])
        lam = st.sb("lam", [P, S])
        states = st.sb("states", [P, S])
        p_w = st.ps("p_w", [P, GW])
        z = st.ps("z", [P, S])
        bu = st.ps("bu", [P, S])
        y = st.ps("y", [P, 2, GT, P])
        s_w = st.sem("w")
        s_turn = st.sem("turn")
        s_wT = st.sem("wT")
        s_z = st.sem("z")
        s_bu = st.sem("bu")
        s_lam = st.sem("lam")
        s_scan = st.sem("scan")
        s_y = st.sem("y")
        s_res = st.sem("res")
        block = st.block()

        @block.sync
        def _(sp):
            sp.dma_start(wl[:, 0, :], W['Wl']).then_inc(s_w, 16)
            sp.dma_start(wl[:, 1, :], W['Wb']).then_inc(s_w, 16)
            sp.dma_start(dp[:, :], W['Dp'].rearrange("(p o) -> p o", o=1)).then_inc(s_w, 16)
            for b in range(B):
                sp.dma_start(wc[:, b, :], W['Wc']).then_inc(s_w, 16)
                sp.dma_start(bl[b * NS:(b + 1) * NS, :], W['bl'].rearrange("(p o) -> p o", o=1)).then_inc(s_w, 16)

        @block.tensor
        def _(pe):
            pe.wait_ge(s_w, 16 * (3 + 2 * B))
            for k in range(2):
                pe.transpose(p_w[:, k * NS:(k + 1) * NS], wl[:, k, :], C["ident"][0:NS, 0:NS])
            pe.transpose(p_w[:, P:2 * P], wc[:, :, :], C["ident"][:, :]).then_inc(s_turn, 1)
            pe.wait_ge(s_wT, 3)
            for k, (dst, sem) in enumerate(((z, s_z), (bu, s_bu))):
                for half in range(2):
                    for b in range(B):
                        cols = slice(half * GW, (half + 1) * GW)
                        t0 = b * S + half * GW
                        mm = pe.matmul(dst[b * NS:(b + 1) * NS, cols], wlT[:, k, :], XnT[:, t0:t0 + GW],
                                       start=True, stop=True)
                mm.then_inc(sem, 1)
            pe.wait_ge(s_scan, 1)
            for g in range(NG):
                b = g // 2
                if g >= 2:
                    pe.wait_ge(s_res, g - 1)
                for i in range(GT):
                    t = g * GT + i
                    at = (t % TB) * P
                    pe.matmul(y[:, g % 2, i, :], states[b * NS:(b + 1) * NS, at:at + P],
                              wcT[b * NS:(b + 1) * NS, :], start=True, stop=False)
                    mm = pe.matmul(y[:, g % 2, i, :], XnT[:, t * P:(t + 1) * P], diag[:, :], start=False, stop=True)
                mm.then_inc(s_y, 1)

        @block.scalar
        def _(act):
            act.wait_ge(s_z, 1)
            act.activation(lam[:, :], z[:, :], ACT.Sigmoid, bias=bl[:, 0:1]).then_inc(s_lam, 1)

        @block.vector
        def _(dve):
            dve.wait_ge(s_turn, 1)
            dve.tensor_copy(wlT[:, :, :], p_w[:, 0:2 * NS].rearrange("p (k n) -> p k n", k=2)).then_inc(s_wT, 1)
            dve.tensor_copy(wcT[:, :], p_w[:, P:2 * P]).then_inc(s_wT, 1)
            dve.tensor_scalar(diag[:, :], C["ident"][:, :], dp[:, 0:1], None, ALU.mult).then_inc(s_wT, 1)
            dve.wait_ge(s_bu, 1)
            dve.wait_ge(s_lam, 1)
            dve.tensor_tensor_scan(states[:, :], lam[:, :], bu[:, :], 0.0, ALU.mult, ALU.add).then_inc(s_scan, 1)
            for g in range(NG):
                dve.wait_ge(s_y, g + 1)
                xt = X[:, g * GT:(g + 1) * GT, :]
                dve.tensor_tensor(xt, y[:, g % 2, :, :], xt, ALU.add).then_inc(s_res, 1)


LIMIT, ALPHA = 7.0, 1.702
ROUTE_AT = 32
FAR = -3.0e38


class Experts:

    def __init__(self, nc, ctx):
        def sb(n, shape, dt=F32):
            return ctx.enter_context(nc.sbuf_tensor(f"experts_{n}", shape, dt))

        self.w1T = sb("w1T", [P, E, P])
        self.w2T = sb("w2T", [P, E, P])
        self.b1 = sb("b1", [P, E])
        self.b2 = sb("b2", [E, P])
        self.gwT = sb("gwT", [P, E])
        self.gb = sb("gb", [P, E])
        self.pick = sb("pick", [96, E, P], BF16)


def load_experts(nc, name, C, W, X_):
    with Stage(nc, name) as st:
        raw = st.sb("raw", [P, 2, E, P])
        b1raw = st.sb("b1raw", [E, 2 * P])
        gw = st.sb("gw", [E, P])
        turned = st.ps("turned", [P, 2, GT, P])
        small = st.ps("small", [P, 2 * E])
        s_w = st.sem("w")
        s_zero = st.sem("zero")
        s_turn = st.sem("turn")
        s_out = st.sem("out")
        s_small = st.sem("small")
        NB = 2 * E // GT
        block = st.block()

        @block.sync
        def _(sp):
            sp.dma_start(raw[:, 0, :, :], W['mlp1_w'].rearrange("e (i s) h -> s i e h", s=2)[0]).then_inc(s_w, 16)
            sp.dma_start(raw[:, 1, :, :], W['mlp2_w'].rearrange("e i h -> i e h")).then_inc(s_w, 16)
            sp.dma_start(b1raw[:, :], W['mlp1_b']).then_inc(s_w, 16)
            sp.dma_start(gw[:, :], W['gate_w']).then_inc(s_w, 16)
            sp.dma_start(X_.b2[:, :], W['mlp2_b']).then_inc(s_w, 16)
            sp.dma_start(X_.gb[:, :], W['gate_b'].rearrange("(o e) -> o e", o=1).to_broadcast([P, E])).then_inc(s_w, 16)

        @block.tensor
        def _(pe):
            pe.wait_ge(s_w, 96)
            pe.transpose(small[:, 0:E], b1raw[:, :].rearrange("e (i s) -> e s i", s=2)[:, 0, :], C["ident"][0:E, 0:E])
            pe.transpose(small[:, E:2 * E], gw[:, :], C["ident"][0:E, 0:E]).then_inc(s_small, 1)
            for n in range(NB):
                if n >= 2:
                    pe.wait_ge(s_out, n - 1)
                for i in range(GT):
                    k, e = n // (NB // 2), (n % (NB // 2)) * GT + i
                    mm = pe.transpose(turned[:, n % 2, i, :], raw[:, k, e, :], C["ident"][:, :])
                mm.then_inc(s_turn, 1)

        @block.vector
        def _(dve):
            dve.wait_ge(s_small, 1)
            dve.tensor_copy(X_.b1[:, :], small[:, 0:E]).then_inc(s_zero, 1)
            dve.tensor_copy(X_.gwT[:, :], small[:, E:2 * E]).then_inc(s_zero, 1)
            dve.tensor_copy(X_.pick[:, :, :], C["pick_row"][:, :].rearrange("k (e o) -> k e o", o=1)
                            .to_broadcast([96, E, P])).then_inc(s_zero, 1)

        @block.scalar
        def _(act):
            for n in range(NB):
                act.wait_ge(s_turn, n + 1)
                e = (n % (NB // 2)) * GT
                dst = (X_.w1T, X_.w2T)[n // (NB // 2)]
                act.copy(dst[:, e:e + GT, :], turned[:, n % 2, :, :]).then_inc(s_out, 1)


def route(nc, name, XnT, C, X_, routeT, routes_b):
    with Stage(nc, name) as st:
        gates = st.sb("gates", [P, NT, E + 8])
        rest_g = st.sb("rest_g", [P, NT, E + 8])
        best = st.sb("best", [P, NT, 8])
        taken = st.sb("taken", [P, NT, E])
        diff = st.sb("diff", [P, NT, E])
        weight = st.sb("weight", [P, NT, E])
        kept = st.sb("kept", [P, NT, E])
        total = st.sb("total", [P, NT])
        inv = st.sb("inv", [P, NT])
        routes = st.sb("routes", [P, NT, E])
        rest = st.sb("rest", [E, 2, TOK // 2])
        logits = st.ps("logits", [P, NT, E])
        turned = st.ps("turned", [E, TOK // 2])
        s_far = st.sem("far")
        s_clear = st.sem("clear")
        s_log = st.sem("log")
        s_gate = st.sem("gate")
        s_best = st.sem("best")
        s_four = st.sem("four")
        s_left = st.sem("left")
        s_diff = st.sem("diff")
        s_exp = st.sem("exp")
        s_step = st.sem("step")
        s_turn = st.sem("turn")
        s_whole = st.sem("whole")
        s_part = st.sem("part")
        block = st.block()

        @block.gpsimd
        def _(pool):
            pool.memset(gates[:, :, E:E + 8], FAR).then_inc(s_far, 1)
            pool.memset(routes_b[:, :], 0.0).then_inc(s_clear, 1)

        @block.tensor
        def _(pe):
            for t in range(NT):
                mm = pe.matmul(logits[:, t, :], XnT[:, t * P:(t + 1) * P], X_.gwT[:, :], start=True, stop=True)
            mm.then_inc(s_log, 1)
            pe.wait_ge(s_step, 5)
            for half in range(2):
                if half:
                    pe.wait_ge(s_part, PARTS + 2)
                for i in range(NT // 2):
                    mm = pe.transpose(turned[:, i * P:(i + 1) * P], routes[:, half * NT // 2 + i, :], C["ident"][:, :])
                mm.then_inc(s_turn, 1)

        @block.scalar
        def _(act):
            act.wait_ge(s_diff, 1)
            act.activation(weight[:, :, :], diff[:, :, :], ACT.Exp).then_inc(s_exp, 1)
            for half in range(2):
                act.wait_ge(s_turn, half + 1)
                act.wait_ge(s_part, half * (PARTS + 2)) if half else None
                act.copy(routeT[:, half * TOK // 2:(half + 1) * TOK // 2], turned[:, :]).then_inc(s_whole, 1)

        @block.vector
        def _(dve):
            dve.wait_ge(s_log, 1)
            gb = X_.gb[:, :].rearrange("p (o e) -> p o e", o=1).to_broadcast([P, NT, E])
            dve.tensor_tensor(gates[:, :, 0:E], logits[:, :, :], gb, ALU.add).then_inc(s_gate, 1)
            dve.wait_ge(s_gate, 1)
            dve.wait_ge(s_far, 1)
            for t in range(NT):
                dve.max(best[:, t, :], gates[:, t, 0:E]).then_inc(s_best, 1)
            dve.wait_ge(s_best, NT)
            dve.tensor_tensor(diff[:, :, :], gates[:, :, 0:E], best[:, :, 0:1].to_broadcast([P, NT, E]),
                              ALU.subtract).then_inc(s_diff, 1)
            dve.memset(best[:, :, TOPK:8], FAR).then_inc(s_four, 1)
            dve.wait_ge(s_four, 1)
            for t in range(NT):
                dve.match_replace(rest_g[:, t, :], best[:, t, :], gates[:, t, :], FAR).then_inc(s_left, 1)
            dve.wait_ge(s_left, NT)
            dve.tensor_scalar(taken[:, :, :], rest_g[:, :, 0:E], FAR, None, ALU.is_equal).then_inc(s_step, 1)
            dve.wait_ge(s_step, 1)
            dve.wait_ge(s_exp, 1)
            dve.tensor_tensor(kept[:, :, :], weight[:, :, :], taken[:, :, :], ALU.mult).then_inc(s_step, 1)
            dve.wait_ge(s_step, 2)
            dve.reduce_sum(total[:, :], kept[:, :, :], AX_X).then_inc(s_step, 1)
            dve.wait_ge(s_step, 3)
            dve.reciprocal(inv[:, :], total[:, :]).then_inc(s_step, 1)
            dve.wait_ge(s_step, 4)
            dve.tensor_tensor(routes[:, :, :], kept[:, :, :], spread(inv[:, :], E), ALU.mult).then_inc(s_step, 1)
            dve.wait_ge(s_clear, 1)
            for half in range(2):
                cols = slice(half * TOK // 2, (half + 1) * TOK // 2)
                dve.wait_ge(s_whole, half + 1)
                src = routeT[:, cols]
                base = half * (PARTS + 2)
                for i in range(PARTS):
                    part = routes_b[i * ROUTE_AT:i * ROUTE_AT + E, cols]
                    dve.wait_ge(s_part, base + 2 * i) if base + 2 * i else None
                    dve.tensor_copy(part, src).then_inc(s_part, 1)
                    if i < PARTS - 1:
                        dve.wait_ge(s_part, base + 2 * i + 1)
                        dve.tensor_tensor(rest[:, i % 2, :], src, part, ALU.subtract).then_inc(s_part, 1)
                        src = rest[:, i % 2, :]


def experts(nc, name, X, XnT, C, X_, routeT, routes_b):
    with Stage(nc, name) as st:
        limited = st.sb("limited", [P, 2, GW])
        glu = st.sb("glu", [P, 2, GW])
        hidden = st.sb("hidden", [P, 2, GW])
        r_slot = st.sb("r_slot", [E, 2, GW])
        h = st.ps("h", [P, 2, GW])
        r_all = st.ps("r_all", [P, 2, GW])
        y = st.ps("y", [P, 2, GT, P])
        s_rs = st.sem("rs")
        s_h = st.sem("h")
        s_lim = st.sem("lim")
        s_glu = st.sem("glu")
        s_hid = st.sem("hid")
        s_r = st.sem("r")
        s_y = st.sem("y")
        s_res = st.sem("res")
        block = st.block()

        @block.tensor
        def _(pe):
            def up(g, e):
                n = g * E + e
                pe.wait_ge(s_lim, n + 1)
                pe.matmul(h[:, e % 2, :], X_.w1T[:, e, :], XnT[:, bass.ds(g * GW, GW)], start=True,
                          stop=True).then_inc(s_h, 1)

            def spread_route(g, e):
                n = g * E + e
                pe.wait_ge(s_hid, n + 1)
                pe.matmul(r_all[:, e % 2, :], X_.pick[:, e, :], routes_b[:, bass.ds(g * GW, GW)], start=True,
                          stop=True).then_inc(s_r, 1)

            def later(g, e):
                return (g, e) if e < E else (g + 1, e - E)

            def group(g, u, final):
                pe.wait_ge(s_res, g + 1)
                pe.wait_ge(s_rs, g + 1)
                for i in range(GT):
                    pe.matmul(y[:, u, i, :], r_slot[:, u, i * P:(i + 1) * P], X_.b2[:, :], start=(i == 0),
                              stop=False, skip_group_check=True)
                for e in range(E):
                    if not final or e + 2 < E:
                        up(*later(g, e + 2))
                    if not final or e + 1 < E:
                        spread_route(*later(g, e + 1))
                    pe.wait_ge(s_hid, g * E + (e + 3))
                    for i in range(GT):
                        mm = pe.matmul(y[:, u, i, :], hidden[:, e % 2, i * P:(i + 1) * P], X_.w2T[:, e, :],
                                       start=False, stop=(e == E - 1), skip_group_check=True)
                    mm.then_inc(s_y, 1)

            pe.sem_inc(s_y, 2 * E)
            up(0, 0)
            up(0, 1)
            spread_route(0, 0)
            with pe.Fori(0, NG // 2 - 1) as r:
                for u in range(2):
                    group(r * 2 + u, u, False)
            group(NG - 2, 0, False)
            group(NG - 1, 1, True)

        @block.scalar
        def _(act):
            with act.Fori(0, NG // 2) as r:
                for u in range(2):
                    g = r * 2 + u
                    act.wait_ge(s_y, g * E + E)
                    act.copy(r_slot[:, u, :], routeT[:, bass.ds(g * GW, GW)]).then_inc(s_rs, 1)
                    for e in range(E):
                        n = g * E + e
                        act.wait_ge(s_lim, n + 3)
                        act.wait_ge(s_hid, n + 1)
                        act.activation(glu[:, e % 2, :], limited[:, e % 2, :], ACT.Gelu_apprx_sigmoid).then_inc(s_glu, 1)

        @block.vector
        def _(dve):
            def limit(g, e):
                n = g * E + e
                dve.wait_ge(s_h, n + 1)
                dve.wait_ge(s_glu, n + 1)
                dve.tensor_scalar(limited[:, e % 2, :], h[:, e % 2, :], X_.b1[:, e:e + 1], LIMIT,
                                  ALU.add, ALU.min).then_inc(s_lim, 1)

            def weigh(g, e):
                n = g * E + e
                dve.wait_ge(s_glu, n + 3)
                dve.wait_ge(s_r, n + 1)
                dve.wait_ge(s_y, n + (2 * E - 1))
                dve.scalar_tensor_tensor(out=hidden[:, e % 2, :], in0=glu[:, e % 2, :], scalar=LIMIT + 1.0,
                                         in1=r_all[:, e % 2, :], op0=ALU.mult, op1=ALU.mult).then_inc(s_hid, 1)

            def group(g, u, final):
                for e in range(E):
                    if e + 1 < E:
                        limit(g, e + 1)
                    elif not final:
                        limit(g + 1, 0)
                    weigh(g, e)
                dve.wait_ge(s_y, g * E + 3 * E)
                xt = X[:, bass.ds(g * GT, GT), :]
                dve.tensor_tensor(xt, y[:, u, :, :], xt, ALU.add).then_inc(s_res, 1)

            dve.sem_inc(s_lim, 2)
            dve.sem_inc(s_hid, 2)
            dve.sem_inc(s_glu, 2)
            dve.sem_inc(s_res, 2)
            limit(0, 0)
            with dve.Fori(0, NG // 2 - 1) as r:
                for u in range(2):
                    group(r * 2 + u, u, False)
            group(NG - 2, 0, False)
            group(NG - 1, 1, True)


NCH = S // P
LEVELS = 7
PROJ = 3 * P + 2


def chunk(t, c):
    if len(t.shape) == 2:
        return t[:, :].rearrange("p (b c n) -> p b c n", b=B, n=P)[:, :, bass.ds(c, 1), :].squeeze(2)
    return t[:, :, :].rearrange("p (b c) n -> p b c n", b=B)[:, :, bass.ds(c, 1), :].squeeze(2)


def scalars(t, c):
    a = t.rearrange("p (b c) -> p b c", b=B)[:, :, bass.ds(c, 1)]
    return a.to_broadcast([P, B, P])


def delta_project(nc, name, XnT, C, W, Kt, Vt, Gt, qT, wo, cols):
    with Stage(nc, name) as st:
        raw = st.sb("raw", [P, 5, P])
        rawab = st.sb("rawab", [1, 2, P])
        wT = st.sb("wT", [P, P])
        wall = st.sb("wall", [P, PROJ])
        brow = st.sb("brow", [1, PROJ])
        bq = st.sb("bq", [P, 1])
        xs = st.sb("xs", [P, 2, GW])
        sq = st.sb("sq", [P, GT, P])
        logit = st.sb("logit", [P, 2, NT])
        length = st.sb("length", [P, NT])
        tmp = st.sb("tmp", [P, 6, NT])
        p_q = st.ps("p_q", [P, GW])
        p_all = st.ps("p_all", [P, GT, GW])
        p_w = st.ps("p_w", [P, 2, GT, P])
        s_w = st.sem("w")
        s_turn = st.sem("turn")
        s_wT = st.sem("wT")
        s_xs = st.sem("xs")
        s_q = st.sem("q")
        s_all = st.sem("all")
        s_qo = st.sem("qo")
        s_kv = st.sem("kv")
        s_gate = st.sem("gate")
        s_sq = st.sem("sq")
        s_len = st.sem("len")
        s_fin = st.sem("fin")
        s_act = st.sem("act")
        s_sum = st.sem("sum")
        names = ('Wq', 'Wk', 'Wv', 'Wg', 'Wo')
        block = st.block()

        @block.sync
        def _(sp):
            for i, n in enumerate(names):
                sp.dma_start(raw[:, i, :], W[n]).then_inc(s_w, 16)
            for i, n in enumerate(('Wa', 'Wb')):
                sp.dma_start(rawab[:, i, :], W[n]).then_inc(s_w, 16)
            sp.dma_start(bq[:, :], W['bq'].rearrange("(p o) -> p o", o=1)).then_inc(s_w, 16)
            for at, n in ((0, 'bk'), (P, 'bv'), (2 * P, 'bg'), (3 * P, 'ba'), (3 * P + 1, 'bb')):
                m = W[n].shape[0]
                sp.dma_start(brow[:, at:at + m], W[n].rearrange("(o n) -> o n", o=1)).then_inc(s_w, 16)

        @block.gpsimd
        def _(pool):
            with pool.Fori(0, NG // 2) as r:
                for u in range(2):
                    g = r * 2 + u
                    pool.wait_ge(s_all, g + 1)
                    pool.tensor_copy(xs[:, u, :], XnT[:, bass.ds(g * GW, GW)]).then_inc(s_xs, 1)

        @block.tensor
        def _(pe):
            pe.wait_ge(s_w, 16 * 13)
            for i in range(5):
                pe.transpose(p_w[:, i // GT, i % GT, :], raw[:, i, :], C["ident"][:, :])
            for i in range(2):
                mm = pe.transpose(p_w[:, 1, 1 + i, 0:1], rawab[:, i, :], C["ident"][0:1, 0:1])
            mm.then_inc(s_turn, 1)
            pe.sem_inc(s_all, 2)
            pe.wait_ge(s_wT, 4)
            with pe.Fori(0, NG // 2) as r:
                for u in range(2):
                    g = r * 2 + u
                    pe.wait_ge(s_xs, g + 1)
                    pe.wait_ge(s_qo, g + 1)
                    pe.matmul(p_q[:, :], wT[:, :], xs[:, u, :], start=True, stop=True).then_inc(s_q, 1)
                    pe.wait_ge(s_kv, g + 1)
                    pe.wait_ge(s_gate, g + 1)
                    for i in range(GT):
                        pe.matmul(p_all[:, i, 0:PROJ], C["ones"][0:1, :], brow[:, :], start=True, stop=False)
                        mm = pe.matmul(p_all[:, i, 0:PROJ], xs[:, u, i * P:(i + 1) * P], wall[:, :], start=False, stop=True)
                    mm.then_inc(s_all, 1)
            pe.wait_ge(s_fin, 8)
            for i, w in enumerate(("upto", "after", "ones")):
                mm = pe.matmul(p_w[:, 0, 0, i * NT:(i + 1) * NT], C[w][:, :], cols["la"][:, :], start=True, stop=True)
            mm.then_inc(s_sum, 1)

        @block.scalar
        def _(act):
            act.sem_inc(s_qo, 1)
            act.sem_inc(s_gate, 1)
            with act.Fori(0, NG // 2) as r:
                for u in range(2):
                    g = r * 2 + u
                    act.wait_ge(s_q, g + 1)
                    act.activation(qT[:, bass.ds(g * GW, GW)], p_q[:, :], ACT.Identity, bias=bq[:, 0:1]).then_inc(s_qo, 1)
                    act.wait_ge(s_all, g + 3)
                    act.activation(sq[:, :, :], p_all[:, :, 0:P], ACT.Square).then_inc(s_sq, 1)
                    act.activation(Gt[:, bass.ds(g * GT, GT), :], p_all[:, :, 2 * P:3 * P], ACT.Sigmoid).then_inc(s_gate, 1)
                    act.wait_ge(s_len, g + 1)
            act.wait_ge(s_kv, NG + 1)
            act.activation(cols["beta"][:, :], logit[:, 1, :], ACT.Sigmoid).then_inc(s_act, 1)
            act.wait_ge(s_fin, 1)
            act.activation(tmp[:, 1, :], tmp[:, 0, :], ACT.Exp, scale=-1.0).then_inc(s_act, 1)
            act.wait_ge(s_fin, 2)
            act.activation(tmp[:, 3, :], tmp[:, 2, :], ACT.Ln).then_inc(s_act, 1)
            act.activation(tmp[:, 4, :], length[:, :], ACT.Sqrt).then_inc(s_act, 1)
            act.wait_ge(s_sum, 1)
            for i, n in enumerate(("upto", "after", "whole")):
                act.activation(cols[n][:, :], p_w[:, 0, 0, i * NT:(i + 1) * NT], ACT.Exp).then_inc(s_act, 1)

        @block.vector
        def _(dve):
            dve.wait_ge(s_turn, 1)
            dve.tensor_copy(wT[:, :], p_w[:, 0, 0, :]).then_inc(s_wT, 1)
            dve.tensor_copy(wall[:, 0:3 * P], p_w[:, 0, 1:4, :].rearrange("p k n -> p (k n)")).then_inc(s_wT, 1)
            dve.tensor_copy(wo[:, :], p_w[:, 1, 0, :]).then_inc(s_wT, 1)
            dve.tensor_copy(wall[:, 3 * P:PROJ], p_w[:, 1, 1:3, 0]).then_inc(s_wT, 1)
            dve.sem_inc(s_kv, 1)
            with dve.Fori(0, NG // 2) as r:
                for u in range(2):
                    g = r * 2 + u
                    t = bass.ds(g * GT, GT)
                    dve.wait_ge(s_sq, g + 1)
                    dve.reduce_sum(length[:, t], sq[:, :, :], AX_X).then_inc(s_len, 1)
                    dve.wait_ge(s_gate, g + 2)
                    dve.tensor_copy(Kt[:, t, :], p_all[:, :, 0:P])
                    dve.tensor_copy(Vt[:, t, :], p_all[:, :, P:2 * P])
                    dve.tensor_copy(logit[:, 0, t], p_all[:, :, 3 * P])
                    dve.tensor_copy(logit[:, 1, t], p_all[:, :, 3 * P + 1]).then_inc(s_kv, 1)
            z = logit[:, 0, :]
            dve.wait_ge(s_kv, NG + 1)
            dve.scalar_tensor_tensor(out=tmp[:, 0, :], in0=z, scalar=-1.0, in1=z, op0=ALU.mult, op1=ALU.max).then_inc(s_fin, 1)
            dve.wait_ge(s_act, 2)
            dve.tensor_scalar(tmp[:, 2, :], tmp[:, 1, :], 1.0, None, ALU.add).then_inc(s_fin, 1)
            dve.wait_ge(s_act, 3)
            dve.scalar_tensor_tensor(out=cols["la"][:, :], in0=z, scalar=0.0, in1=tmp[:, 3, :], op0=ALU.min,
                                     op1=ALU.subtract).then_inc(s_fin, 1)
            dve.wait_ge(s_act, 4)
            dve.tensor_scalar(tmp[:, 5, :], tmp[:, 4, :], 1e-12, None, ALU.max).then_inc(s_fin, 1)
            dve.wait_ge(s_fin, 4)
            dve.reciprocal(cols["inv"][:, :], tmp[:, 5, :]).then_inc(s_fin, 1)
            dve.wait_ge(s_fin, 5)
            dve.tensor_tensor(cols["rate"][:, :], cols["inv"][:, :], cols["beta"][:, :], ALU.mult).then_inc(s_fin, 1)
            dve.tensor_tensor(Kt[:, :, :], Kt[:, :, :], spread(cols["inv"], P), ALU.mult).then_inc(s_fin, 1)
            dve.tensor_tensor(Vt[:, :, :], Vt[:, :, :], spread(cols["beta"], P), ALU.mult).then_inc(s_fin, 1)


def delta_invert(nc, name, C, Kt, cols, TT, WT, LT):
    LANES = 4
    with Stage(nc, name) as st:
        def lanes(n):
            return [st.sb(f"{n}{v}", [P, B, P]) for v in range(LANES)]

        kn, kb, kT, kbT, mt, prod = map(lanes, ("kn", "kb", "kT", "kbT", "mt", "prod"))
        lad = prod
        bgk = kn
        x, xt = kT, kbT
        A = [st.ps(f"bankA{v}", [P, B, P]) for v in range(LANES)]
        Bk = [st.ps(f"bankB{v}", [P, B, P]) for v in range(LANES)]
        s_in = [st.sem(f"in{v}") for v in range(LANES)]
        s_pe = [st.sem(f"pe{v}") for v in range(LANES)]
        s_act = [st.sem(f"act{v}") for v in range(LANES)]
        s_dve = [st.sem(f"dve{v}") for v in range(LANES)]
        s_up = st.sem("up")
        N_IN = 4
        N_PE = 2 + 2 + 1 + 2 * (LEVELS - 1) + 1
        N_ACT = 2 + 1 + 1 + 1
        N_DVE = 3 + 2 * (LEVELS - 1)
        block = st.block()

        def mask(n):
            return C[n][:, :].rearrange("p (o n) -> p o n", o=1).to_broadcast([P, B, P])

        @block.gpsimd
        def _(pool):
            for v in range(LANES):
                pool.sem_inc(s_in[v], N_IN)
            with pool.Fori(0, NCH // LANES) as r:
                for v in range(LANES):
                    c = r * LANES + v
                    pool.wait_ge(s_pe[v], (r + 1) * N_PE)
                    pool.wait_ge(s_in[v], (r + 1) * N_IN)
                    pool.tensor_copy(kn[v][:, :, :], chunk(Kt, c)).then_inc(s_in[v], 1)
                    pool.tensor_tensor(kb[v][:, :, :], chunk(Kt, c), scalars(cols["beta"], c), ALU.mult).then_inc(s_in[v], 1)
                    pool.tensor_tensor(lad[v][:, :, :], mask("after"), scalars(cols["la"], c), ALU.mult).then_inc(s_in[v], 1)
                for v in range(LANES):
                    c = r * LANES + v
                    pool.wait_ge(s_in[v], r * N_IN + (N_IN + 3))
                    pool.wait_ge(s_pe[v], (r + 1) * N_PE + 2)
                    pool.tensor_tensor(bgk[v][:, :, :], kb[v][:, :, :], scalars(cols["upto"], c), ALU.mult).then_inc(s_in[v], 1)
                    pool.wait_ge(s_dve[v], r * N_DVE + (1 + N_DVE))
                    pool.tensor_tensor(chunk(LT, c), chunk(LT, c), mask("upto"), ALU.mult).then_inc(s_up, 1)

        @block.tensor
        def _(pe):
            for v in range(LANES):
                pe.sem_inc(s_pe[v], N_PE)
            with pe.Fori(0, NCH // LANES) as r:
                a, d = (r + 1) * N_ACT, (r + 1) * N_DVE
                for v in range(LANES):
                    pe.wait_ge(s_in[v], r * N_IN + (N_IN + 3))
                    pe.wait_ge(s_act[v], a)
                    pe.wait_ge(s_dve[v], d)
                    for b in range(B):
                        mm = pe.transpose(A[v][:, b, :], kn[v][:, b, :], C["ident"][:, :])
                    mm.then_inc(s_pe[v], 1)
                    for b in range(B):
                        mm = pe.transpose(Bk[v][:, b, :], kb[v][:, b, :], C["ident"][:, :])
                    mm.then_inc(s_pe[v], 1)
                for v in range(LANES):
                    pe.wait_ge(s_act[v], a + 2)
                    for b in range(B):
                        mm = pe.matmul(A[v][:, b, :], kT[v][:, b, :], kbT[v][:, b, :], start=True, stop=True)
                    mm.then_inc(s_pe[v], 1)
                    for b in range(B):
                        mm = pe.matmul(Bk[v][:, b, :], lad[v][:, b, :], C["upto"][:, :], start=True, stop=True)
                    mm.then_inc(s_pe[v], 1)
                for v in range(LANES):
                    pe.wait_ge(s_dve[v], d + 3)
                    for b in range(B):
                        mm = pe.transpose(A[v][:, b, :], xt[v][:, b, :], C["ident"][:, :])
                    mm.then_inc(s_pe[v], 1)
                for n in range(1, LEVELS):
                    for v in range(LANES):
                        if n == 1:
                            pe.wait_ge(s_act[v], a + 4)
                        pe.wait_ge(s_dve[v], d + 1 + 2 * n)
                        for b in range(B):
                            mm = pe.matmul(A[v][:, b, :], mt[v][:, b, :], x[v][:, b, :], start=True, stop=True)
                        mm.then_inc(s_pe[v], 1)
                    for v in range(LANES):
                        pe.wait_ge(s_dve[v], d + 2 + 2 * n)
                        for b in range(B):
                            if n < LEVELS - 1:
                                pe.matmul(Bk[v][:, b, :], xt[v][:, b, :], prod[v][:, b, :], start=True, stop=True)
                            mm = pe.matmul(A[v][:, b, :], prod[v][:, b, :], xt[v][:, b, :], start=True, stop=True)
                        mm.then_inc(s_pe[v], 1)
                for v in range(LANES):
                    c = r * LANES + v
                    pe.wait_ge(s_in[v], r * N_IN + 2 * N_IN)
                    pe.wait_ge(s_dve[v], d + N_DVE)
                    for b in range(B):
                        mm = pe.matmul(Bk[v][:, b, :], bgk[v][:, b, :], chunk(TT, c)[:, b, :], start=True, stop=True)
                    mm.then_inc(s_pe[v], 1)

        @block.scalar
        def _(act):
            for v in range(LANES):
                act.sem_inc(s_act[v], N_ACT)
            with act.Fori(0, NCH // LANES) as r:
                p = (r + 1) * N_PE
                for v in range(LANES):
                    act.wait_ge(s_pe[v], p + 1)
                    act.copy(kT[v][:, :, :], A[v][:, :, :]).then_inc(s_act[v], 1)
                    act.wait_ge(s_pe[v], p + 2)
                    act.copy(kbT[v][:, :, :], Bk[v][:, :, :]).then_inc(s_act[v], 1)
                for v in range(LANES):
                    act.wait_ge(s_pe[v], p + 4)
                    act.activation(chunk(LT, r * LANES + v), Bk[v][:, :, :], ACT.Exp).then_inc(s_act[v], 1)
                for v in range(LANES):
                    act.wait_ge(s_pe[v], p + 5)
                    act.copy(x[v][:, :, :], A[v][:, :, :]).then_inc(s_act[v], 1)
                for v in range(LANES):
                    act.wait_ge(s_pe[v], p + N_PE)
                    act.mul(chunk(WT, r * LANES + v), Bk[v][:, :, :], -1.0).then_inc(s_act[v], 1)

        @block.vector
        def _(dve):
            for v in range(LANES):
                dve.sem_inc(s_dve[v], N_DVE)
            with dve.Fori(0, NCH // LANES) as r:
                p, a, d = (r + 1) * N_PE, (r + 1) * N_ACT, (r + 1) * N_DVE
                for v in range(LANES):
                    dve.wait_ge(s_act[v], a + 3)
                    dve.tensor_tensor(mt[v][:, :, :], A[v][:, :, :], chunk(LT, r * LANES + v), ALU.mult).then_inc(s_dve[v], 1)
                for v in range(LANES):
                    dve.wait_ge(s_dve[v], d + 1)
                    dve.tensor_tensor(xt[v][:, :, :], mt[v][:, :, :], mask("level0"), ALU.mult).then_inc(s_dve[v], 1)
                for v in range(LANES):
                    dve.wait_ge(s_dve[v], d + 2)
                    dve.tensor_tensor(xt[v][:, :, :], mask("ident"), xt[v][:, :, :], ALU.subtract).then_inc(s_dve[v], 1)
                for n in range(1, LEVELS):
                    for v in range(LANES):
                        dve.wait_ge(s_pe[v], p + 4 + 2 * n)
                        dve.tensor_tensor(prod[v][:, :, :], A[v][:, :, :], mask(f"level{n}"), ALU.mult).then_inc(s_dve[v], 1)
                    for v in range(LANES):
                        dve.wait_ge(s_pe[v], p + 5 + 2 * n)
                        to = xt[v][:, :, :]
                        if n < LEVELS - 1:
                            dve.tensor_tensor(x[v][:, :, :], x[v][:, :, :], Bk[v][:, :, :], ALU.subtract)
                        else:
                            to = chunk(TT, r * LANES + v)
                        dve.tensor_tensor(to, xt[v][:, :, :], A[v][:, :, :], ALU.subtract).then_inc(s_dve[v], 1)


def delta_scan(nc, name, C, Kt, Vt, Gt, qT, cols, TT, WT, LT):
    with Stage(nc, name) as st:
        def pair(n):
            return st.sb(n, [P, 2, B, P])

        tt, wt, qs, kn, bv, kd = map(pair, ("tt", "wt", "qs", "kn", "bv", "kd"))
        Ss = st.sb("S", [P, B, P])
        ST = st.sb("ST", [P, B, P])
        Sd = st.sb("Sd", [P, B, P])
        STd = st.sb("STd", [P, B, P])
        U = st.sb("U", [P, B, P])
        UT = st.sb("UT", [P, B, P])
        o1 = st.sb("o1", [P, B, P])
        o = st.sb("o", [P, B, P])
        pm = st.sb("pm", [P, B, P])
        p_u, p_ut, p_o1, p_s, p_st, p_p, p_o = (st.ps(n, [P, B, P]) for n in (
            "p_u", "p_ut", "p_o1", "p_s", "p_st", "p_p", "p_o"))
        s_load = [st.sem("load0"), st.sem("load1")]
        s_in = st.sem("in")
        s_dec = st.sem("dec")
        s_pe = st.sem("pe")
        s_u = st.sem("u")
        s_ut = st.sem("ut")
        s_dve = st.sem("dve")
        s_state = st.sem("state")
        s_og = st.sem("og")
        N_PE, N_DVE = 7, 3
        block = st.block()

        @block.sync
        def _(sp):
            with sp.Fori(0, NCH // 2) as r:
                for u in range(2):
                    c = r * 2 + u
                    sp.wait_ge(s_pe, c * N_PE + N_PE)
                    for dst, src in ((tt, TT), (wt, WT), (qs, qT), (kn, Kt), (bv, Vt)):
                        sp.dma_start(dst[:, u, :, :], chunk(src, c)).then_inc(s_load[u], 16)

        @block.gpsimd
        def _(pool):
            pool.sem_inc(s_og, 1)
            with pool.Fori(0, NCH // 2) as r:
                for u in range(2):
                    c = r * 2 + u
                    pool.wait_ge(s_pe, c * N_PE + N_PE)
                    pool.tensor_tensor(kd[:, u, :, :], chunk(Kt, c), scalars(cols["after"], c), ALU.mult).then_inc(s_in, 1)
                    pool.wait_ge(s_state, c * 2 + 2)
                    pool.tensor_tensor(STd[:, :, :], ST[:, :, :], scalars(cols["whole"], c), ALU.mult).then_inc(s_dec, 1)
                    pool.tensor_tensor(Sd[:, :, :], Ss[:, :, :], scalars(cols["whole"], c), ALU.mult).then_inc(s_dec, 1)
                    pool.wait_ge(s_dve, c * N_DVE + 2 * N_DVE)
                    pool.tensor_tensor(chunk(Gt, c), o[:, :, :], chunk(Gt, c), ALU.mult).then_inc(s_og, 1)

        @block.tensor
        def _(pe):
            pe.sem_inc(s_pe, 2 * N_PE)
            with pe.Fori(0, NCH // 2) as r:
                for u in range(2):
                    c = r * 2 + u
                    pe.wait_ge(s_load[u], 80 * (r + 1))
                    pe.wait_ge(s_state, c * 2 + 2)
                    for b in range(B):
                        pe.matmul(p_u[:, b, :], tt[:, u, b, :], bv[:, u, b, :], start=True, stop=False)
                        mm = pe.matmul(p_u[:, b, :], wt[:, u, b, :], ST[:, b, :], start=False, stop=True)
                    mm.then_inc(s_pe, 1)
                    for b in range(B):
                        pe.matmul(p_ut[:, b, :], bv[:, u, b, :], tt[:, u, b, :], start=True, stop=False)
                        mm = pe.matmul(p_ut[:, b, :], ST[:, b, :], wt[:, u, b, :], start=False, stop=True)
                    mm.then_inc(s_pe, 1)
                    for b in range(B):
                        mm = pe.matmul(p_o1[:, b, :], qs[:, u, b, :], Ss[:, b, :], start=True, stop=True)
                    mm.then_inc(s_pe, 1)
                    pe.wait_ge(s_u, c + 1)
                    pe.wait_ge(s_in, c + 1)
                    for b in range(B):
                        mm = pe.matmul(p_st[:, b, :], kd[:, u, b, :], U[:, b, :], start=True, stop=True)
                    mm.then_inc(s_pe, 1)
                    for b in range(B):
                        mm = pe.matmul(p_s[:, b, :], U[:, b, :], kd[:, u, b, :], start=True, stop=True)
                    mm.then_inc(s_pe, 1)
                    pe.wait_ge(s_ut, c + 1)
                    for b in range(B):
                        mm = pe.matmul(p_p[:, b, :], UT[:, b, :], qs[:, u, b, :], start=True, stop=True)
                    mm.then_inc(s_pe, 1)
                    pe.wait_ge(s_dve, c * N_DVE + (2 + N_DVE))
                    for b in range(B):
                        mm = pe.matmul(p_o[:, b, :], pm[:, b, :], kn[:, u, b, :], start=True, stop=True)
                    mm.then_inc(s_pe, 1)

        @block.scalar
        def _(act):
            with act.Fori(0, NCH // 2) as r:
                for u in range(2):
                    c = r * 2 + u
                    act.wait_ge(s_pe, c * N_PE + (1 + 2 * N_PE))
                    act.copy(U[:, :, :], p_u[:, :, :]).then_inc(s_u, 1)
                    act.wait_ge(s_pe, c * N_PE + (2 + 2 * N_PE))
                    act.copy(UT[:, :, :], p_ut[:, :, :]).then_inc(s_ut, 1)

        @block.vector
        def _(dve):
            dve.sem_inc(s_dve, N_DVE)
            dve.memset(Ss[:, :, :], 0.0).then_inc(s_state, 1)
            dve.memset(ST[:, :, :], 0.0).then_inc(s_state, 1)
            with dve.Fori(0, NCH // 2) as r:
                for u in range(2):
                    c = r * 2 + u
                    dve.wait_ge(s_pe, c * N_PE + (3 + 2 * N_PE))
                    dve.wait_ge(s_dve, c * N_DVE + N_DVE)
                    dve.tensor_tensor(o1[:, :, :], p_o1[:, :, :], scalars(cols["upto"], c), ALU.mult).then_inc(s_dve, 1)
                    dve.wait_ge(s_pe, c * N_PE + (4 + 2 * N_PE))
                    dve.wait_ge(s_dec, c * 2 + 2)
                    dve.tensor_tensor(ST[:, :, :], p_st[:, :, :], STd[:, :, :], ALU.add).then_inc(s_state, 1)
                    dve.wait_ge(s_pe, c * N_PE + (5 + 2 * N_PE))
                    dve.tensor_tensor(Ss[:, :, :], p_s[:, :, :], Sd[:, :, :], ALU.add).then_inc(s_state, 1)
                    dve.wait_ge(s_pe, c * N_PE + (6 + 2 * N_PE))
                    dve.tensor_tensor(pm[:, :, :], p_p[:, :, :], chunk(LT, c), ALU.mult).then_inc(s_dve, 1)
                    dve.wait_ge(s_pe, c * N_PE + 3 * N_PE)
                    dve.wait_ge(s_og, c + 1)
                    dve.wait_ge(s_dve, c * N_DVE + (1 + N_DVE))
                    dve.tensor_tensor(o[:, :, :], p_o[:, :, :], o1[:, :, :], ALU.add).then_inc(s_dve, 1)


def delta_out(nc, name, X, Gt, C, W, wo):
    with Stage(nc, name) as st:
        bo = st.sb("bo", [1, P])
        gT = st.sb("gT", [P, 2, GT, P])
        turned = st.ps("turned", [P, 2, GT, P])
        y = st.ps("y", [P, 2, GT, P])
        s_w = st.sem("w")
        s_turn = st.sem("turn")
        s_gT = st.sem("gT")
        s_y = st.sem("y")
        s_res = st.sem("res")
        block = st.block()

        @block.sync
        def _(sp):
            sp.dma_start(bo[:, :], W['bo'].rearrange("(o n) -> o n", o=1)).then_inc(s_w, 16)

        @block.tensor
        def _(pe):
            for g in range(NG + 1):
                if g < NG:
                    if g >= 2:
                        pe.wait_ge(s_gT, g - 1)
                    for i in range(GT):
                        mm = pe.transpose(turned[:, g % 2, i, :], Gt[:, g * GT + i, :], C["ident"][:, :])
                    mm.then_inc(s_turn, 1)
                if g >= 1:
                    h = g - 1
                    if h == 0:
                        pe.wait_ge(s_w, 16)
                    pe.wait_ge(s_gT, h + 1)
                    if h >= 2:
                        pe.wait_ge(s_res, h - 1)
                    for i in range(GT):
                        pe.matmul(y[:, h % 2, i, :], C["ones"][0:1, :], bo[:, :], start=True, stop=False)
                        mm = pe.matmul(y[:, h % 2, i, :], gT[:, h % 2, i, :], wo[:, :], start=False, stop=True)
                    mm.then_inc(s_y, 1)

        @block.scalar
        def _(act):
            for g in range(NG):
                act.wait_ge(s_turn, g + 1)
                if g >= 2:
                    act.wait_ge(s_y, g - 1)
                act.copy(gT[:, g % 2, :, :], turned[:, g % 2, :, :]).then_inc(s_gT, 1)

        @block.vector
        def _(dve):
            for g in range(NG):
                dve.wait_ge(s_y, g + 1)
                xt = X[:, g * GT:(g + 1) * GT, :]
                dve.tensor_tensor(xt, y[:, g % 2, :, :], xt, ALU.add).then_inc(s_res, 1)


def delta_rule(nc, name, X, XnT, C, W):
    with ExitStack() as ctx:
        def sb(n, shape):
            return ctx.enter_context(nc.sbuf_tensor(f"{name}_{n}", shape, F32))

        cols = {n: sb(n, [P, NT]) for n in ("la", "beta", "inv", "rate", "upto", "after", "whole")}
        wo = sb("wo", [P, P])
        Kt, Vt, Gt = (sb(n, [P, NT, P]) for n in ("K", "V", "G"))
        qT = sb("qT", [P, TOK])
        delta_project(nc, f"{name}p", XnT, C, W, Kt, Vt, Gt, qT, wo, cols)
        WT, LT = (sb(n, [P, NT, P]) for n in ("WT", "LT"))
        TT = XnT
        delta_invert(nc, f"{name}i", C, Kt, cols, TT, WT, LT)
        delta_scan(nc, f"{name}r", C, Kt, Vt, Gt, qT, cols, TT, WT, LT)
        delta_out(nc, f"{name}o", X, Gt, C, W, wo)


INPUTS = ['L0_attn_a_x', 'L0_attn_a_W_DQ', 'L0_attn_a_W_UQ', 'L0_attn_a_W_QR', 'L0_attn_a_W_DKV',
          'L0_attn_a_W_UK', 'L0_attn_a_W_UV', 'L0_attn_a_W_KR', 'L0_attn_a_W_O',
          'L0_attn_b_Wc_down', 'L0_attn_b_Wq_up', 'L0_attn_b_Wkv_up', 'L0_attn_b_Wc_proj',
          'L0_ffn_w_gate', 'L0_ffn_w_up', 'L0_ffn_w_down',
          'L1_attn_a_Wl', 'L1_attn_a_bl', 'L1_attn_a_Wb', 'L1_attn_a_Wc', 'L1_attn_a_Dp',
          'L1_attn_b_Wq', 'L1_attn_b_bq', 'L1_attn_b_Wk', 'L1_attn_b_bk', 'L1_attn_b_Wv', 'L1_attn_b_bv',
          'L1_attn_b_Wa', 'L1_attn_b_ba', 'L1_attn_b_Wb', 'L1_attn_b_bb', 'L1_attn_b_Wg', 'L1_attn_b_bg',
          'L1_attn_b_Wo', 'L1_attn_b_bo',
          'L1_ffn_scale', 'L1_ffn_gate_w', 'L1_ffn_gate_b', 'L1_ffn_mlp1_w', 'L1_ffn_mlp1_b',
          'L1_ffn_mlp2_w', 'L1_ffn_mlp2_b']


def constants():
    p = np.arange(P)
    keys, queries = p[:, None], p[None, :]
    hi = np.float32(np.exp(CLIP * (DH + DR) ** -0.5))
    pos = np.arange(S, dtype=np.float32)[None, :]
    freq = np.float32(10000.0) ** (-np.arange(0, DR, 2, dtype=np.float32) / DR)
    n = np.arange(H * DR + DR)
    angle = (pos * freq[(n % DR) // 2][:, None]).astype(np.float32)
    return {
        "ident": np.eye(P, dtype=np.float32),
        "neg_kq": np.where(keys > queries, NEG, 0).astype(np.float32),
        "neg_qk": np.where(queries > keys, NEG, 0).astype(np.float32),
        "ones": np.ones((P, P), np.float32),
        "upto": (keys <= queries).astype(np.float32),
        "after": (keys > queries).astype(np.float32),
        **{f"level{n}": ((keys >> (n + 1) == queries >> (n + 1)) & ((keys if n else queries) >> n & 1 == 1)
                         & ((queries if n else keys) >> n & 1 == 0)).astype(np.float32) for n in range(LEVELS)},
        "pick_row": (np.arange(96)[:, None] % ROUTE_AT == np.arange(E)[None, :]).astype(np.float32),
        "top_kq": np.where(keys > queries, 0, hi).astype(np.float32),
        "pick_sum": (keys == 32 * (queries // 32) + DH).astype(np.float32),
        "cos": np.cos(angle),
        "sin": np.sin(angle) * np.where(n % 2, 1, -1).astype(np.float32)[:, None],
    }


STAGES = "afbfsmdm"


def build(nc, I, consts, out):
    with ExitStack() as ctx:
        X = ctx.enter_context(nc.sbuf_tensor("X", [P, NT, D], F32))
        C = {n: ctx.enter_context(nc.sbuf_tensor(f"c_{n}", list(a.shape), F32)) for n, a in consts.items()
             if n not in ("cos", "sin")}
        XnT = ctx.enter_context(nc.sbuf_tensor("XnT", [P, TOK], F32))
        for n in ("ident", "neg_kq", "neg_qk"):
            C[f"{n}_b"] = ctx.enter_context(nc.sbuf_tensor(f"c_{n}_b", [P, P], BF16))
        load_x(nc, I['L0_attn_a_x'], consts, X, C)
        X_ = None
        for n, s in enumerate(STAGES):
            if s == "a":
                W = {n: I[f'L0_attn_a_{n}'] for n in ('W_DQ', 'W_UQ', 'W_QR', 'W_DKV', 'W_UK', 'W_UV', 'W_KR', 'W_O')}
                norm_stage(nc, f"norm{n}", X, XnT, C)
                W["cos"], W["sin"] = consts["cos"], consts["sin"]
                attention_a(nc, f"attn{n}", X, XnT, C, W)
            if s == "b":
                W = {n: I[f'L0_attn_b_{n}'] for n in ('Wc_down', 'Wq_up', 'Wkv_up', 'Wc_proj')}
                norm_stage(nc, f"norm{n}", X, XnT, C)
                attention_b(nc, f"attn{n}", X, XnT, C, W)
            if s == "s":
                W = {n: I[f'L1_attn_a_{n}'] for n in ('Wl', 'bl', 'Wb', 'Wc', 'Dp')}
                norm_stage(nc, f"norm{n}", X, XnT, C)
                recurrence(nc, f"scan{n}", X, XnT, C, W)
            if s == "m":
                W = {n: I[f'L1_ffn_{n}'] for n in ('scale', 'gate_w', 'gate_b', 'mlp1_w', 'mlp1_b', 'mlp2_w', 'mlp2_b')}
                if X_ is None:
                    X_ = Experts(nc, ctx)
                    load_experts(nc, "experts", C, W, X_)
                norm_stage(nc, f"norm{n}", X, XnT, C, W['scale'])
                with nc.sbuf_tensor(f"routeT{n}", [E, TOK], F32) as routeT, \
                        nc.sbuf_tensor(f"routes{n}", [96, TOK], BF16) as routes_b:
                    route(nc, f"route{n}", XnT, C, X_, routeT, routes_b)
                    experts(nc, f"moe{n}", X, XnT, C, X_, routeT, routes_b)
            if s == "d":
                W = {n: I[f'L1_attn_b_{n}'] for n in ('Wq', 'bq', 'Wk', 'bk', 'Wv', 'bv', 'Wa', 'ba', 'Wb', 'bb',
                                                      'Wg', 'bg', 'Wo', 'bo')}
                norm_stage(nc, f"norm{n}", X, XnT, C)
                delta_rule(nc, f"delta{n}", X, XnT, C, W)
            if s == "f":
                norm_stage(nc, f"norm{n}", X, XnT, C)
                gated_mlp(nc, f"mlp{n}", X, XnT, C, I['L0_ffn_w_gate'], I['L0_ffn_w_up'], I['L0_ffn_w_down'])
        store_x(nc, X, out)


def kernel(**inputs):
    import concourse.bacc as _bacc
    from concourse.bass_utils import run_bass_kernel_spmd as _run

    nc = _bacc.Bacc("TRN2", target_bir_lowering=False, num_devices=1)
    arrays, args, tables = {}, {}, {}
    for name in INPUTS:
        a = np.ascontiguousarray(inputs[name])
        arrays[f"in_{name}_dram"] = a
        args[name] = nc.dram_tensor(f"in_{name}_dram", a.shape, mybir.dt.from_np(a.dtype), kind="ExternalInput").ap()
    for name, a in constants().items():
        arrays[f"const_{name}_dram"] = a
        tables[name] = nc.dram_tensor(f"const_{name}_dram", a.shape, mybir.dt.from_np(a.dtype), kind="ExternalInput").ap()
    out = nc.dram_tensor("out_0_dram", (B, S, D), F32, kind="ExternalOutput").ap()
    build(nc, args, tables, out)
    r = _run(nc, [arrays], core_ids=[0])
    return r.results[0]["out_0_dram"]
```
